# Optimizing a Trainium2 kernel written in Bass

```python
import numpy as np
import jax
import jax.numpy as jnp

def _softmax(x, axis=-1):
    return jax.nn.softmax(x, axis=axis)

def _gelu(x):
    return jax.nn.gelu(x, approximate=True)

def _silu(x):
    return jax.nn.silu(x)

def _sigmoid(x):
    return jax.nn.sigmoid(x)

def _layernorm(x, axis=-1, eps=1e-05):
    m = jnp.mean(x, axis=axis, keepdims=True)
    v = jnp.var(x, axis=axis, keepdims=True)
    return (x - m) / jnp.sqrt(v + eps)

def _scatter_add(tgt, idx, src, axis=0):
    return tgt.at[idx].add(src)

def _segment_sum(src, seg, n):
    return jax.ops.segment_sum(src, seg, n)
kernel_name = 'mk_gnn_ffn_d1_gnn_r16_45c428'

def setup_inputs(seed: int=0):
    np.random.seed(seed)
    _w = jnp.asarray

    def _rec_inputs():
        import jax
        import jax.numpy as jnp
        _gk = jax.random.key(seed)
        x = -0.0006008 + 1.001 * jax.random.normal(jax.random.fold_in(_gk, 1), (6250, 256), jnp.float32)
        src = jax.random.randint(jax.random.fold_in(_gk, 2), (100000,), 0, 6250, jnp.int32)
        dst = jax.random.randint(jax.random.fold_in(_gk, 3), (100000,), 0, 6250, jnp.int32)
        _o = jnp.argsort(dst, stable=True)
        src = src[_o]
        dst = dst[_o]
        return (x, src, dst)
    x, src, dst = _rec_inputs()

    def _L0_gnn_setup():
        import jax, jax.numpy as jnp
        import numpy as np
        N, E, D = (625, 20000, 256)
        key = jax.random.key(seed)
        k1, k2, k3, k4 = jax.random.split(key, 4)
        x = jax.random.normal(k1, (N, D), dtype=jnp.float32)
        edge_index = jax.random.randint(k2, (2, E), 0, N, dtype=jnp.int64)
        s = 1.0 / np.sqrt(D)
        w1 = jax.random.uniform(k3, (D, D), dtype=jnp.float32, minval=-s, maxval=s)
        b1 = jnp.zeros((D,), dtype=jnp.float32)
        w2 = jax.random.uniform(k4, (D, D), dtype=jnp.float32, minval=-s, maxval=s)
        b2 = jnp.zeros((D,), dtype=jnp.float32)
        return {'x': x, 'edge_index': edge_index, 'w1': w1, 'b1': b1, 'w2': w2, 'b2': b2}
    _L0_gnn_all = _L0_gnn_setup()
    _L0_gnn_in = {k: v for k, v in _L0_gnn_all.items() if k in ('w1', 'b1', 'w2', 'b2')}
    del _L0_gnn_all

    def _L0_ffn_setup():
        import math
        import jax, jax.numpy as jnp
        import numpy as np
        CAPACITY_FACTOR = 1.25
        TOP_K = 2
        LN_EPS = 1e-05

        def _layer_norm(x, gamma, beta):
            mu = jnp.mean(x, axis=-1, keepdims=True)
            var = jnp.var(x, axis=-1, keepdims=True)
            return (x - mu) * jax.lax.rsqrt(var + LN_EPS) * gamma + beta
        key = jax.random.key(seed)
        ks = jax.random.split(key, 4)
        B, S, D, F, E = (8, 256, 256, 512, 8)
        x = jax.random.normal(ks[0], (B, S, D), dtype=jnp.float32)
        Wr = jax.random.normal(ks[1], (D, E), dtype=jnp.float32) / np.sqrt(D)
        br = jnp.zeros((E,), jnp.float32)
        W1 = jax.random.normal(ks[2], (E, D, F), dtype=jnp.float32) / np.sqrt(D)
        b1 = jnp.zeros((E, F), jnp.float32)
        W2 = jax.random.normal(ks[3], (E, F, D), dtype=jnp.float32) / np.sqrt(F)
        b2 = jnp.zeros((E, D), jnp.float32)
        gamma = jnp.ones((D,), jnp.float32)
        beta = jnp.zeros((D,), jnp.float32)
        return {'x': x, 'Wr': Wr, 'br': br, 'W1': W1, 'b1': b1, 'W2': W2, 'b2': b2, 'gamma': gamma, 'beta': beta}
    _L0_ffn_all = _L0_ffn_setup()
    _L0_ffn_in = {k: v for k, v in _L0_ffn_all.items() if k in ('Wr', 'br', 'W1', 'b1', 'W2', 'b2', 'gamma', 'beta')}
    del _L0_ffn_all
    return {'x': x, 'src': src, 'dst': dst, 'L0_gnn_w1': _L0_gnn_in['w1'], 'L0_gnn_b1': _L0_gnn_in['b1'], 'L0_gnn_w2': _L0_gnn_in['w2'], 'L0_gnn_b2': _L0_gnn_in['b2'], 'L0_ffn_Wr': _L0_ffn_in['Wr'], 'L0_ffn_br': _L0_ffn_in['br'], 'L0_ffn_W1': _L0_ffn_in['W1'], 'L0_ffn_b1': _L0_ffn_in['b1'], 'L0_ffn_W2': _L0_ffn_in['W2'], 'L0_ffn_b2': _L0_ffn_in['b2'], 'L0_ffn_gamma': _L0_ffn_in['gamma'], 'L0_ffn_beta': _L0_ffn_in['beta']}

def reference(x, src, dst, L0_gnn_w1, L0_gnn_b1, L0_gnn_w2, L0_gnn_b2, L0_ffn_Wr, L0_ffn_br, L0_ffn_W1, L0_ffn_b1, L0_ffn_W2, L0_ffn_b2, L0_ffn_gamma, L0_ffn_beta):
    import jax
    import jax.numpy as jnp

    def _L0_gnn_ref(x, edge_index, w1, b1, w2, b2):
        import jax, jax.numpy as jnp
        import numpy as np
        N, E, D = (625, 20000, 256)

        def mlp(h):
            return jax.nn.relu(h @ w1 + b1) @ w2 + b2
        row, col = (edge_index[0], edge_index[1])
        msgs = mlp(x[col])
        agg = jax.ops.segment_sum(msgs, row, num_segments=x.shape[0])
        return mlp(x + agg)

    def _L0_ffn_ref(x, Wr, br, W1, b1, W2, b2, gamma, beta):
        import math
        import jax, jax.numpy as jnp
        import numpy as np
        CAPACITY_FACTOR = 1.25
        TOP_K = 2
        LN_EPS = 1e-05

        def _layer_norm(x, gamma, beta):
            mu = jnp.mean(x, axis=-1, keepdims=True)
            var = jnp.var(x, axis=-1, keepdims=True)
            return (x - mu) * jax.lax.rsqrt(var + LN_EPS) * gamma + beta
        B, S, D = x.shape
        E = Wr.shape[1]
        N = B * S
        K = TOP_K
        logits = jnp.mean(x, axis=1) @ Wr + br
        routing_weights = jax.nn.softmax(logits, axis=-1)
        capacity = float(math.ceil(N * CAPACITY_FACTOR / E))
        expected_loads = routing_weights.sum(axis=0) * (N / B)
        scale = jnp.where(expected_loads > capacity, capacity / expected_loads, 1.0)
        routing_weights = jax.nn.softmax(routing_weights * scale, axis=-1)
        rw_tok = jnp.broadcast_to(routing_weights[:, None, :], (B, S, E)).reshape(N, E)
        top_w, top_i = jax.lax.top_k(rw_tok, K)
        top_w = jax.nn.softmax(top_w, axis=-1)
        xf = x.reshape(N, D)
        h = jax.nn.gelu(jnp.einsum('nd,edf->enf', xf, W1) + b1[:, None, :], approximate=False)
        y = jnp.einsum('enf,efd->end', h, W2) + b2[:, None, :]
        w_dense = jnp.zeros((N, E), x.dtype).at[jnp.arange(N)[:, None], top_i].add(top_w)
        out = jnp.einsum('ne,end->nd', w_dense, y).reshape(B, S, D)
        out = _layer_norm(out + x, gamma, beta)
        return out
    edge_index = jnp.stack([src, dst])
    x = x + _L0_gnn_ref(_layernorm(x, axis=-1), edge_index, L0_gnn_w1, L0_gnn_b1, L0_gnn_w2, L0_gnn_b2)
    x = x + _L0_ffn_ref(_layernorm(x, axis=-1)[None], L0_ffn_Wr, L0_ffn_br, L0_ffn_W1, L0_ffn_b1, L0_ffn_W2, L0_ffn_b2, L0_ffn_gamma, L0_ffn_beta)[0]
    return x

_drawn_inputs = setup_inputs


def setup_inputs(seed=0):
    import zlib

    import numpy as np

    out = dict(_drawn_inputs(seed))
    spreads = {'L0_gnn_b1': (0.0, 0.1),
     'L0_gnn_b2': (0.0, 0.1),
     'L0_ffn_br': (0.0, 0.1),
     'L0_ffn_b1': (0.0, 0.385),
     'L0_ffn_b2': (0.0, 0.273),
     'L0_ffn_gamma': (1.0, 0.2),
     'L0_ffn_beta': (0.0, 0.1)}
    factors = {'L0_ffn_Wr': 8.0}
    for name, (base, spread) in spreads.items():
        noise = np.random.default_rng([zlib.crc32(name.encode()), seed]).standard_normal(out[name].shape)
        drawn = base * np.exp(spread * noise) if base else spread * noise
        out[name] = jnp.asarray(drawn.astype(out[name].dtype))
    for name, factor in factors.items():
        out[name] = (out[name] * factor).astype(out[name].dtype)
    return out
```

```python
from contextlib import ExitStack

import concourse.bass as bass
from concourse import mybir

F32 = mybir.dt.float32
I32 = mybir.dt.int32
BF16 = mybir.dt.bfloat16
ALU = mybir.AluOpType
ACT = mybir.ActivationFunctionType
AX = mybir.AxisListType

P = 128
N = 6250
D = 256
EDGES = 100000
F = 512
EXPERTS = 8
TOP_K = 2
EPS = 1e-5
CAPACITY = float(-(-N * 125 // (100 * EXPERTS)))

KD = D // P
KF = F // P
TILES = -(-N // P)
LAST = N - (TILES - 1) * P

SLOTS = 1024
LOG_SLOTS = 10
LOG_ALL = 17
EDGE_ROWS = 125
EDGE_COLS = EDGES // EDGE_ROWS
NODE_BITS = 13
NODE_MASK = (1 << NODE_BITS) - 1
KEY_BITS = (1 << 2 * NODE_BITS) - 1
KEY_TOP = 1 << 2 * NODE_BITS
KEY_NONE = KEY_TOP | NODE_MASK << NODE_BITS

BUCKET_TILES = [17] * (TILES - 1) + [15]
GROUP = 9
RING = 3
XGROUP = 7
QTILES = 4


def halves(b):
    n = BUCKET_TILES[b]
    first = (n + 1) // 2
    return [(0, first), (first, n - first)]


def build(nc, x, src, dst, w1, b1, w2, b2, wr, br, fw1, fb1, fw2, fb2, gamma, beta, cf, ci, out):
    ctx = ExitStack()
    with ctx:
        def sb(name, shape, dt=F32):
            return ctx.enter_context(nc.sbuf_tensor(name, shape, dt))

        def sem(name):
            return ctx.enter_context(nc.semaphore(name))

        table = nc.dram_tensor("table", (TILES * P, D), F32, kind="Internal").ap()
        edge_list = nc.dram_tensor("edge_list", (P * SLOTS,), I32, kind="Internal").ap()

        X = sb("X", [P, TILES, D])
        XT = sb("XT", [P, TILES, KD, P])
        WORK_WORDS = 13568
        work = sb("work", [P, WORK_WORDS])
        used = [0]

        def carve(shape, dt=F32, words=None):
            n = 1
            for s in shape:
                n *= s
            n = words or n
            a = work[:, used[0]:used[0] + n]
            used[0] += n
            assert used[0] <= WORK_WORDS, used
            if dt is not F32:
                a = a.bitcast(dt)
            if len(shape) == 2:
                a = a.rearrange("p (a b) -> p a b", b=shape[1])
            if len(shape) == 3:
                a = a.rearrange("p (a b c) -> p a b c", b=shape[1], c=shape[2])
            return a

        src_in = carve([EDGE_COLS], I32)
        dst_in = carve([EDGE_COLS], I32)
        sign_out = carve([EDGE_COLS], BF16, words=EDGE_COLS // 2)
        key = [carve([SLOTS], I32), carve([SLOTS], I32)]
        key_high = carve([SLOTS // 2])
        xn_in = [carve([QTILES, D]) for _ in range(2)]
        xn_t = [carve([KD, QTILES * P]) for _ in range(2)]
        hid_t = [carve([KD, QTILES * P]) for _ in range(2)]
        m_out = [carve([QTILES, D]) for _ in range(2)]
        used[0] = 0
        rows = [carve([GROUP, D]) for _ in range(RING)]
        onehot = [carve([GROUP, P]) for _ in range(2)]
        used[0] = 0
        ew1 = carve([TOP_K * KD, F])
        ew2 = carve([TOP_K * KF, D])
        act = [carve([TOP_K * KF, QTILES * P]) for _ in range(2)]

        cfs = sb("cfs", [P, 2 * P])
        ident = cfs[:, 0:P]
        iota = cfs[:, P:2 * P]
        ones = sb("ones", [P, P])
        masks = sb("masks", [P, 16], I32)
        w1s = sb("w1s", [P, KD, D])
        w2s = sb("w2s", [P, KD, D])
        b1s = sb("b1s", [P, KD])
        b2s = sb("b2s", [1, D])
        wrs = sb("wrs", [P, KD, EXPERTS])
        brs = sb("brs", [1, EXPERTS])
        gam = sb("gam", [P, D])
        bet = sb("bet", [P, D])
        stat = sb("stat", [P, XGROUP, 6])
        mv = sb("mv", [P, TILES, 2])
        rs = sb("rs", [P, TILES])
        nmr = sb("nmr", [P, TILES])
        rq = [sb(f"rq{i}", [P, XGROUP]) for i in range(3)]
        sign_sum = sb("sign_sum", [P, TILES])
        starts = sb("starts", [1, TILES + 1], I32)
        startf = sb("startf", [1, TILES + 1])
        over = sb("over", [1, TILES])
        fits = sb("fits", [1, 2])
        crowded = sb("crowded", [1, 1], I32)
        keep = sb("keep", [P, 1])
        kt = [sb(f"kt{i}", [P, 17], I32) for i in range(4)]
        ki = [sb(f"ki{i}", [P, 17], I32) for i in range(2)]
        klo = sb("klo", [P, 17], I32)
        lo = [sb(f"lo{i}", [P, 17]) for i in range(2)]
        U = [sb(f"U{i}", [P, D]) for i in range(2)]
        UT = [sb(f"UT{i}", [P, KD, P]) for i in range(2)]
        HC = [sb(f"HC{i}", [P, KD, P]) for i in range(2)]
        XB = [sb(f"XB{i}", [P, D]) for i in range(2)]
        stat2 = sb("stat2", [P, 6])
        mv2 = sb("mv2", [P, TILES, 2])
        rs2 = sb("rs2", [P, TILES])
        nmr2 = sb("nmr2", [P, TILES])
        colsum = sb("colsum", [P, KD, TILES])
        msum = sb("msum", [P, KD])
        R = sb("R", [1, 64, EXPERTS])
        chosen = sb("chosen", [1, TOP_K], I32)
        wts = sb("wts", [1, TOP_K])
        wb = sb("wb", [P, TOP_K])
        eb1 = sb("eb1", [P, TOP_K, KF])
        eb2 = sb("eb2", [P, TOP_K, D])
        bias = sb("bias", [P, D])
        res = [sb(f"res{i}", [P, QTILES, D]) for i in range(2)]
        stat3 = sb("stat3", [P, QTILES, 6])
        mv3 = sb("mv3", [P, QTILES, 2])
        rs3 = sb("rs3", [P, QTILES])
        nmr3 = sb("nmr3", [P, QTILES])

        bank = [ctx.enter_context(nc.psum_tensor(f"bank{i}", [P, 512], F32)) for i in range(8)]

        s_edges = sem("s_edges")
        s_masks = sem("s_masks")
        s_const = sem("s_const")
        s_x = [sem(f"s_xload{j}") for j in range(TILES // XGROUP)]
        s_xpad = sem("s_xpad")
        s_extra = sem("s_extra")
        s_own = sem("s_own")
        s_keys = sem("s_keys")
        s_stat = sem("s_stat")
        s_sign = sem("s_sign")
        s_bnd = sem("s_bnd")
        s_starts = sem("s_starts")
        s_kv = sem("s_kv")
        s_kt = sem("s_kt")
        s_kc = sem("s_kc")
        s_sorted = sem("s_sorted")
        s_list = sem("s_list")
        s_xn = sem("s_xn")
        s_tp = sem("s_tp")
        s_xt = sem("s_xt")
        s_h = sem("s_h")
        s_relu = sem("s_relu")
        s_m = sem("s_m")
        s_mc = sem("s_mc")
        s_mst = [sem(f"s_mst{i}") for i in range(2)]
        s_kload = [sem(f"s_kload{i}") for i in range(4)]
        s_idx = sem("s_idx")
        s_oh = sem("s_oh")
        s_row = [sem(f"s_row{i}") for i in range(RING)]
        s_agg = sem("s_agg")
        s_u = sem("s_u")
        s_tu = sem("s_tu")
        s_ut = sem("s_ut")
        s_hc = sem("s_hc")
        s_rc = sem("s_rc")
        s_g = sem("s_g2")
        s_x1 = sem("s_x1")
        s_xb = sem("s_xb")
        s_tx = sem("s_tx")
        s_txc = sem("s_txc")
        s_msum = sem("s_msum")
        s_logit = sem("s_logit")
        s_dif = sem("s_dif")
        s_exp = sem("s_exp")
        s_route = sem("s_route")
        s_wbp = sem("s_wbp")
        s_eb = sem("s_eb")
        s_ew1 = sem("s_ew1")
        s_ew2 = sem("s_ew2")
        s_w2s = sem("s_w2s")
        s_bias = sem("s_bias")
        s_eh = sem("s_eh")
        s_gelu = sem("s_gelu")
        s_y = sem("s_y")
        s_xr = sem("s_xr")
        s_yr = sem("s_yr")
        s_ln = sem("s_ln")
        s_fin = sem("s_fin")
        s_out = [sem(f"s_out{i}") for i in range(2)]
        s_pool = sem("s_pool")
        s_keep = sem("s_keep")
        g_load = sem("g_load")
        g_idx = sem("g_idx")
        g_rows = sem("g_rows")
        g_sum = sem("g_sum")
        g_done = sem("g_done")
        g_own = sem("g_own")

        STEPS = -(-TILES // QTILES)
        N_CONST = 8

        def tiles_of(q):
            return range(q * QTILES, min((q + 1) * QTILES, TILES))

        def stores_of(q):
            return 16 * (q // 2 + 1)

        plan = []
        n_before = 6
        plan += [("mlp", q) for q in range(n_before)]
        for i, k in enumerate(range(LOG_SLOTS + 1, LOG_ALL + 1)):
            plan += [("turn", k, 0), ("turn", k, 1)]
            if n_before + i < STEPS:
                plan.append(("mlp", n_before + i))
        plan += [("mlp", q) for q in range(n_before + LOG_ALL - LOG_SLOTS, STEPS)]
        n_turns = 2 * (LOG_ALL - LOG_SLOTS)

        def turn_no(k, back):
            return 2 * (k - LOG_SLOTS - 1) + back

        def key_after(stages):
            return stages % 2

        SORTED_IN = key_after(LOG_ALL * (LOG_ALL + 1) // 2)

        def turn_in(k, back):
            return key[key_after(k * (k - 1) // 2 + (k - LOG_SLOTS if back else 0))]

        rows_until, on_slot = [], [0] * RING
        for b in range(TILES):
            for _, n in halves(b):
                on_slot[len(rows_until) % RING] += n
                rows_until.append(on_slot[len(rows_until) % RING])

        def crowded_path(e, body):
            with e.If(e.value_load(crowded[0:1, 0:1], min_val=0, max_val=1) > 0):
                for pair in range(0, TILES, 2):
                    lo_ = e.value_load(starts[0:1, pair:pair + 1], min_val=0, max_val=EDGES)
                    end = min(pair + 2, TILES)
                    hi_ = e.value_load(starts[0:1, end:end + 1], min_val=0, max_val=EDGES)
                    with e.Fori(0, -(-EDGES // P)) as chunk:
                        with e.If(chunk * P < hi_):
                            with e.If((chunk + 1) * P > lo_):
                                body(pair, chunk)

        def taken(e, s, n=1):
            e.wait_ge(s, n)
            e.sem_clear(s)

        block = ctx.enter_context(nc.Block())

        @block.sync
        def _(e):
            e.dma_start(src_in[0:EDGE_ROWS, :], src.rearrange("(p t) -> p t", t=EDGE_COLS)).then_inc(s_edges, 16)
            e.dma_start(dst_in[0:EDGE_ROWS, :], dst.rearrange("(p t) -> p t", t=EDGE_COLS)).then_inc(s_edges, 16)
            e.dma_start(cfs[:, :], cf).then_inc(s_masks, 16)
            e.dma_start(masks[:, :], ci).then_inc(s_masks, 16)
            for j in range(TILES // XGROUP):
                a, z = j * XGROUP, (j + 1) * XGROUP
                if z * P <= N:
                    e.dma_start(X[:, a:z, :], x[a * P:z * P, :].rearrange("(t p) f -> p t f", p=P)).then_inc(s_x[j], 16)
                    continue
                e.dma_start(X[:, a:z - 1, :], x[a * P:(z - 1) * P, :].rearrange("(t p) f -> p t f", p=P)).then_inc(s_x[j], 16)
                e.wait_ge(s_xpad, 1)
                e.dma_start(X[0:LAST, z - 1, :], x[(z - 1) * P:N, :]).then_inc(s_x[j], 16)
            e.dma_start(w1s[:, :, :], w1).then_inc(s_const, 16)
            e.dma_start(w2s[:, :, :], w2).then_inc(s_const, 16)
            e.dma_start(b1s[:, :], b1).then_inc(s_const, 16)
            e.dma_start(b2s[:, :], b2.unsqueeze(0)).then_inc(s_const, 16)
            e.dma_start(wrs[:, :, :], wr).then_inc(s_const, 16)
            e.dma_start(brs[:, :], br.unsqueeze(0)).then_inc(s_const, 16)
            e.dma_start(gam[:, :], gamma.unsqueeze(0).broadcast_to([P, D])).then_inc(s_const, 16)
            e.dma_start(bet[:, :], beta.unsqueeze(0).broadcast_to([P, D])).then_inc(s_const, 16)
            for q in range(STEPS):
                t = tiles_of(q)
                e.wait_ge(s_mc, 2 * q + (len(t) + 1) // 2)
                e.dma_start(table[t[0] * P:(t[-1] + 1) * P, :].rearrange("(t p) f -> p t f", p=P),
                            m_out[q % 2][:, 0:len(t), :]).then_inc(s_mst[q % 2], 16)
            e.wait_ge(s_sorted, 1)
            e.dma_start(edge_list.rearrange("(p t) -> p t", p=P), key[SORTED_IN][:, :]).then_inc(s_list, 16)
            e.wait_ge(s_list, 16)
            e.wait_ge(s_starts, 2)

            def load_chunk(pair, chunk):
                e.dma_start(kt[0][:, 0:1], edge_list[bass.DynSlice(chunk * P, P)].rearrange("(p t) -> p t", p=P))\
                    .then_inc(g_load, 16)
                taken(e, g_done)

            crowded_path(e, load_chunk)
            for b in range(TILES):
                at = e.value_load(starts[0:1, b:b + 1], min_val=0, max_val=EDGES)
                if b >= 4:
                    e.wait_ge(s_idx, b - 3)
                n = BUCKET_TILES[b]
                e.dma_start(kt[b % 4][:, 0:n], edge_list[bass.DynSlice(at, n * P)].rearrange("(p t) -> p t", p=P))\
                    .then_inc(s_kload[b % 4], 16)
            e.wait_ge(s_route, 1)
            for i in range(TOP_K):
                ex = e.value_load(chosen[0:1, i:i + 1], min_val=0, max_val=EXPERTS - 1)
                e.dma_start(ew1[:, i * KD:(i + 1) * KD, :],
                            fw1[bass.DynSlice(ex, 1), :, :, :].rearrange("a p k f -> p (a k) f")).then_inc(s_ew1, 16)
                e.dma_start(eb1[:, i, :], fb1[bass.DynSlice(ex, 1), :, :].rearrange("a p k -> p (a k)")).then_inc(s_eb, 16)
                e.dma_start(eb2[:, i, :], fb2[bass.DynSlice(ex, 1), :].broadcast_to([P, D])).then_inc(s_eb, 16)
                e.dma_start(ew2[:, i * KF:(i + 1) * KF, :],
                            fw2[bass.DynSlice(ex, 1), :, :, :].rearrange("a p k f -> p (a k) f")).then_inc(s_ew2, 16)
            for c in range(STEPS):
                t = tiles_of(c)
                e.wait_ge(s_fin, c + 1)
                if t[-1] < TILES - 1:
                    e.dma_start(out[t[0] * P:(t[-1] + 1) * P, :].rearrange("(t p) f -> p t f", p=P),
                                res[c % 2][:, 0:len(t), :]).then_inc(s_out[c % 2], 16)
                else:
                    assert len(t) == 1
                    e.dma_start(out[t[0] * P:N, :], res[c % 2][0:LAST, 0, :]).then_inc(s_out[c % 2], 16)
            for i in range(2):
                e.wait_ge(s_out[i], 16 * len(range(i, STEPS, 2)))

        @block.gpsimd
        def _(e):
            e.memset(X[:, TILES - 1, :], 0.0).then_inc(s_xpad, 1)
            e.memset(ones[:, :], 1.0).then_inc(s_xpad, 1)
            e.memset(XT[:, :, :, :].rearrange("p a b c -> p (a b c)"), 0.0).then_inc(s_extra, 1)
            for i in range(2):
                e.wait_ge(s_mst[i], 16 * len(range(i, STEPS, 2)))
            e.wait_ge(s_starts, 2)

            def gather_chunk(pair, chunk):
                taken(e, g_idx)
                e.indirect_dma_start(rows[0][:, 0, :], None, table,
                                     bass.IndirectOffsetOnAxis(ap=ki[0][:, 0:1], axis=0)).then_inc(g_rows, 16)

            crowded_path(e, gather_chunk)
            g = 0
            for b in range(TILES):
                e.wait_ge(s_idx, b + 1)
                for first, n in halves(b):
                    if g >= RING:
                        e.wait_ge(s_agg, g - RING + 1)
                    for j in range(n):
                        e.indirect_dma_start(
                            rows[g % RING][:, j, :], None, table,
                            bass.IndirectOffsetOnAxis(ap=ki[b % 2][:, first + j:first + j + 1], axis=0),
                        ).then_inc(s_row[g % RING], 16)
                    g += 1
            own = 0
            e.wait_ge(s_bias, 1)
            e.wait_ge(s_const, 16 * N_CONST)
            for c in range(STEPS + 1):
                if c < STEPS:
                    if c >= 2:
                        e.wait_ge(s_out[c % 2], 16 * (c // 2))
                    for i, t in enumerate(tiles_of(c)):
                        e.tensor_scalar(res[c % 2][:, i, :], X[:, t, :], rs2[:, t:t + 1], nmr2[:, t:t + 1],
                                        ALU.mult, ALU.add).then_inc(s_pool, 1)
                    own += len(tiles_of(c))
                    e.wait_ge(s_pool, own)
                    for i, t in enumerate(tiles_of(c)):
                        e.tensor_tensor(res[c % 2][:, i, :], res[c % 2][:, i, :], bias[:, :], ALU.add).then_inc(s_xr, 1)
                        e.tensor_tensor(X[:, t, :], X[:, t, :], bet[:, :], ALU.add).then_inc(s_pool, 1)
                    own += len(tiles_of(c))
                if c >= 1:
                    e.wait_ge(s_ln, c)
                    e.wait_ge(s_pool, own)
                    for i, t in enumerate(tiles_of(c - 1)):
                        e.tensor_tensor(res[(c - 1) % 2][:, i, :], res[(c - 1) % 2][:, i, :], gam[:, :],
                                        ALU.mult).then_inc(s_pool, 1)
                    own += len(tiles_of(c - 1))
                    e.wait_ge(s_pool, own)
                    for i, t in enumerate(tiles_of(c - 1)):
                        ins = e.tensor_tensor(res[(c - 1) % 2][:, i, :], res[(c - 1) % 2][:, i, :], X[:, t, :], ALU.add)
                    ins.then_inc(s_fin, 1)

        @block.scalar
        def _(e):
            e.wait_ge(s_edges, 32)
            for b in range(1, TILES):
                e.activation(sign_out[0:EDGE_ROWS, :], src_in[0:EDGE_ROWS, :], ACT.Sign, bias=b * P - 0.5, scale=-1.0,
                             accum_out=sign_sum[0:EDGE_ROWS, b:b + 1]).then_inc(s_sign, 1)
                e.wait_ge(s_sign, b)

            def normalise(q):
                if q >= 2:
                    e.wait_ge(s_tp, 2 * (q - 1))
                for i, t in enumerate(tiles_of(q)):
                    e.wait_ge(s_stat, t // XGROUP + 1)
                    e.activation(xn_in[q % 2][:, i, :], X[:, t, :], ACT.Identity, bias=nmr[:, t:t + 1],
                                 scale=rs[:, t:t + 1]).then_inc(s_xn, 1)

            def copy_m(q):
                for i in range((len(tiles_of(q)) + 1) // 2):
                    e.wait_ge(s_m, 2 * q + i + 1)
                    if q >= 2:
                        e.wait_ge(s_mst[q % 2], stores_of(q - 2))
                    n = min(2, len(tiles_of(q)) - 2 * i)
                    e.activation(m_out[q % 2][:, 2 * i:2 * i + n, :].rearrange("p a b -> p (a b)"),
                                 bank[4 + i][:, 0:n * D], ACT.Copy).then_inc(s_mc, 1)

            normalise(0)
            e.wait_ge(s_const, 16 * N_CONST)
            for step in plan:
                if step[0] == "mlp":
                    q = step[1]
                    n = len(tiles_of(q)) * P
                    for k in range(KD):
                        e.wait_ge(s_tp, 2 * q + k + 1)
                        if q >= 2 and k == 0:
                            e.wait_ge(s_h, 2 * (q - 1))
                        e.activation(xn_t[q % 2][:, k, 0:n], bank[k][:, 0:n], ACT.Copy).then_inc(s_xt, 1)
                    if q + 1 < STEPS:
                        normalise(q + 1)
                    for m in range(KD):
                        e.wait_ge(s_h, 2 * q + m + 1)
                        if q >= 2 and m == 0:
                            e.wait_ge(s_m, 2 * (q - 1))
                        e.activation(hid_t[q % 2][:, m, 0:n], bank[2 + m][:, 0:n], ACT.Relu,
                                     bias=b1s[:, m:m + 1]).then_inc(s_relu, 1)
                    if q >= 1:
                        copy_m(q - 1)
                    if q == STEPS - 1:
                        copy_m(q)
                else:
                    _, k, back = step
                    no = turn_no(k, back)
                    if not back:
                        r = 1 << (k - LOG_SLOTS - 1)
                        for h in range(2):
                            e.wait_ge(s_kt, 2 * no + h + 1)
                            v = bank[6 + h][:, :].rearrange("p (n c r) -> p n c r", c=2, r=r)
                            e.activation(key_high[:, h * 256:(h + 1) * 256].rearrange("p (n r) -> p n r", r=r),
                                         v[:, :, 1, :], ACT.Copy).then_inc(s_kc, 1)
                    else:
                        e.wait_ge(s_kt, 2 * no + 2)
                        e.activation(key_high[:, :], bank[7][:, :], ACT.Copy).then_inc(s_kc, 1)

            for b in range(TILES + 1):
                if b < TILES:
                    e.wait_ge(s_tu, b + 1)
                    e.activation(UT[b % 2][:, :, :].rearrange("p a b -> p (a b)"), bank[2][:, 0:D], ACT.Copy)\
                        .then_inc(s_ut, 1)
                    e.wait_ge(s_hc, b + 1)
                    if b >= 2:
                        e.wait_ge(s_g, b - 1)
                    for m in range(KD):
                        e.activation(HC[b % 2][:, m, :], bank[3][:, m * P:(m + 1) * P], ACT.Relu,
                                     bias=b1s[:, m:m + 1]).then_inc(s_rc, 1)
                if b >= 1:
                    t = b - 1
                    n = P if t < TILES - 1 else LAST
                    e.wait_ge(s_tx, t + 1)
                    for k in range(KD):
                        e.activation(XT[:, t, k, 0:n], bank[5][:, k * P:k * P + n], ACT.Identity,
                                     accum_out=colsum[:, k, t:t + 1]).then_inc(s_txc, 1)
            e.wait_ge(s_dif, 1)
            e.activation(R[:, 2, :], R[:, 1, :], ACT.Exp).then_inc(s_exp, 1)

            for c in range(STEPS):
                tok = len(tiles_of(c)) * P if c < STEPS - 1 else LAST
                for i in range(TOP_K):
                    for m in range(KF):
                        f = i * KF + m
                        n = c * TOP_K * KF + f
                        if n == 0:
                            e.wait_ge(s_eb, 32 * TOP_K)
                        e.wait_ge(s_eh, n + 1)
                        if c >= 2 and f == 0:
                            e.wait_ge(s_y, tiles_of(c - 2)[-1] + 1)
                        e.activation(act[c % 2][:, f, 0:tok], bank[n % 4][:, 0:tok], ACT.Gelu,
                                     bias=eb1[:, i, m:m + 1]).then_inc(s_gelu, 1)

        @block.tensor
        def _(e):
            e.wait_ge(s_masks, 32)
            e.wait_ge(s_const, 16 * N_CONST)
            e.wait_ge(s_xpad, 2)
            e.wait_ge(s_sign, TILES - 1)
            e.matmul(bank[6][0:1, 1:TILES], ones[0:EDGE_ROWS, 0:1], sign_sum[0:EDGE_ROWS, 1:TILES],
                     start=True, stop=True).then_inc(s_bnd, 1)

            def transposes(q):
                e.wait_ge(s_xn, tiles_of(q)[-1] + 1)
                if q >= 1:
                    e.wait_ge(s_xt, 2 * q)
                for k in range(KD):
                    for i in range(len(tiles_of(q))):
                        ins = e.transpose(bank[k][:, i * P:(i + 1) * P], xn_in[q % 2][:, i, k * P:(k + 1) * P], ident)
                    ins.then_inc(s_tp, 1)

            def hidden(q):
                n = len(tiles_of(q)) * P
                e.wait_ge(s_xt, 2 * q + 2)
                if q >= 1:
                    e.wait_ge(s_relu, 2 * q)
                for m in range(KD):
                    for k in range(KD):
                        ins = e.matmul(bank[2 + m][:, 0:n], w1s[:, k, m * P:(m + 1) * P], xn_t[q % 2][:, k, 0:n],
                                       start=(k == 0), stop=(k == KD - 1))
                    ins.then_inc(s_h, 1)

            def second(q):
                e.wait_ge(s_relu, 2 * q + 2)
                if q >= 1:
                    e.wait_ge(s_mc, 2 * q)
                n = len(tiles_of(q))
                for i in range(n):
                    o = bank[4 + i // 2][:, (i % 2) * D:(i % 2 + 1) * D]
                    for k in range(KD):
                        e.matmul(o, hid_t[q % 2][:, k, i * P:(i + 1) * P], w2s[:, k, :], start=(k == 0), stop=False)
                    ins = e.matmul(o, ones[0:1, :], b2s[0:1, :], start=False, stop=True)
                    if i % 2 or i == n - 1:
                        ins.then_inc(s_m, 1)

            for step in plan:
                if step[0] == "mlp":
                    q = step[1]
                    transposes(q)
                    hidden(q)
                    if q >= 1:
                        second(q - 1)
                    if q == STEPS - 1:
                        second(q)
                else:
                    _, k, back = step
                    no = turn_no(k, back)
                    for h in range(2):
                        e.wait_ge(s_kv, 2 * no + h + 1)
                        source = turn_in(k, back).bitcast(F32)
                        for g in range(4):
                            ins = e.transpose(bank[6 + h][:, g * P:(g + 1) * P],
                                              source[:, (4 * h + g) * P:(4 * h + g + 1) * P], ident)
                        ins.then_inc(s_kt, 1)

            def sums(b, h):
                g = 2 * b + h
                first, n = halves(b)[h]
                e.wait_ge(s_oh, g + 1)
                e.wait_ge(s_row[g % RING], 16 * rows_until[g])
                if h == 0 and b >= 2:
                    e.wait_ge(s_u, b - 1)
                for j in range(n):
                    ins = e.matmul(bank[b % 2][:, 0:D], onehot[g % 2][:, j, :], rows[g % RING][:, j, :],
                                   start=(first + j == 0), stop=(first + j == BUCKET_TILES[b] - 1))
                ins.then_inc(s_agg, 1)

            def turn_u(b):
                e.wait_ge(s_u, b + 1)
                if b >= 1:
                    e.wait_ge(s_ut, b)
                for k in range(KD):
                    ins = e.transpose(bank[2][:, k * P:(k + 1) * P], U[b % 2][:, k * P:(k + 1) * P], ident)
                ins.then_inc(s_tu, 1)

            def hidden2(b):
                e.wait_ge(s_ut, b + 1)
                if b >= 1:
                    e.wait_ge(s_rc, 2 * b)
                for m in range(KD):
                    for k in range(KD):
                        ins = e.matmul(bank[3][:, m * P:(m + 1) * P], w1s[:, k, m * P:(m + 1) * P], UT[b % 2][:, k, :],
                                       start=(k == 0), stop=(k == KD - 1))
                ins.then_inc(s_hc, 1)

            def second2(b):
                e.wait_ge(s_rc, 2 * b + 2)
                if b >= 1:
                    e.wait_ge(s_x1, b)
                for k in range(KD):
                    e.matmul(bank[4][:, 0:D], HC[b % 2][:, k, :], w2s[:, k, :], start=(k == 0), stop=False)
                e.matmul(bank[4][:, 0:D], ones[0:1, :], b2s[0:1, :], start=False, stop=True).then_inc(s_g, 1)

            def turn_x(b):
                e.wait_ge(s_xb, b + 1)
                if b >= 1:
                    e.wait_ge(s_txc, 2 * b)
                for k in range(KD):
                    ins = e.transpose(bank[5][:, k * P:(k + 1) * P], XB[b % 2][:, k * P:(k + 1) * P], ident)
                ins.then_inc(s_tx, 1)

            e.wait_ge(s_starts, 2)
            e.wait_ge(s_sorted, 1)
            e.matmul(bank[6][:, 0:1], ones[0:1, :], fits[0:1, 0:1], start=True, stop=True).then_inc(s_keep, 1)

            gathered = e.alloc_register("gathered")
            e.reg_mov(gathered, 0)

            def sum_chunk(pair, chunk):
                e.reg_add(gathered, gathered, 16)
                e.wait_ge(g_rows, e.snap(gathered))
                for h in range(2):
                    ins = e.matmul(bank[7][:, h * D:(h + 1) * D], onehot[0][:, h, :], rows[0][:, 0, :],
                                   start=True, stop=True)
                ins.then_inc(g_sum, 1)

            crowded_path(e, sum_chunk)
            for b in range(TILES + 2):
                if 1 <= b <= TILES:
                    turn_u(b - 1)
                if b < TILES:
                    sums(b, 0)
                if 1 <= b <= TILES:
                    hidden2(b - 1)
                    second2(b - 1)
                if b < TILES:
                    sums(b, 1)
                if b >= 2:
                    turn_x(b - 2)

            e.wait_ge(s_msum, 1)
            for k in range(KD):
                ins = e.matmul(bank[6][0:1, 0:EXPERTS], msum[:, k:k + 1], wrs[:, k, :], start=(k == 0), stop=(k == KD - 1))
            ins.then_inc(s_logit, 1)
            e.wait_ge(s_route, 1)
            e.matmul(bank[6][:, 0:TOP_K], ones[0:1, :], wts[0:1, :], start=True, stop=True).then_inc(s_wbp, 1)

            def expert_hidden(c):
                tiles = tiles_of(c)
                tok = len(tiles) * P if c < STEPS - 1 else LAST
                for i in range(TOP_K):
                    for m in range(KF):
                        n = c * TOP_K * KF + i * KF + m
                        if n >= 4:
                            e.wait_ge(s_gelu, n - 3)
                        for k in range(KD):
                            moving = XT[:, tiles[0]:tiles[-1] + 1, k, :] if tok > P else XT[:, tiles[0], k, 0:tok]
                            o = bank[n % 4][:, 0:tok]
                            if tok > P:
                                o = o.rearrange("p (a b) -> p a b", b=P)
                            ins = e.matmul(o, ew1[:, i * KD + k, m * P:(m + 1) * P], moving,
                                           start=(k == 0), stop=(k == KD - 1))
                        ins.then_inc(s_eh, 1)

            def expert_out(c):
                for i, t in enumerate(tiles_of(c)):
                    n = P if t < TILES - 1 else LAST
                    if i == 0:
                        e.wait_ge(s_gelu, (c + 1) * TOP_K * KF)
                    if t >= 2:
                        e.wait_ge(s_yr, t - 1)
                    for f in range(TOP_K * KF):
                        ins = e.matmul(bank[4 + t % 2][0:n, 0:D], act[c % 2][:, f, i * P:i * P + n], ew2[:, f, :],
                                       start=(f == 0), stop=(f == TOP_K * KF - 1))
                    ins.then_inc(s_y, 1)

            e.wait_ge(s_ew1, 16 * TOP_K)
            for c in range(STEPS + 1):
                if c < STEPS:
                    expert_hidden(c)
                if c == 1:
                    e.wait_ge(s_w2s, TOP_K)
                if c >= 1:
                    expert_out(c - 1)

        @block.vector
        def _(e):
            own = [0]

            def step(ins):
                own[0] += 1
                ins.then_inc(s_own, 1)

            def settle():
                e.wait_ge(s_own, own[0])

            def chain(ins):
                step(ins)
                settle()

            def rsqrt(y, v, t, w):
                chain(e.tensor_scalar(w, v, EPS, None, ALU.add))
                chain(e.tensor_scalar(y.bitcast(I32), w.bitcast(I32), -0.5, 1597463007.0, ALU.mult, ALU.add))
                for _ in range(3):
                    chain(e.tensor_tensor(t, y, y, ALU.mult))
                    chain(e.tensor_tensor(t, t, w, ALU.mult))
                    chain(e.tensor_scalar(t, t, -0.5, 1.5, ALU.mult, ALU.add))
                    chain(e.tensor_tensor(y, y, t, ALU.mult))

            def minus_mean(o, mean, y):
                return e.scalar_tensor_tensor(out=o, in0=mean, scalar=-1.0, in1=y, op0=ALU.mult, op1=ALU.mult)

            def kf(i):
                return key[i][:, :].bitcast(F32)

            chain(e.memset(key[0][:, :], KEY_NONE))
            e.wait_ge(s_edges, 32)
            chain(e.tensor_scalar(key[1][0:EDGE_ROWS, 0:EDGE_COLS], src_in[0:EDGE_ROWS, :], NODE_BITS, KEY_TOP,
                                  ALU.logical_shift_left, ALU.bitwise_or))
            chain(e.tensor_tensor(key[0][0:EDGE_ROWS, 0:EDGE_COLS], key[1][0:EDGE_ROWS, 0:EDGE_COLS],
                                  dst_in[0:EDGE_ROWS, :], ALU.bitwise_or))
            v = key[0][:, :].rearrange("p (n c r) -> p n c r", c=2, r=2)
            chain(e.tensor_scalar(v[:, :, 1, :], v[:, :, 1, :], KEY_BITS, None, ALU.bitwise_xor))
            e.wait_ge(s_masks, 32)
            cur = [0]

            def stage(j, last=None):
                s, o = kf(cur[0]), kf(1 - cur[0])
                sv = s.rearrange("p (n c r) -> p n c r", c=2, r=1 << j)
                ov = o.rearrange("p (n c r) -> p n c r", c=2, r=1 << j)
                step(e.tensor_tensor(ov[:, :, 0, :], sv[:, :, 0, :], sv[:, :, 1, :], ALU.min))
                ins = e.tensor_tensor(ov[:, :, 1, :], sv[:, :, 0, :], sv[:, :, 1, :], ALU.max)
                if last is None:
                    step(ins)
                else:
                    ins.then_inc(last, 1)

            def flip(k):
                c = key[cur[0]]
                if k + 1 < LOG_SLOTS:
                    v = c[:, :].rearrange("p (n c r) -> p n c r", c=4, r=1 << k)
                    chain(e.tensor_scalar(v[:, :, 1:3, :], v[:, :, 1:3, :], KEY_BITS, None, ALU.bitwise_xor))
                elif k + 1 == LOG_SLOTS:
                    h = SLOTS // 2
                    step(e.tensor_scalar(c[:, 0:h], c[:, 0:h], masks[:, 0:1], None, ALU.bitwise_xor))
                    step(e.tensor_scalar(c[:, h:], c[:, h:], masks[:, 1:2], None, ALU.bitwise_xor))
                    settle()
                else:
                    m = 2 + k - LOG_SLOTS
                    for h in range(2):
                        a, z = h * SLOTS // 2, (h + 1) * SLOTS // 2
                        e.tensor_scalar(c[:, a:z], c[:, a:z], masks[:, m:m + 1], None, ALU.bitwise_xor).then_inc(s_kv, 1)

            def free_merge(k):
                for j in reversed(range(k)):
                    stage(j)
                    settle()
                    cur[0] = 1 - cur[0]
                flip(k)

            for k in range(1, 6):
                free_merge(k)

            for j in range(TILES // XGROUP):
                e.wait_ge(s_x[j], 32 if j == TILES // XGROUP - 1 else 16)
                for i in range(XGROUP):
                    step(e.bn_stats(stat[:, i, :], X[:, j * XGROUP + i, :]))
                settle()
                for i in range(XGROUP):
                    step(e.bn_aggr(mv[:, j * XGROUP + i, :], stat[:, i, :]))
                settle()
                g = slice(j * XGROUP, (j + 1) * XGROUP)
                rsqrt(rs[:, g], mv[:, g, 1], rq[0][:, :], rq[1][:, :])
                minus_mean(nmr[:, g], mv[:, g, 0], rs[:, g]).then_inc(s_stat, 1)

            e.wait_ge(s_bnd, 1)
            chain(e.memset(startf[:, 0:1], 0.0))
            chain(e.memset(startf[:, TILES:TILES + 1], float(EDGES)))
            chain(e.tensor_scalar(startf[:, 1:TILES], bank[6][0:1, 1:TILES], float(EDGES), 0.5, ALU.add, ALU.mult))
            chain(e.tensor_copy(starts[:, :], startf[:, :]))
            chain(e.tensor_tensor(over[:, :], startf[:, 1:TILES + 1], startf[:, 0:TILES], ALU.subtract))
            for b, z in ((0, TILES - 1), (TILES - 1, TILES)):
                chain(e.tensor_scalar(over[:, b:z], over[:, b:z], float(-BUCKET_TILES[b] * P), None, ALU.add))
            chain(e.tensor_reduce(fits[:, 1:2], over[:, :], AX.X, ALU.max))
            e.tensor_scalar(fits[:, 0:1], fits[:, 1:2], 0.0, None, ALU.is_le).then_inc(s_starts, 1)
            e.tensor_scalar(crowded[:, :], fits[:, 1:2], 0.0, None, ALU.is_gt).then_inc(s_starts, 1)

            for k in range(6, LOG_SLOTS + 1):
                free_merge(k)

            halfn = SLOTS // 2
            for k in range(LOG_SLOTS + 1, LOG_ALL + 1):
                assert turn_in(k, 0) is key[cur[0]]
                no = turn_no(k, 0)
                top = k - LOG_SLOTS - 1
                r = 1 << top
                o = kf(1 - cur[0])
                for h in range(2):
                    e.wait_ge(s_kc, 3 * (k - LOG_SLOTS - 1) + h + 1)
                    lo_ = bank[6 + h][:, :].rearrange("p (n c r) -> p n c r", c=2, r=r)[:, :, 0, :]
                    hi_ = key_high[:, h * 256:(h + 1) * 256].rearrange("p (n r) -> p n r", r=r)
                    ov = o[:, h * halfn:(h + 1) * halfn].rearrange("p (n c r) -> p n c r", c=2, r=r)
                    step(e.tensor_tensor(ov[:, :, 0, :], lo_, hi_, ALU.min))
                    last = e.tensor_tensor(ov[:, :, 1, :], lo_, hi_, ALU.max)
                    if top == 0:
                        last.then_inc(s_kv, 1)
                    else:
                        step(last)
                cur[0] = 1 - cur[0]
                if top:
                    e.wait_ge(s_kt, 2 * no + 2)
                    settle()
                for j in reversed(range(top)):
                    s, o = kf(cur[0]), kf(1 - cur[0])
                    for h in range(2):
                        a, z = h * halfn, (h + 1) * halfn
                        sv = s[:, a:z].rearrange("p (n c r) -> p n c r", c=2, r=1 << j)
                        ov = o[:, a:z].rearrange("p (n c r) -> p n c r", c=2, r=1 << j)
                        step(e.tensor_tensor(ov[:, :, 0, :], sv[:, :, 0, :], sv[:, :, 1, :], ALU.min))
                        last = e.tensor_tensor(ov[:, :, 1, :], sv[:, :, 0, :], sv[:, :, 1, :], ALU.max)
                        if j == 0:
                            last.then_inc(s_kv, 1)
                        else:
                            step(last)
                    if j:
                        settle()
                    cur[0] = 1 - cur[0]
                assert turn_in(k, 1) is key[cur[0]]
                e.wait_ge(s_kc, 3 * (k - LOG_SLOTS - 1) + 3)
                settle()
                o = kf(1 - cur[0])
                step(e.tensor_tensor(o[:, 0:halfn], bank[6][:, :], key_high[:, :], ALU.min))
                step(e.tensor_tensor(o[:, halfn:], bank[6][:, :], key_high[:, :], ALU.max))
                settle()
                cur[0] = 1 - cur[0]
                for j in reversed(range(LOG_SLOTS - 1)):
                    stage(j, last=s_sorted if (k, j) == (LOG_ALL, 0) else None)
                    settle()
                    cur[0] = 1 - cur[0]
                if k < LOG_ALL:
                    flip(k)
            assert cur[0] == SORTED_IN

            def unpack(b):
                n = BUCKET_TILES[b]
                e.wait_ge(s_kload[b % 4], 16 * (b // 4 + 1))
                if b >= 2:
                    e.wait_ge(s_agg, 2 * b - 2)
                k = kt[b % 4]
                chain(e.tensor_scalar(klo[:, 0:n], k[:, 0:n], NODE_BITS, NODE_MASK, ALU.logical_shift_right,
                                      ALU.bitwise_and))
                step(e.tensor_scalar(lo[b % 2][:, 0:n], klo[:, 0:n], float(-b * P), None, ALU.add))
                e.tensor_scalar(ki[b % 2][:, 0:n], k[:, 0:n], NODE_MASK, None, ALU.bitwise_and).then_inc(s_idx, 1)
                settle()

            def one_hot(b, h):
                g = 2 * b + h
                first, n = halves(b)[h]
                if g >= 2:
                    e.wait_ge(s_agg, g - 1)
                e.tensor_tensor(onehot[g % 2][:, 0:n, :], iota.unsqueeze(1).broadcast_to([P, n, P]),
                                lo[b % 2][:, first:first + n].unsqueeze(2).broadcast_to([P, n, P]),
                                ALU.is_equal).then_inc(s_oh, 1)

            def sum_in(b):
                if b >= 2:
                    e.wait_ge(s_tu, b - 1)
                u = U[b % 2][:, :]
                chain(e.tensor_scalar(u, X[:, b, :], rs[:, b:b + 1], nmr[:, b:b + 1], ALU.mult, ALU.add))
                chain(e.tensor_tensor(u, u, XT[:, b, :, :].rearrange("p a b -> p (a b)"), ALU.add))
                e.wait_ge(s_agg, 2 * b + 2)
                e.scalar_tensor_tensor(out=u, in0=bank[b % 2][:, 0:D], scalar=keep[:, 0:1], in1=u,
                                       op0=ALU.mult, op1=ALU.add).then_inc(s_u, 1)

            def residual(b):
                e.wait_ge(s_g, b + 1)
                e.tensor_tensor(X[:, b, :], X[:, b, :], bank[4][:, 0:D], ALU.add).then_inc(s_x1, 1)
                e.wait_ge(s_x1, b + 1)
                chain(e.bn_stats(stat2[:, :], X[:, b, :]))
                chain(e.bn_aggr(mv2[:, b, :], stat2[:, :]))
                rsqrt(rs2[:, b:b + 1], mv2[:, b, 1:2], rq[0][:, 0:1], rq[1][:, 0:1])
                chain(minus_mean(nmr2[:, b:b + 1], mv2[:, b, 0:1], rs2[:, b:b + 1]))
                if b >= 2:
                    e.wait_ge(s_tx, b - 1)
                e.tensor_scalar(XB[b % 2][:, :], X[:, b, :], rs2[:, b:b + 1], nmr2[:, b:b + 1], ALU.mult, ALU.add)\
                    .then_inc(s_xb, 1)

            e.wait_ge(s_extra, 1)
            for i in range(2):
                e.wait_ge(s_mst[i], 16 * len(range(i, STEPS, 2)))
            e.wait_ge(s_list, 16)
            e.wait_ge(s_keep, 1)
            chain(e.tensor_copy(keep[:, :], bank[6][:, 0:1]))

            def add_chunk(pair, chunk):
                def one(ins):
                    ins.then_inc(g_own, 1)
                    taken(e, g_own)

                taken(e, g_load, 16)
                k = kt[0][:, 0:1]
                one(e.tensor_scalar(klo[:, 0:1], k, NODE_BITS, NODE_MASK, ALU.logical_shift_right, ALU.bitwise_and))
                for h in range(2):
                    one(e.tensor_scalar(lo[0][:, h:h + 1], klo[:, 0:1], float(-(pair + h) * P), None, ALU.add))
                    one(e.tensor_scalar(onehot[0][:, h, :], iota, lo[0][:, h:h + 1], None, ALU.is_equal))
                e.tensor_scalar(ki[0][:, 0:1], k, NODE_MASK, None, ALU.bitwise_and).then_inc(g_idx, 1)
                taken(e, g_sum)
                for h in range(min(2, TILES - pair)):
                    extra = XT[:, pair + h, :, :].rearrange("p a b -> p (a b)")
                    one(e.tensor_tensor(extra, extra, bank[7][:, h * D:(h + 1) * D], ALU.add))
                e.memset(klo[:, 0:1], 0).then_inc(g_done, 1)

            crowded_path(e, add_chunk)
            unpack(0)
            for b in range(TILES + 2):
                if b < TILES:
                    one_hot(b, 0)
                if 1 <= b <= TILES:
                    sum_in(b - 1)
                if b + 1 < TILES:
                    unpack(b + 1)
                if b < TILES:
                    one_hot(b, 1)
                if b >= 2:
                    residual(b - 2)

            e.wait_ge(s_txc, 2 * TILES)
            e.tensor_reduce(msum[:, :], colsum[:, :, :], AX.X, ALU.add).then_inc(s_msum, 1)
            free = [3]

            def row(n=EXPERTS):
                free[0] += 1
                return R[:, free[0] - 1, 0:n]

            def exp_small(d, n):
                acc = row(n)
                chain(e.memset(acc, 1.0))
                for k in range(8, 0, -1):
                    chain(e.scalar_tensor_tensor(out=acc, in0=acc, scalar=1.0 / k, in1=d, op0=ALU.mult, op1=ALU.mult))
                    chain(e.tensor_scalar(acc, acc, 1.0, None, ALU.add))
                return acc

            def over_sum(v):
                t, o = row(1), row()
                chain(e.tensor_reduce(t, v, AX.X, ALU.add))
                chain(e.reciprocal(t, t))
                chain(e.tensor_scalar(o, v, t, None, ALU.mult))
                return o

            def less_max(v, o):
                t = row(1)
                chain(e.tensor_reduce(t, v, AX.X, ALU.max))
                return e.tensor_scalar(o, v, t, None, ALU.subtract)

            e.wait_ge(s_logit, 1)
            logits = R[:, 0, :]
            chain(e.scalar_tensor_tensor(out=logits, in0=bank[6][0:1, 0:EXPERTS], scalar=1.0 / N, in1=brs[:, :],
                                         op0=ALU.mult, op1=ALU.add))
            less_max(logits, R[:, 1, :]).then_inc(s_dif, 1)
            e.wait_ge(s_exp, 1)
            probs = over_sum(R[:, 2, :])
            scale, capped = row(), row()
            chain(e.tensor_scalar(scale, probs, float(N), 1.0, ALU.mult, ALU.max))
            chain(e.reciprocal(scale, scale))
            chain(e.tensor_scalar(scale, scale, CAPACITY, 1.0, ALU.mult, ALU.min))
            chain(e.tensor_tensor(capped, probs, scale, ALU.mult))
            dif = row()
            chain(less_max(capped, dif))
            weights = over_sum(exp_small(dif, EXPERTS))
            best, at = [], []
            for i in range(TOP_K):
                m, t, a = row(1), row(), row(1)
                chain(e.tensor_reduce(m, weights, AX.X, ALU.max))
                chain(e.tensor_scalar(t, weights, m, None, ALU.is_equal))
                down = row()
                chain(e.tensor_scalar(down, iota[0:1, 0:EXPERTS], -1.0, float(EXPERTS), ALU.mult, ALU.add))
                chain(e.tensor_tensor(t, t, down, ALU.mult))
                chain(e.tensor_reduce(a, t, AX.X, ALU.max))
                chain(e.tensor_scalar(a, a, -1.0, float(EXPERTS), ALU.mult, ALU.add))
                chain(e.tensor_copy(chosen[:, i:i + 1], a))
                best.append(m)
                if i + 1 < TOP_K:
                    chain(e.tensor_scalar(t, iota[0:1, 0:EXPERTS], a, -2.0, ALU.is_equal, ALU.mult))
                    left = row()
                    chain(e.tensor_tensor(left, weights, t, ALU.add))
                    weights = left
            d, tot = row(1), row(1)
            chain(e.tensor_tensor(d, best[1], best[0], ALU.subtract))
            ex = exp_small(d, 1)
            chain(e.tensor_scalar(tot, ex, 1.0, None, ALU.add))
            chain(e.reciprocal(wts[:, 0:1], tot))
            e.tensor_tensor(wts[:, 1:2], ex, wts[:, 0:1], ALU.mult).then_inc(s_route, 1)

            e.wait_ge(s_wbp, 1)
            chain(e.tensor_copy(wb[:, :], bank[6][:, 0:TOP_K]))
            e.wait_ge(s_eb, 32 * TOP_K)
            chain(e.tensor_scalar(bias[:, :], eb2[:, 0, :], wb[:, 0:1], None, ALU.mult))
            e.scalar_tensor_tensor(out=bias[:, :], in0=eb2[:, 1, :], scalar=wb[:, 1:2], in1=bias[:, :],
                                   op0=ALU.mult, op1=ALU.add).then_inc(s_bias, 1)
            e.wait_ge(s_ew2, 16 * TOP_K)
            for i in range(TOP_K):
                w = ew2[:, i * KF:(i + 1) * KF, :]
                e.tensor_scalar(w, w, wb[:, i:i + 1], None, ALU.mult).then_inc(s_w2s, 1)

            for c in range(STEPS):
                tiles = tiles_of(c)
                r = res[c % 2]
                n = P if c < STEPS - 1 else LAST
                for i, t in enumerate(tiles):
                    e.wait_ge(s_xr, t + 1)
                    e.wait_ge(s_y, t + 1)
                    e.tensor_tensor(r[0:n, i, :], r[0:n, i, :], bank[4 + t % 2][0:n, 0:D], ALU.add).then_inc(s_yr, 1)
                    if i:
                        step(e.bn_stats(stat3[:, i - 1, :], r[:, i - 1, :]))
                    e.wait_ge(s_yr, t + 1)
                step(e.bn_stats(stat3[:, len(tiles) - 1, :], r[:, len(tiles) - 1, :]))
                settle()
                for i in range(len(tiles)):
                    step(e.bn_aggr(mv3[:, i, :], stat3[:, i, :]))
                settle()
                g = slice(0, len(tiles))
                rsqrt(rs3[:, g], mv3[:, g, 1], rq[0][:, g], rq[1][:, g])
                chain(minus_mean(nmr3[:, g], mv3[:, g, 0], rs3[:, g]))
                for i in range(len(tiles)):
                    ins = e.tensor_scalar(r[:, i, :], r[:, i, :], rs3[:, i:i + 1], nmr3[:, i:i + 1], ALU.mult, ALU.add)
                ins.then_inc(s_ln, 1)


_INS = ["x", "src", "dst", "L0_gnn_w1", "L0_gnn_b1", "L0_gnn_w2", "L0_gnn_b2", "L0_ffn_Wr", "L0_ffn_br",
        "L0_ffn_W1", "L0_ffn_b1", "L0_ffn_W2", "L0_ffn_b2", "L0_ffn_gamma", "L0_ffn_beta"]


def constants():
    import numpy as np
    p = np.arange(P)
    cf = np.concatenate([np.eye(P), np.broadcast_to(p, (P, P))], axis=1).astype(np.float32)
    ci = np.zeros((P, 16), np.int32)
    ci[:, 0] = KEY_BITS * (p & 1)
    ci[:, 1] = KEY_BITS * (1 - (p & 1))
    for k in range(LOG_SLOTS, LOG_ALL):
        m = k - LOG_SLOTS
        ci[:, 2 + m] = KEY_BITS * ((p >> m ^ p >> (m + 1)) & 1)
    return cf, ci


def kernel(**inputs):
    import numpy as np
    import concourse.bacc as bacc
    from concourse.bass_utils import run_bass_kernel_spmd

    nc = bacc.Bacc("TRN2", target_bir_lowering=False, num_devices=1)
    cf, ci = constants()
    given = {name: np.asarray(inputs[name]) for name in _INS}
    for name in ("L0_gnn_w1", "L0_gnn_w2", "L0_ffn_Wr"):
        given[name] = given[name].reshape(KD, P, -1).transpose(1, 0, 2)
    given["L0_gnn_b1"] = given["L0_gnn_b1"].reshape(KD, P).T
    given["L0_ffn_W1"] = given["L0_ffn_W1"].reshape(EXPERTS, KD, P, F).transpose(0, 2, 1, 3)
    given["L0_ffn_b1"] = given["L0_ffn_b1"].reshape(EXPERTS, KF, P).transpose(0, 2, 1)
    given["L0_ffn_W2"] = given["L0_ffn_W2"].reshape(EXPERTS, KF, P, D).transpose(0, 2, 1, 3)
    given |= {"cf": cf, "ci": ci}
    arrays, args = {}, []
    for name, a in given.items():
        a = np.ascontiguousarray(a)
        arrays[f"in_{name}"] = a
        args.append(nc.dram_tensor(f"in_{name}", a.shape, mybir.dt.from_np(a.dtype), kind="ExternalInput").ap())
    args.append(nc.dram_tensor("out_0", (N, D), F32, kind="ExternalOutput").ap())
    build(nc, *args)
    r = run_bass_kernel_spmd(nc, [arrays], core_ids=[0])
    return r.results[0]["out_0"]
```

```python
from contextlib import ExitStack

import concourse.bass as bass
from concourse import mybir

F32 = mybir.dt.float32
I32 = mybir.dt.int32
BF16 = mybir.dt.bfloat16
F16 = mybir.dt.float16
ALU = mybir.AluOpType
ACT = mybir.ActivationFunctionType
AX = mybir.AxisListType

P = 128
N = 6250
D = 256
EDGES = 100000
F = 512
EXPERTS = 8
TOP_K = 2
EPS = 1e-5
CAPACITY = float(-(-N * 125 // (100 * EXPERTS)))

KD = D // P
KF = F // P
TILES = -(-N // P)
LAST = N - (TILES - 1) * P

SLOTS = 1024
LOG_SLOTS = 10
LOG_ALL = 17
EDGE_ROWS = 125
EDGE_COLS = EDGES // EDGE_ROWS
NODE_BITS = 13
NODE_MASK = (1 << NODE_BITS) - 1
KEY_BITS = (1 << 2 * NODE_BITS) - 1
KEY_TOP = 1 << 2 * NODE_BITS
KEY_NONE = KEY_TOP | NODE_MASK << NODE_BITS

DENSE_PAIRS = 9
PAIR = 2 * P
DENSE_NODES = DENSE_PAIRS * PAIR
CELLS = DENSE_PAIRS * TILES
LOG_P = 7
LOG_PAIR = 8
CELL_BITS = 15
CELL_PAIR_BIT = LOG_PAIR + 13
CELL_GROUPS = 4
RUN = 256
CHUNK = 2
PAIR_CHUNKS = [CHUNK] * (TILES // CHUNK) + [TILES % CHUNK] * (TILES % CHUNK > 0)
CHUNKS = DENSE_PAIRS * len(PAIR_CHUNKS)
SRING = 3
ARING = 3

FIRST = 2 * DENSE_PAIRS
ROUNDS = TILES - FIRST
BUCKET_TILES = [17] * (ROUNDS - 1) + [15]
GROUPS = 3
GROUP = 6
RING = 4
LNORM_MAX = 16.0
HALF_TOP = 14
XGROUP = 7
QTILES = 4


def groups(r):
    n = BUCKET_TILES[r]
    size = -(-n // GROUPS)
    return [(i * size, min(size, n - i * size)) for i in range(GROUPS)]


def schedule():
    room = [6 * r + 2 * i + 1 for r in range(2, ROUNDS - 1) for i in range(GROUPS)]
    batches = []
    for pair in range(DENSE_PAIRS):
        c, z = pair * len(PAIR_CHUNKS), (pair + 1) * len(PAIR_CHUNKS)
        n = len(room) // DENSE_PAIRS
        cuts = [c + (z - c) * i // n for i in range(n + 1)]
        batches += [(pair, range(a, b)) for a, b in zip(cuts, cuts[1:]) if b > a]
    slots = []
    for r in range(ROUNDS):
        for g in range(GROUPS):
            slots += [("gather", r, g), ("cells", range(0))]
    items = []
    for i, (pair, chunks) in enumerate(batches):
        k = room[i * len(room) // len(batches)]
        slots[k] = ("cells", chunks)
        if chunks[-1] == (pair + 1) * len(PAIR_CHUNKS) - 1:
            items += [(k, 2 * pair), (k + 1, 2 * pair + 1)]
    items += [(6 * r + 4, FIRST + r) for r in range(ROUNDS)]
    items.sort()
    starts, t = [], -1
    for k, tile in items:
        t = max(t + 1, k)
        starts.append((t, tile))
    return slots, starts


def build(nc, x, src, dst, w1, b1, w2, b2, wr, br, fw1, fb1, fw2, fb2, gamma, beta, cf, ci, out):
    ctx = ExitStack()
    with ctx:
        def sb(name, shape, dt=F32):
            return ctx.enter_context(nc.sbuf_tensor(name, shape, dt))

        def sem(name):
            return ctx.enter_context(nc.semaphore(name))

        table = nc.dram_tensor("table", (TILES * P, 2 * D), F16, kind="Internal").ap()
        edge_list = nc.dram_tensor("edge_list", (P * SLOTS,), I32, kind="Internal").ap()

        X = sb("X", [P, TILES, D])
        XT = sb("XT", [P, TILES, KD, P])
        MHL = sb("MHL", [P, TILES, 2 * D], F16)
        G_WORDS = 8960
        G = sb("G", [P, G_WORDS])

        def carver(flat, words):
            used = [0]

            def carve(shape, dt=F32):
                n = 1
                for s in shape:
                    n *= s
                if dt in (F16, BF16):
                    n //= 2
                a = flat[:, used[0]:used[0] + n]
                used[0] += n
                assert used[0] <= words, used
                if dt is not F32:
                    a = a.bitcast(dt)
                if len(shape) == 2:
                    a = a.rearrange("p (a b) -> p a b", b=shape[1])
                if len(shape) == 3:
                    a = a.rearrange("p (a b c) -> p a b c", b=shape[1], c=shape[2])
                return a
            return carve, used

        xt_flat = XT[:, :, :, :].rearrange("p a b c -> p (a b c)")
        XT_WORDS = TILES * KD * P
        carve, used = carver(xt_flat, XT_WORDS)
        src_in = carve([EDGE_COLS], I32)
        dst_in = carve([EDGE_COLS], I32)
        sign_out = carve([EDGE_COLS], BF16)
        key_part = [carve([EDGE_COLS]), carve([EDGE_COLS])]
        key = [carve([SLOTS], I32), carve([SLOTS], I32)]
        key_high = carve([SLOTS // 2])
        search_at = used[0]
        xn_in = [carve([QTILES, D]) for _ in range(2)]
        xn_t = [carve([KD, QTILES * P]) for _ in range(2)]
        hid_t = [carve([KD, QTILES * P]) for _ in range(2)]
        used[0] = search_at
        below = carve([CELL_GROUPS, P * SLOTS // RUN])
        run_keys = carve([CELL_GROUPS, RUN], I32)
        cell_keys = carve([CELL_GROUPS, P + 1], I32)
        cell_part = [carve([CELL_GROUPS, P], I32) for _ in range(2)]
        cell_partf = [carve([CELL_GROUPS, P]) for _ in range(2)]
        search_end = used[0]
        carve, used = carver(G, G_WORDS)
        abs_w = [carve([KD, D]) for _ in range(2)]
        abs_b1 = carve([KD])
        abs_b2 = carve([D])
        m_out = [carve([2, D]) for _ in range(2)]
        used[0] = 0
        rows = [carve([GROUP, 2 * D], F16) for _ in range(RING)]
        onehot = [carve([GROUP, P], F16) for _ in range(2)]
        dst_hot = [carve([CHUNK, P], F16) for _ in range(SRING)]
        src_hot = [carve([CHUNK, PAIR], F16) for _ in range(SRING)]
        blocks = [carve([CHUNK, PAIR], F16) for _ in range(ARING)]
        used[0] = 0
        R = carve([64, EXPERTS])[0:1, :, :]
        eb2 = carve([TOP_K, D])
        bias = carve([D])
        gam = carve([D])
        bet = carve([D])
        res = [carve([QTILES, D]) for i in range(2)]
        carve, used = carver(MHL[:, :, :].rearrange("p a b -> p (a b)").bitcast(F32), TILES * D)
        ew1 = carve([TOP_K * KD, F])
        ew2 = carve([TOP_K * KF, D])
        act = [carve([TOP_K * KF, QTILES * P]) for _ in range(2)]

        cfs = sb("cfs", [P, P + PAIR])
        ident = cfs[:, 0:P]
        iota = cfs[:, P:P + PAIR]
        iota16 = sb("iota16", [P, PAIR], F16)
        ones = sb("ones", [P, P])
        masks = sb("masks", [P, 16 + CELL_GROUPS], I32)
        cell_base = masks[:, 16:16 + CELL_GROUPS]
        w1s = sb("w1s", [P, KD, D])
        w2s = sb("w2s", [P, KD, D])
        b1s = sb("b1s", [P, KD])
        b2s = sb("b2s", [1, D])
        wrs = sb("wrs", [P, KD, EXPERTS])
        brs = sb("brs", [1, EXPERTS])
        bound = sb("bound", [1, 4])
        hidden_bound = sb("hidden_bound", [P, KD])
        scales = sb("scales", [P, 2])
        b1_scaled = sb("b1_scaled", [P, KD])
        scale_row = sb("scale_row", [1, P])
        stat = sb("stat", [P, XGROUP, 6])
        mv = sb("mv", [P, TILES, 2])
        rs = sb("rs", [P, TILES])
        nmr = sb("nmr", [P, TILES])
        rq = [sb(f"rq{i}", [P, XGROUP]) for i in range(3)]
        N_STARTS = FIRST // 2 + ROUNDS + 1
        sign_sum = sb("sign_sum", [P, N_STARTS - 2])
        starts = sb("starts", [1, N_STARTS], I32)
        startf = sb("startf", [1, N_STARTS])
        over = sb("over", [1, ROUNDS])
        fits = sb("fits", [1, 2])
        crowded = sb("crowded", [1, 1], I32)
        keep = sb("keep", [P, 1])
        kt = [sb(f"kt{i}", [P, 17], I32) for i in range(4)]
        ki = [sb(f"ki{i}", [P, 17], I32) for i in range(3)]
        klo = sb("klo", [P, 17], I32)
        g_ki = sb("g_ki", [P, 1], I32)
        g_lo = sb("g_lo", [P, KD])
        lo = [sb(f"lo{i}", [P, 17]) for i in range(3)]
        cell_n = sb("cell_n", [P, CELL_GROUPS])
        run_no = sb("run_no", [P, CELL_GROUPS])
        run_no_i = sb("run_no_i", [P, CELL_GROUPS], I32)
        cell_start = sb("cell_start", [P, CELL_GROUPS], I32)
        full = sb("full", [P, CELL_GROUPS + 1])
        dst_in_cell = sb("dst_in_cell", [P, CELL_GROUPS * P])
        src_in_cell = sb("src_in_cell", [P, CELL_GROUPS * P])
        U = [sb(f"U{i}", [P, D]) for i in range(2)]
        UT = [sb("UT", [P, KD, P])] * 2
        HC = [sb("HC", [P, KD, P])] * 2
        XB = [sb(f"XB{i}", [P, D]) for i in range(2)]
        stat2 = sb("stat2", [P, 6])
        mv2 = sb("mv2", [P, TILES, 2])
        rs2 = sb("rs2", [P, TILES])
        nmr2 = sb("nmr2", [P, TILES])
        colsum = sb("colsum", [P, KD, TILES])
        msum = sb("msum", [P, KD])
        chosen = sb("chosen", [1, TOP_K], I32)
        wts = sb("wts", [1, TOP_K])
        wb = sb("wb", [P, TOP_K])
        eb1 = sb("eb1", [P, TOP_K, KF])
        stat3 = sb("stat3", [P, QTILES, 6])
        mv3 = sb("mv3", [P, QTILES, 2])
        rs3 = sb("rs3", [P, QTILES])
        nmr3 = sb("nmr3", [P, QTILES])

        bank = [ctx.enter_context(nc.psum_tensor(f"bank{i}", [P, 512], F32)) for i in range(8)]

        g_onehot = XB[0][:, :].bitcast(F16).rearrange("p (a b) -> p a b", b=P)
        g_row = U[0][:, :].bitcast(F16)
        g_key = kt[3]

        s_edges = sem("s_edges")
        s_masks = sem("s_masks")
        s_const = sem("s_const")
        s_weights = sem("s_weights")
        s_x = [sem(f"s_xload{j}") for j in range(TILES // XGROUP)]
        s_xpad = sem("s_xpad")
        s_extra = sem("s_extra")
        s_own = sem("s_own")
        s_keys = sem("s_keys")
        s_stat = sem("s_stat")
        s_sign = sem("s_sign")
        s_bnd = sem("s_bnd")
        s_starts = sem("s_starts")
        s_kv = sem("s_kv")
        s_kt = sem("s_kt")
        s_kc = sem("s_kc")
        s_sorted = sem("s_sorted")
        s_list = sem("s_list")
        s_xn = sem("s_xn")
        s_tp = sem("s_tp")
        s_xt = sem("s_xt")
        s_h = sem("s_h")
        s_relu = sem("s_relu")
        s_m = sem("s_m")
        s_mc = sem("s_mc")
        s_ml = sem("s_ml")
        s_mst = sem("s_mst")
        s_abs = sem("s_abs")
        s_hb = sem("s_hb")
        s_hbc = sem("s_hbc")
        s_scale = sem("s_scale")
        s_scp = sem("s_scp")
        s_first = sem("s_first")
        s_run = sem("s_run")
        s_runs = sem("s_runs")
        s_cstart = sem("s_cstart")
        s_ckeys = sem("s_ckeys")
        s_part = sem("s_part")
        s_turned = sem("s_turned")
        s_cell = sem("s_cell")
        s_crowd = sem("s_crowd")
        s_hot = sem("s_hot")
        s_blk = sem("s_blk")
        s_ev = sem("s_ev")
        s_mul = sem("s_mul")
        s_kload = [sem(f"s_kload{i}") for i in range(4)]
        s_idx = sem("s_idx")
        s_oh = sem("s_oh")
        s_row = [sem(f"s_row{i}") for i in range(RING)]
        s_agg = sem("s_agg")
        s_u = sem("s_u")
        s_tu = sem("s_tu")
        s_ut = sem("s_ut")
        s_hc = sem("s_hc")
        s_rc = sem("s_rc")
        s_g = sem("s_g2")
        s_x1 = sem("s_x1")
        s_xb = sem("s_xb")
        s_tx = sem("s_tx")
        s_txc = sem("s_txc")
        s_msum = sem("s_msum")
        s_logit = sem("s_logit")
        s_dif = sem("s_dif")
        s_exp = sem("s_exp")
        s_route = sem("s_route")
        s_wbp = sem("s_wbp")
        s_eb = sem("s_eb")
        s_ew1 = sem("s_ew1")
        s_ew2 = sem("s_ew2")
        s_w2s = sem("s_w2s")
        s_bias = sem("s_bias")
        s_eh = sem("s_eh")
        s_gelu = sem("s_gelu")
        s_y = sem("s_y")
        s_xr = sem("s_xr")
        s_yr = sem("s_yr")
        s_ln = sem("s_ln")
        s_fin = sem("s_fin")
        s_out = [sem(f"s_out{i}") for i in range(2)]
        s_pool = sem("s_pool")
        s_keep = sem("s_keep")
        g_load = sem("g_load")
        g_idx = sem("g_idx")
        g_rows = sem("g_rows")
        g_sum = sem("g_sum")
        g_done = sem("g_done")
        g_own = sem("g_own")

        STEPS = -(-TILES // QTILES)
        N_WEIGHTS = 4
        N_CONST = 4

        def tiles_of(q):
            return range(q * QTILES, min((q + 1) * QTILES, TILES))

        plan = []
        n_before = 6
        plan += [("mlp", q) for q in range(n_before)]
        for i, k in enumerate(range(LOG_SLOTS + 1, LOG_ALL + 1)):
            plan += [("turn", k, 0), ("turn", k, 1)]
            if n_before + i < STEPS:
                plan.append(("mlp", n_before + i))
        plan += [("mlp", q) for q in range(n_before + LOG_ALL - LOG_SLOTS, STEPS)]
        n_turns = 2 * (LOG_ALL - LOG_SLOTS)

        def turn_no(k, back):
            return 2 * (k - LOG_SLOTS - 1) + back

        def key_after(stages):
            return stages % 2

        SORTED_IN = key_after(LOG_ALL * (LOG_ALL + 1) // 2)

        def turn_in(k, back):
            return key[key_after(k * (k - 1) // 2 + (k - LOG_SLOTS if back else 0))]

        rows_until, on_slot = [], [0] * RING
        for r in range(ROUNDS):
            for _, n in groups(r):
                on_slot[len(rows_until) % RING] += n
                rows_until.append(on_slot[len(rows_until) % RING])

        BOUNDS = list(range(2, FIRST, 2)) + list(range(FIRST, TILES))
        bound_at = {b: i for i, b in enumerate([0] + BOUNDS + [TILES])}
        PAIRS = list(range(0, TILES, 2))
        assert len(BOUNDS) + 2 == N_STARTS

        slots, items = schedule()
        SLOTS_ALL = items[-1][0] + 6
        place = {tile: s for s, (_, tile) in enumerate(items)}
        PART = 4

        def due(k, after):
            return [(s, tile) for s, (t, tile) in enumerate(items) if t == k - after]

        def slot(k):
            return slots[k] if k < len(slots) else ("cells", range(0))

        def early(k):
            return slot(k)[1][:2] if slot(k)[0] == "cells" else range(0)

        def late(k):
            return slot(k)[1][2:] if slot(k)[0] == "cells" else range(0)

        def cells_of(c):
            pair, i = divmod(c, len(PAIR_CHUNKS))
            first = pair * TILES + i * CHUNK
            return range(first, first + PAIR_CHUNKS[i])

        def crowded_path(e, body):
            with e.If(e.value_load(crowded[0:1, 0:1], min_val=0, max_val=1) > 0):
                for pair in PAIRS:
                    lo_ = e.value_load(starts[0:1, bound_at[pair]:bound_at[pair] + 1], min_val=0, max_val=EDGES)
                    end = bound_at[min(pair + 2, TILES)]
                    hi_ = e.value_load(starts[0:1, end:end + 1], min_val=0, max_val=EDGES)
                    with e.Fori(0, -(-EDGES // P)) as chunk:
                        with e.If(chunk * P < hi_):
                            with e.If((chunk + 1) * P > lo_):
                                body(pair, chunk)

        def since(e, s, n):
            if n:
                e.wait_ge(s, n)

        def taken(e, s, n=1):
            e.wait_ge(s, n)
            e.sem_clear(s)

        block = ctx.enter_context(nc.Block())

        @block.sync
        def _(e):
            e.dma_start(src_in[0:EDGE_ROWS, :], src.rearrange("(p t) -> p t", t=EDGE_COLS)).then_inc(s_edges, 16)
            e.dma_start(dst_in[0:EDGE_ROWS, :], dst.rearrange("(p t) -> p t", t=EDGE_COLS)).then_inc(s_edges, 16)
            e.dma_start(cfs[:, :], cf).then_inc(s_masks, 16)
            e.dma_start(masks[:, :], ci).then_inc(s_masks, 16)
            for a, b in ((w1s[:, :, :], w1), (b1s[:, :], b1), (w2s[:, :, :], w2), (b2s[:, :], b2.unsqueeze(0))):
                e.dma_start(a, b).then_inc(s_weights, 16)
            for j in range(TILES // XGROUP):
                a, z = j * XGROUP, (j + 1) * XGROUP
                if z * P <= N:
                    e.dma_start(X[:, a:z, :], x[a * P:z * P, :].rearrange("(t p) f -> p t f", p=P)).then_inc(s_x[j], 16)
                    continue
                e.dma_start(X[:, a:z - 1, :], x[a * P:(z - 1) * P, :].rearrange("(t p) f -> p t f", p=P)).then_inc(s_x[j], 16)
                e.wait_ge(s_xpad, 1)
                e.dma_start(X[0:LAST, z - 1, :], x[(z - 1) * P:N, :]).then_inc(s_x[j], 16)
            for a, b in ((wrs[:, :, :], wr), (brs[:, :], br.unsqueeze(0))):
                e.dma_start(a, b).then_inc(s_const, 16)
            for q in range(STEPS):
                t = tiles_of(q)
                e.wait_ge(s_ml, 2 * q + (len(t) + 1) // 2)
                e.dma_start(table[t[0] * P:(t[-1] + 1) * P, :].rearrange("(t p) f -> p t f", p=P),
                            MHL[:, t[0]:t[-1] + 1, :]).then_inc(s_mst, 16)
            e.wait_ge(s_sorted, 1)
            e.dma_start(edge_list.rearrange("(p t) -> p t", p=P), key[SORTED_IN][:, :]).then_inc(s_list, 16)
            e.wait_ge(s_list, 16)
            e.wait_ge(s_starts, 1)

            def load_keys(r):
                first = bound_at[FIRST + r]
                at = e.value_load(starts[0:1, first:first + 1], min_val=0, max_val=EDGES)
                if r >= 4:
                    e.wait_ge(s_idx, r - 3)
                n = BUCKET_TILES[r]
                e.dma_start(kt[r % 4][:, 0:n], edge_list[bass.DynSlice(at, n * P)].rearrange("(p t) -> p t", p=P))\
                    .then_inc(s_kload[r % 4], 16)

            for r in range(3):
                load_keys(r)
            e.wait_ge(s_crowd, 2)

            def load_chunk(pair, chunk):
                e.dma_start(g_key[:, 0:1], edge_list[bass.DynSlice(chunk * P, P)].rearrange("(p t) -> p t", p=P))\
                    .then_inc(g_load, 16)
                taken(e, g_done)

            crowded_path(e, load_chunk)
            for r in range(3, ROUNDS):
                load_keys(r)
            e.wait_ge(s_agg, GROUPS * ROUNDS)
            e.wait_ge(s_mul, CHUNKS)
            e.dma_start(gam, gamma.unsqueeze(0).broadcast_to([P, D])).then_inc(s_const, 16)
            e.dma_start(bet, beta.unsqueeze(0).broadcast_to([P, D])).then_inc(s_const, 16)
            e.wait_ge(s_route, 1)
            for i in range(TOP_K):
                ex = e.value_load(chosen[0:1, i:i + 1], min_val=0, max_val=EXPERTS - 1)
                e.dma_start(ew1[:, i * KD:(i + 1) * KD, :],
                            fw1[bass.DynSlice(ex, 1), :, :, :].rearrange("a p k f -> p (a k) f")).then_inc(s_ew1, 16)
                e.dma_start(eb1[:, i, :], fb1[bass.DynSlice(ex, 1), :, :].rearrange("a p k -> p (a k)")).then_inc(s_eb, 16)
                e.dma_start(eb2[:, i, :], fb2[bass.DynSlice(ex, 1), :].broadcast_to([P, D])).then_inc(s_eb, 16)
                e.dma_start(ew2[:, i * KF:(i + 1) * KF, :],
                            fw2[bass.DynSlice(ex, 1), :, :, :].rearrange("a p k f -> p (a k) f")).then_inc(s_ew2, 16)
            for c in range(STEPS):
                t = tiles_of(c)
                e.wait_ge(s_fin, c + 1)
                if t[-1] < TILES - 1:
                    e.dma_start(out[t[0] * P:(t[-1] + 1) * P, :].rearrange("(t p) f -> p t f", p=P),
                                res[c % 2][:, 0:len(t), :]).then_inc(s_out[c % 2], 16)
                else:
                    assert len(t) == 1
                    e.dma_start(out[t[0] * P:N, :], res[c % 2][0:LAST, 0, :]).then_inc(s_out[c % 2], 16)
            for i in range(2):
                e.wait_ge(s_out[i], 16 * len(range(i, STEPS, 2)))

        @block.gpsimd
        def _(e):
            e.memset(X[:, TILES - 1, :], 0.0).then_inc(s_xpad, 1)
            e.memset(ones[:, :], 1.0).then_inc(s_xpad, 1)
            e.wait_ge(s_masks, 32)
            e.tensor_copy(iota16[:, :], iota).then_inc(s_xpad, 1)
            for q in range(STEPS):
                for i in range((len(tiles_of(q)) + 1) // 2):
                    t, n = tiles_of(q)[2 * i], min(2, len(tiles_of(q)) - 2 * i)
                    e.wait_ge(s_mc, 2 * q + i + 1)
                    m = m_out[(2 * q + i) % 2][:, 0:n, :]
                    e.tensor_copy(MHL[:, t:t + n, 0:D], m).then_inc(s_pool, 1)
                    e.wait_ge(s_pool, 2 * q + i + 1)
                    e.tensor_tensor(MHL[:, t:t + n, D:2 * D], m, MHL[:, t:t + n, 0:D], ALU.subtract).then_inc(s_ml, 1)
            e.wait_ge(s_mst, 16 * STEPS)

            def gather_chunk(pair, chunk):
                taken(e, g_idx)
                e.indirect_dma_start(g_row, None, table,
                                     bass.IndirectOffsetOnAxis(ap=g_ki[:, 0:1], axis=0)).then_inc(g_rows, 16)

            for g in range(GROUPS * ROUNDS):
                r, h = divmod(g, GROUPS)
                first, n = groups(r)[h]
                if h == 0:
                    e.wait_ge(s_idx, r + 1)
                if g >= RING:
                    e.wait_ge(s_agg, g - RING + 1)
                for j in range(n):
                    e.indirect_dma_start(
                        rows[g % RING][:, j, :], None, table,
                        bass.IndirectOffsetOnAxis(ap=ki[r % 3][:, first + j:first + j + 1], axis=0),
                    ).then_inc(s_row[g % RING], 16)
                if g == 0:
                    e.wait_ge(s_list, 16)
                    e.wait_ge(s_run, 1)
                    for i in range(CELL_GROUPS):
                        e.indirect_dma_start(
                            run_keys[:, i, :], None, edge_list.rearrange("(r t) -> r t", t=RUN),
                            bass.IndirectOffsetOnAxis(ap=run_no_i[:, i:i + 1], axis=0)).then_inc(s_runs, 16)
                if g == 1:
                    e.wait_ge(s_cstart, 1)
                    for i in range(CELL_GROUPS):
                        e.indirect_dma_start(
                            cell_keys[:, i, :], None, edge_list.rearrange("(r t) -> r t", t=1),
                            bass.IndirectOffsetOnAxis(ap=cell_start[:, i:i + 1], axis=0)).then_inc(s_ckeys, 16)
                if g == RING - 1:
                    e.wait_ge(s_crowd, 2)
                    crowded_path(e, gather_chunk)
            own = 2 * STEPS - 1
            e.wait_ge(s_bias, 1)
            e.wait_ge(s_const, 16 * N_CONST)
            for c in range(STEPS + 1):
                if c < STEPS:
                    if c >= 2:
                        e.wait_ge(s_out[c % 2], 16 * (c // 2))
                    for i, t in enumerate(tiles_of(c)):
                        e.tensor_scalar(res[c % 2][:, i, :], X[:, t, :], rs2[:, t:t + 1], nmr2[:, t:t + 1],
                                        ALU.mult, ALU.add).then_inc(s_pool, 1)
                    own += len(tiles_of(c))
                    e.wait_ge(s_pool, own)
                    for i, t in enumerate(tiles_of(c)):
                        e.tensor_tensor(res[c % 2][:, i, :], res[c % 2][:, i, :], bias[:, :], ALU.add).then_inc(s_xr, 1)
                        e.tensor_tensor(X[:, t, :], X[:, t, :], bet[:, :], ALU.add).then_inc(s_pool, 1)
                    own += len(tiles_of(c))
                if c >= 1:
                    e.wait_ge(s_ln, c)
                    e.wait_ge(s_pool, own)
                    for i, t in enumerate(tiles_of(c - 1)):
                        e.tensor_tensor(res[(c - 1) % 2][:, i, :], res[(c - 1) % 2][:, i, :], gam[:, :],
                                        ALU.mult).then_inc(s_pool, 1)
                    own += len(tiles_of(c - 1))
                    e.wait_ge(s_pool, own)
                    for i, t in enumerate(tiles_of(c - 1)):
                        ins = e.tensor_tensor(res[(c - 1) % 2][:, i, :], res[(c - 1) % 2][:, i, :], X[:, t, :], ALU.add)
                    ins.then_inc(s_fin, 1)

        @block.scalar
        def _(e):
            e.wait_ge(s_edges, 32)
            for i, b in enumerate(BOUNDS):
                e.activation(sign_out[0:EDGE_ROWS, :], src_in[0:EDGE_ROWS, :], ACT.Sign, bias=b * P - 0.5, scale=-1.0,
                             accum_out=sign_sum[0:EDGE_ROWS, i:i + 1]).then_inc(s_sign, 1)
                e.wait_ge(s_sign, i + 1)
                if i == 1:
                    e.wait_ge(s_weights, 16 * N_WEIGHTS)
                    for a, w in ((abs_w[0], w1s[:, :, :]), (abs_w[1], w2s[:, :, :]), (abs_b1, b1s[:, :]),
                                 (abs_b2[0:1], b2s[:, :])):
                        e.activation(a, w, ACT.Abs).then_inc(s_abs, 1)
                if i == 3:
                    e.wait_ge(s_hb, 1)
                    e.wait_ge(s_abs, 4)
                    for m in range(KD):
                        e.activation(hidden_bound[:, m:m + 1], bank[7][:, m:m + 1], ACT.Identity,
                                     bias=abs_b1[:, m:m + 1], scale=LNORM_MAX).then_inc(s_hbc, 1)

            def normalise(q):
                if q >= 2:
                    e.wait_ge(s_tp, 2 * (q - 1))
                for i, t in enumerate(tiles_of(q)):
                    e.wait_ge(s_stat, t // XGROUP + 1)
                    e.activation(xn_in[q % 2][:, i, :], X[:, t, :], ACT.Identity, bias=nmr[:, t:t + 1],
                                 scale=rs[:, t:t + 1]).then_inc(s_xn, 1)

            def copy_m(q):
                for i in range((len(tiles_of(q)) + 1) // 2):
                    e.wait_ge(s_m, 2 * q + i + 1)
                    since(e, s_ml, max(2 * q + i - 1, 0))
                    n = min(2, len(tiles_of(q)) - 2 * i)
                    e.activation(m_out[(2 * q + i) % 2].rearrange("p a b -> p (a b)")[:, 0:n * D], bank[4 + i][:, 0:n * D],
                                 ACT.Copy).then_inc(s_mc, 1)

            normalise(0)
            e.wait_ge(s_scale, 2)
            for step in plan:
                if step[0] == "mlp":
                    q = step[1]
                    n = len(tiles_of(q)) * P
                    for k in range(KD):
                        e.wait_ge(s_tp, 2 * q + k + 1)
                        if q >= 2 and k == 0:
                            e.wait_ge(s_h, 2 * (q - 1))
                        e.activation(xn_t[q % 2][:, k, 0:n], bank[k][:, 0:n], ACT.Copy).then_inc(s_xt, 1)
                    if q + 1 < STEPS:
                        normalise(q + 1)
                    for m in range(KD):
                        e.wait_ge(s_h, 2 * q + m + 1)
                        if q >= 2 and m == 0:
                            e.wait_ge(s_m, 2 * (q - 1))
                        e.activation(hid_t[q % 2][:, m, 0:n], bank[2 + m][:, 0:n], ACT.Relu,
                                     bias=b1_scaled[:, m:m + 1], scale=scales[:, 0:1]).then_inc(s_relu, 1)
                    if q >= 1:
                        copy_m(q - 1)
                    if q == STEPS - 1:
                        copy_m(q)
                else:
                    _, k, back = step
                    no = turn_no(k, back)
                    if not back:
                        r = 1 << (k - LOG_SLOTS - 1)
                        for h in range(2):
                            e.wait_ge(s_kt, 2 * no + h + 1)
                            v = bank[6 + h][:, :].rearrange("p (n c r) -> p n c r", c=2, r=r)
                            e.activation(key_high[:, h * 256:(h + 1) * 256].rearrange("p (n r) -> p n r", r=r),
                                         v[:, :, 1, :], ACT.Copy).then_inc(s_kc, 1)
                    else:
                        e.wait_ge(s_kt, 2 * no + 2)
                        e.activation(key_high[:, :], bank[7][:, :], ACT.Copy).then_inc(s_kc, 1)

            def clear(a, z):
                e.activation(xt_flat[:, a:z], ones[:, 0:1].broadcast_to([P, z - a]), ACT.Copy, scale=0.0)\
                    .then_inc(s_extra, 1)

            e.wait_ge(s_m, 2 * STEPS - 1)
            clear(search_end, XT_WORDS)
            e.wait_ge(s_list, 16)
            e.wait_ge(s_first, 1)
            clear(0, search_at)
            e.wait_ge(s_turned, 1)
            for i, a in enumerate((dst_in_cell, src_in_cell)):
                e.activation(a[:, :], bank[5 + i][:, :], ACT.Copy).then_inc(s_cell, 1)
            clear(search_at, search_end)

            def copy_blocks(chunks):
                for c in chunks:
                    e.wait_ge(s_blk, c + 1)
                    if c >= ARING:
                        e.wait_ge(s_mul, c - ARING + 1)
                    n = len(cells_of(c)) * PAIR
                    e.activation(blocks[c % ARING].rearrange("p a b -> p (a b)")[:, 0:n], bank[3 + c % 2][:, 0:n],
                                 ACT.Copy).then_inc(s_ev, 1)

            for k in range(SLOTS_ALL):
                copy_blocks(early(k + 1))
                copy_blocks(late(k))
                for s, t in due(k, 5):
                    n = P if t < TILES - 1 else LAST
                    e.wait_ge(s_tx, s + 1)
                    for h in range(KD):
                        e.activation(XT[:, t, h, 0:n], bank[5][:, D + h * P:D + h * P + n], ACT.Identity,
                                     accum_out=colsum[:, h, t:t + 1]).then_inc(s_txc, 1)
                for s, t in due(k, 2):
                    e.wait_ge(s_hc, s + 1)
                    since(e, s_g, s)
                    for m in range(KD):
                        e.activation(HC[s % 2][:, m, :], bank[6][:, m * P:(m + 1) * P], ACT.Relu,
                                     bias=b1s[:, m:m + 1]).then_inc(s_rc, 1)
                for s, t in due(k, 1):
                    e.wait_ge(s_tu, s + 1)
                    since(e, s_hc, s)
                    e.activation(UT[s % 2][:, :, :].rearrange("p a b -> p (a b)"), bank[5][:, 0:D], ACT.Copy)\
                        .then_inc(s_ut, 1)
            e.wait_ge(s_dif, 1)
            e.activation(R[:, 2, :], R[:, 1, :], ACT.Exp).then_inc(s_exp, 1)

            for c in range(STEPS):
                tok = len(tiles_of(c)) * P if c < STEPS - 1 else LAST
                for i in range(TOP_K):
                    for m in range(KF):
                        f = i * KF + m
                        n = c * TOP_K * KF + f
                        if n == 0:
                            e.wait_ge(s_eb, 32 * TOP_K)
                        e.wait_ge(s_eh, n + 1)
                        if c >= 2 and f == 0:
                            e.wait_ge(s_y, tiles_of(c - 2)[-1] + 1)
                        e.activation(act[c % 2][:, f, 0:tok], bank[n % 4][:, 0:tok], ACT.Gelu,
                                     bias=eb1[:, i, m:m + 1]).then_inc(s_gelu, 1)

        @block.tensor
        def _(e):
            e.wait_ge(s_masks, 32)
            e.wait_ge(s_xpad, 3)
            e.wait_ge(s_abs, 4)
            for m in range(KD):
                for k in range(KD):
                    ins = e.matmul(bank[7][:, m:m + 1], abs_w[0][:, k, m * P:(m + 1) * P], ones[:, 0:1],
                                   start=(k == 0), stop=(k == KD - 1))
            ins.then_inc(s_hb, 1)
            e.wait_ge(s_hbc, KD)
            for k in range(KD):
                e.matmul(bank[7][0:1, 0:D], hidden_bound[:, k:k + 1], abs_w[1][:, k, :], start=(k == 0), stop=False)
            e.matmul(bank[7][0:1, 0:D], ones[0:1, 0:1], abs_b2[0:1, :], start=False, stop=True).then_inc(s_hb, 1)
            e.wait_ge(s_scale, 1)
            e.matmul(bank[7][:, 0:2], ones[0:1, :], bound[0:1, 2:4], start=True, stop=True).then_inc(s_scp, 1)
            n_bounds = len(BOUNDS)
            e.wait_ge(s_sign, n_bounds)
            e.matmul(bank[6][0:1, 0:n_bounds], ones[0:EDGE_ROWS, 0:1], sign_sum[0:EDGE_ROWS, :],
                     start=True, stop=True).then_inc(s_bnd, 1)
            e.wait_ge(s_scale, 2)

            def transposes(q):
                e.wait_ge(s_xn, tiles_of(q)[-1] + 1)
                if q >= 1:
                    e.wait_ge(s_xt, 2 * q)
                for k in range(KD):
                    for i in range(len(tiles_of(q))):
                        ins = e.transpose(bank[k][:, i * P:(i + 1) * P], xn_in[q % 2][:, i, k * P:(k + 1) * P], ident)
                    ins.then_inc(s_tp, 1)

            def hidden(q):
                n = len(tiles_of(q)) * P
                e.wait_ge(s_xt, 2 * q + 2)
                if q >= 1:
                    e.wait_ge(s_relu, 2 * q)
                for m in range(KD):
                    for k in range(KD):
                        ins = e.matmul(bank[2 + m][:, 0:n], w1s[:, k, m * P:(m + 1) * P], xn_t[q % 2][:, k, 0:n],
                                       start=(k == 0), stop=(k == KD - 1))
                    ins.then_inc(s_h, 1)

            def second(q):
                e.wait_ge(s_relu, 2 * q + 2)
                if q >= 1:
                    e.wait_ge(s_mc, 2 * q)
                n = len(tiles_of(q))
                for i in range(n):
                    o = bank[4 + i // 2][:, (i % 2) * D:(i % 2 + 1) * D]
                    for k in range(KD):
                        e.matmul(o, hid_t[q % 2][:, k, i * P:(i + 1) * P], w2s[:, k, :], start=(k == 0), stop=False)
                    ins = e.matmul(o, scale_row[0:1, :], b2s[0:1, :], start=False, stop=True)
                    if i % 2 or i == n - 1:
                        ins.then_inc(s_m, 1)

            for step in plan:
                if step[0] == "mlp":
                    q = step[1]
                    transposes(q)
                    hidden(q)
                    if q >= 1:
                        second(q - 1)
                    if q == STEPS - 1:
                        second(q)
                else:
                    _, k, back = step
                    no = turn_no(k, back)
                    for h in range(2):
                        e.wait_ge(s_kv, 2 * no + h + 1)
                        source = turn_in(k, back).bitcast(F32)
                        for g in range(4):
                            ins = e.transpose(bank[6 + h][:, g * P:(g + 1) * P],
                                              source[:, (4 * h + g) * P:(4 * h + g + 1) * P], ident)
                        ins.then_inc(s_kt, 1)

            e.wait_ge(s_sorted, 1)
            last_keys = key[SORTED_IN][:, :].bitcast(F32)
            for i in range(SLOTS // RUN):
                ins = e.transpose(bank[5][:, i * P:(i + 1) * P], last_keys[:, i * RUN:i * RUN + 1].broadcast_to([P, P]),
                                  ident)
            ins.then_inc(s_first, 1)

            def sums(r, h):
                g = GROUPS * r + h
                first, n = groups(r)[h]
                e.wait_ge(s_oh, g + 1)
                e.wait_ge(s_row[g % RING], 16 * rows_until[g])
                if h == 0 and r >= 1:
                    e.wait_ge(s_u, place[FIRST + r - 1] + 1)
                for j in range(n):
                    ins = e.matmul(bank[0][:, :], onehot[g % 2][:, j, :], rows[g % RING][:, j, :],
                                   start=(first + j == 0), stop=(first + j == BUCKET_TILES[r] - 1))
                ins.then_inc(s_agg, 1)

            def make_blocks(c):
                e.wait_ge(s_hot, c + 1)
                if c >= 2:
                    e.wait_ge(s_ev, c - 1)
                for i in range(len(cells_of(c))):
                    ins = e.matmul(bank[3 + c % 2][:, i * PAIR:(i + 1) * PAIR], dst_hot[c % SRING][:, i, :],
                                   src_hot[c % SRING][:, i, :], start=True, stop=True)
                ins.then_inc(s_blk, 1)

            def multiply(c):
                for i, cell in enumerate(cells_of(c)):
                    pair, t = divmod(cell, TILES)
                    if t == 0 and pair:
                        e.wait_ge(s_u, place[2 * pair - 1] + 1)
                    for h in range(2):
                        ins = e.matmul(bank[1 + h][:, :], blocks[c % ARING][:, i, h * P:(h + 1) * P], MHL[:, t, :],
                                       start=(t == 0), stop=(t == TILES - 1))
                ins.then_inc(s_mul, 1)

            def turn_u(s):
                e.wait_ge(s_u, s + 1)
                since(e, s_ut, turned[0])
                since(e, s_txc, 2 * turned[1])
                for k in range(KD):
                    ins = e.transpose(bank[5][:, k * P:(k + 1) * P], U[s % 2][:, k * P:(k + 1) * P], ident)
                ins.then_inc(s_tu, 1)
                turned[0] += 1

            def hidden2(s):
                e.wait_ge(s_ut, s + 1)
                since(e, s_rc, 2 * s)
                for m in range(KD):
                    for k in range(KD):
                        ins = e.matmul(bank[6][:, m * P:(m + 1) * P], w1s[:, k, m * P:(m + 1) * P], UT[s % 2][:, k, :],
                                       start=(k == 0), stop=(k == KD - 1))
                ins.then_inc(s_hc, 1)

            def second2(s):
                e.wait_ge(s_rc, 2 * s + 2)
                since(e, s_x1, s)
                for k in range(KD):
                    e.matmul(bank[7][:, 0:D], HC[s % 2][:, k, :], w2s[:, k, :], start=(k == 0), stop=False)
                e.matmul(bank[7][:, 0:D], ones[0:1, :], b2s[0:1, :], start=False, stop=True).then_inc(s_g, 1)

            def turn_x(s):
                e.wait_ge(s_xb, s + 1)
                since(e, s_ut, turned[0])
                since(e, s_txc, 2 * turned[1])
                for k in range(KD):
                    ins = e.transpose(bank[5][:, D + k * P:D + (k + 1) * P], XB[s % 2][:, k * P:(k + 1) * P], ident)
                ins.then_inc(s_tx, 1)
                turned[1] += 1

            def turn_cells():
                e.wait_ge(s_part, 1)
                for i in range(2):
                    for g in range(CELL_GROUPS):
                        e.transpose(bank[5 + i][:, g * P:(g + 1) * P], cell_partf[i][:, g, :], ident)
                e.matmul(bank[7][0:1, 0:1], ones[:, 0:1], full[:, CELL_GROUPS:CELL_GROUPS + 1], start=True, stop=True)\
                    .then_inc(s_turned, 1)

            gathered = e.alloc_register("gathered")
            e.reg_mov(gathered, 0)

            def sum_chunk(pair, chunk):
                e.reg_add(gathered, gathered, 16)
                e.wait_ge(g_rows, e.snap(gathered))
                for h in range(2):
                    ins = e.matmul(bank[6 + h][:, :], g_onehot[:, h, :], g_row, start=True, stop=True)
                ins.then_inc(g_sum, 1)

            turned = [0, 0]
            for k in range(SLOTS_ALL):
                if k == PART:
                    turn_cells()
                for c in early(k + 1):
                    make_blocks(c)
                if slot(k)[0] == "gather":
                    sums(*slot(k)[1:])
                else:
                    chunks = slot(k)[1]
                    for c in chunks:
                        e.wait_ge(s_ev, c + 1)
                        if c + 2 in chunks:
                            make_blocks(c + 2)
                        multiply(c)
                if k == PART:
                    e.wait_ge(s_crowd, 2)
                    e.wait_ge(s_cell, 2)
                    e.matmul(bank[7][:, 0:1], ones[0:1, :], fits[0:1, 0:1], start=True, stop=True).then_inc(s_keep, 1)
                    crowded_path(e, sum_chunk)
                for s, _ in due(k, 5):
                    turn_x(s)
                for s, _ in due(k, 3):
                    second2(s)
                for s, _ in due(k, 2):
                    hidden2(s)
                for s, _ in due(k, 1):
                    turn_u(s)

            e.wait_ge(s_msum, 1)
            for k in range(KD):
                ins = e.matmul(bank[6][0:1, 0:EXPERTS], msum[:, k:k + 1], wrs[:, k, :], start=(k == 0), stop=(k == KD - 1))
            ins.then_inc(s_logit, 1)
            e.wait_ge(s_route, 1)
            e.matmul(bank[6][:, 0:TOP_K], ones[0:1, :], wts[0:1, :], start=True, stop=True).then_inc(s_wbp, 1)

            def expert_hidden(c):
                tiles = tiles_of(c)
                tok = len(tiles) * P if c < STEPS - 1 else LAST
                for i in range(TOP_K):
                    for m in range(KF):
                        n = c * TOP_K * KF + i * KF + m
                        if n >= 4:
                            e.wait_ge(s_gelu, n - 3)
                        for k in range(KD):
                            moving = XT[:, tiles[0]:tiles[-1] + 1, k, :] if tok > P else XT[:, tiles[0], k, 0:tok]
                            o = bank[n % 4][:, 0:tok]
                            if tok > P:
                                o = o.rearrange("p (a b) -> p a b", b=P)
                            ins = e.matmul(o, ew1[:, i * KD + k, m * P:(m + 1) * P], moving,
                                           start=(k == 0), stop=(k == KD - 1))
                        ins.then_inc(s_eh, 1)

            def expert_out(c):
                for i, t in enumerate(tiles_of(c)):
                    n = P if t < TILES - 1 else LAST
                    if i == 0:
                        e.wait_ge(s_gelu, (c + 1) * TOP_K * KF)
                    if t >= 2:
                        e.wait_ge(s_yr, t - 1)
                    for f in range(TOP_K * KF):
                        ins = e.matmul(bank[4 + t % 2][0:n, 0:D], act[c % 2][:, f, i * P:i * P + n], ew2[:, f, :],
                                       start=(f == 0), stop=(f == TOP_K * KF - 1))
                    ins.then_inc(s_y, 1)

            e.wait_ge(s_ew1, 16 * TOP_K)
            for c in range(STEPS + 1):
                if c < STEPS:
                    expert_hidden(c)
                if c == 1:
                    e.wait_ge(s_w2s, TOP_K)
                if c >= 1:
                    expert_out(c - 1)

        @block.vector
        def _(e):
            own = [0]

            def step(ins):
                own[0] += 1
                ins.then_inc(s_own, 1)

            def settle():
                e.wait_ge(s_own, own[0])

            def chain(ins):
                step(ins)
                settle()

            def rsqrt(y, v, t, w):
                chain(e.tensor_scalar(w, v, EPS, None, ALU.add))
                chain(e.tensor_scalar(y.bitcast(I32), w.bitcast(I32), -0.5, 1597463007.0, ALU.mult, ALU.add))
                for _ in range(3):
                    chain(e.tensor_tensor(t, y, y, ALU.mult))
                    chain(e.tensor_tensor(t, t, w, ALU.mult))
                    chain(e.tensor_scalar(t, t, -0.5, 1.5, ALU.mult, ALU.add))
                    chain(e.tensor_tensor(y, y, t, ALU.mult))

            def minus_mean(o, mean, y):
                return e.scalar_tensor_tensor(out=o, in0=mean, scalar=-1.0, in1=y, op0=ALU.mult, op1=ALU.mult)

            def kf(i):
                return key[i][:, :].bitcast(F32)

            chain(e.memset(key[0][:, :], KEY_NONE))
            e.wait_ge(s_edges, 32)
            s_, d_ = src_in[0:EDGE_ROWS, :], dst_in[0:EDGE_ROWS, :]
            k_, h_ = key[0][0:EDGE_ROWS, 0:EDGE_COLS], key[1][0:EDGE_ROWS, 0:EDGE_COLS]
            a_, b_ = key_part[0][0:EDGE_ROWS, :], key_part[1][0:EDGE_ROWS, :]
            top = NODE_MASK & ~(PAIR - 1)
            step(e.tensor_scalar(a_, s_, float(DENSE_NODES), float(PAIR - 1), ALU.is_lt, ALU.mult))
            step(e.tensor_scalar(b_, s_, float(DENSE_NODES), float(-NODE_MASK), ALU.is_lt, ALU.mult))
            step(e.tensor_scalar(h_, s_, PAIR - 1, None, ALU.bitwise_and))
            settle()
            step(e.scalar_tensor_tensor(out=a_, in0=a_, scalar=1.0, in1=d_, op0=ALU.add, op1=ALU.mult))
            step(e.scalar_tensor_tensor(out=b_, in0=b_, scalar=float(NODE_MASK + 1), in1=h_, op0=ALU.add, op1=ALU.mult))
            settle()
            step(e.tensor_scalar(h_, s_, top, 1 << NODE_BITS, ALU.bitwise_and, ALU.bitwise_or))
            step(e.tensor_tensor(k_, a_, b_, ALU.add))
            settle()
            chain(e.tensor_scalar(h_, h_, NODE_BITS, None, ALU.logical_shift_left))
            chain(e.tensor_tensor(k_, k_, h_, ALU.bitwise_or))
            v = key[0][:, :].rearrange("p (n c r) -> p n c r", c=2, r=2)
            chain(e.tensor_scalar(v[:, :, 1, :], v[:, :, 1, :], KEY_BITS, None, ALU.bitwise_xor))
            e.wait_ge(s_masks, 32)
            cur = [0]

            def stage(j, last=None):
                s, o = kf(cur[0]), kf(1 - cur[0])
                sv = s.rearrange("p (n c r) -> p n c r", c=2, r=1 << j)
                ov = o.rearrange("p (n c r) -> p n c r", c=2, r=1 << j)
                step(e.tensor_tensor(ov[:, :, 0, :], sv[:, :, 0, :], sv[:, :, 1, :], ALU.min))
                ins = e.tensor_tensor(ov[:, :, 1, :], sv[:, :, 0, :], sv[:, :, 1, :], ALU.max)
                if last is None:
                    step(ins)
                else:
                    ins.then_inc(last, 1)

            def flip(k):
                c = key[cur[0]]
                if k + 1 < LOG_SLOTS:
                    v = c[:, :].rearrange("p (n c r) -> p n c r", c=4, r=1 << k)
                    chain(e.tensor_scalar(v[:, :, 1:3, :], v[:, :, 1:3, :], KEY_BITS, None, ALU.bitwise_xor))
                elif k + 1 == LOG_SLOTS:
                    h = SLOTS // 2
                    step(e.tensor_scalar(c[:, 0:h], c[:, 0:h], masks[:, 0:1], None, ALU.bitwise_xor))
                    step(e.tensor_scalar(c[:, h:], c[:, h:], masks[:, 1:2], None, ALU.bitwise_xor))
                    settle()
                else:
                    m = 2 + k - LOG_SLOTS
                    for h in range(2):
                        a, z = h * SLOTS // 2, (h + 1) * SLOTS // 2
                        e.tensor_scalar(c[:, a:z], c[:, a:z], masks[:, m:m + 1], None, ALU.bitwise_xor).then_inc(s_kv, 1)

            def free_merge(k):
                for j in reversed(range(k)):
                    stage(j)
                    settle()
                    cur[0] = 1 - cur[0]
                flip(k)

            for k in range(1, 6):
                free_merge(k)
                if k == 3:
                    e.wait_ge(s_hb, 2)
                    b, bi = bound, bound[:, :].bitcast(I32)
                    one_bit = 1 << 23
                    chain(e.tensor_reduce(b[:, 0:1], bank[7][0:1, 0:D], AX.X, ALU.max))
                    chain(e.tensor_scalar(b[:, 0:1], b[:, 0:1], 1e-18, 1e18, ALU.max, ALU.min))
                    chain(e.tensor_scalar(bi[:, 1:2], bi[:, 0:1], 0xff * one_bit, None, ALU.bitwise_and))
                    chain(e.tensor_scalar(bi[:, 2:3], bi[:, 1:2], -1.0, float((2 * 127 + HALF_TOP) * one_bit),
                                          ALU.mult, ALU.add))
                    chain(e.tensor_scalar(bi[:, 3:4], bi[:, 1:2], float(-HALF_TOP * one_bit), None, ALU.add))
                    e.tensor_scalar(scale_row[:, :], ones[0:1, :], b[:, 2:3], None, ALU.mult).then_inc(s_scale, 1)
                    e.wait_ge(s_scp, 1)
                    chain(e.tensor_copy(scales[:, :], bank[7][:, 0:2]))
                    e.tensor_scalar(b1_scaled[:, :], b1s[:, :], scales[:, 0:1], None, ALU.mult).then_inc(s_scale, 1)

            for j in range(TILES // XGROUP):
                e.wait_ge(s_x[j], 32 if j == TILES // XGROUP - 1 else 16)
                for i in range(XGROUP):
                    step(e.bn_stats(stat[:, i, :], X[:, j * XGROUP + i, :]))
                settle()
                for i in range(XGROUP):
                    step(e.bn_aggr(mv[:, j * XGROUP + i, :], stat[:, i, :]))
                settle()
                g = slice(j * XGROUP, (j + 1) * XGROUP)
                rsqrt(rs[:, g], mv[:, g, 1], rq[0][:, :], rq[1][:, :])
                minus_mean(nmr[:, g], mv[:, g, 0], rs[:, g]).then_inc(s_stat, 1)

            e.wait_ge(s_bnd, 1)
            n = N_STARTS - 1
            chain(e.memset(startf[:, 0:1], 0.0))
            chain(e.memset(startf[:, n:n + 1], float(EDGES)))
            chain(e.tensor_scalar(startf[:, 1:n], bank[6][0:1, 0:n - 1], float(EDGES), 0.5, ALU.add, ALU.mult))
            chain(e.tensor_copy(starts[:, :], startf[:, :]))
            at = bound_at[FIRST]
            chain(e.tensor_tensor(over[:, :], startf[:, at + 1:], startf[:, at:n], ALU.subtract))
            for a, z in ((0, ROUNDS - 1), (ROUNDS - 1, ROUNDS)):
                chain(e.tensor_scalar(over[:, a:z], over[:, a:z], float(-BUCKET_TILES[a] * P), None, ALU.add))
            e.tensor_reduce(fits[:, 1:2], over[:, :], AX.X, ALU.max).then_inc(s_starts, 1)

            for k in range(6, LOG_SLOTS + 1):
                free_merge(k)

            halfn = SLOTS // 2
            for k in range(LOG_SLOTS + 1, LOG_ALL + 1):
                assert turn_in(k, 0) is key[cur[0]]
                no = turn_no(k, 0)
                top = k - LOG_SLOTS - 1
                r = 1 << top
                o = kf(1 - cur[0])
                for h in range(2):
                    e.wait_ge(s_kc, 3 * (k - LOG_SLOTS - 1) + h + 1)
                    lo_ = bank[6 + h][:, :].rearrange("p (n c r) -> p n c r", c=2, r=r)[:, :, 0, :]
                    hi_ = key_high[:, h * 256:(h + 1) * 256].rearrange("p (n r) -> p n r", r=r)
                    ov = o[:, h * halfn:(h + 1) * halfn].rearrange("p (n c r) -> p n c r", c=2, r=r)
                    step(e.tensor_tensor(ov[:, :, 0, :], lo_, hi_, ALU.min))
                    last = e.tensor_tensor(ov[:, :, 1, :], lo_, hi_, ALU.max)
                    if top == 0:
                        last.then_inc(s_kv, 1)
                    else:
                        step(last)
                cur[0] = 1 - cur[0]
                if top:
                    e.wait_ge(s_kt, 2 * no + 2)
                    settle()
                for j in reversed(range(top)):
                    s, o = kf(cur[0]), kf(1 - cur[0])
                    for h in range(2):
                        a, z = h * halfn, (h + 1) * halfn
                        sv = s[:, a:z].rearrange("p (n c r) -> p n c r", c=2, r=1 << j)
                        ov = o[:, a:z].rearrange("p (n c r) -> p n c r", c=2, r=1 << j)
                        step(e.tensor_tensor(ov[:, :, 0, :], sv[:, :, 0, :], sv[:, :, 1, :], ALU.min))
                        last = e.tensor_tensor(ov[:, :, 1, :], sv[:, :, 0, :], sv[:, :, 1, :], ALU.max)
                        if j == 0:
                            last.then_inc(s_kv, 1)
                        else:
                            step(last)
                    if j:
                        settle()
                    cur[0] = 1 - cur[0]
                assert turn_in(k, 1) is key[cur[0]]
                e.wait_ge(s_kc, 3 * (k - LOG_SLOTS - 1) + 3)
                settle()
                o = kf(1 - cur[0])
                step(e.tensor_tensor(o[:, 0:halfn], bank[6][:, :], key_high[:, :], ALU.min))
                step(e.tensor_tensor(o[:, halfn:], bank[6][:, :], key_high[:, :], ALU.max))
                settle()
                cur[0] = 1 - cur[0]
                for j in reversed(range(LOG_SLOTS - 1)):
                    stage(j, last=s_sorted if (k, j) == (LOG_ALL, 0) else None)
                    settle()
                    cur[0] = 1 - cur[0]
                if k < LOG_ALL:
                    flip(k)
            assert cur[0] == SORTED_IN

            def unpack(r):
                n = BUCKET_TILES[r]
                e.wait_ge(s_kload[r % 4], 16 * (r // 4 + 1))
                if r >= 3:
                    e.wait_ge(s_agg, GROUPS * (r - 2))
                k = kt[r % 4]
                chain(e.tensor_scalar(klo[:, 0:n], k[:, 0:n], NODE_BITS, NODE_MASK, ALU.logical_shift_right,
                                      ALU.bitwise_and))
                step(e.tensor_scalar(lo[r % 3][:, 0:n], klo[:, 0:n], float(-(FIRST + r) * P), None, ALU.add))
                e.tensor_scalar(ki[r % 3][:, 0:n], k[:, 0:n], NODE_MASK, None, ALU.bitwise_and).then_inc(s_idx, 1)
                settle()

            def one_hots(r, h):
                g = GROUPS * r + h
                first, n = groups(r)[h]
                if g >= 2:
                    e.wait_ge(s_agg, g - 1)
                for j in range(n):
                    ins = e.tensor_scalar(onehot[g % 2][:, j, :], iota16[:, 0:P], lo[r % 3][:, first + j:first + j + 1],
                                          None, ALU.is_equal)
                ins.then_inc(s_oh, 1)

            def cell_one_hots(c):
                if c >= SRING:
                    e.wait_ge(s_blk, c - SRING + 1)
                for i, cell in enumerate(cells_of(c)):
                    e.tensor_scalar(dst_hot[c % SRING][:, i, :], iota16[:, 0:P], dst_in_cell[:, cell:cell + 1],
                                    None, ALU.is_equal)
                    ins = e.tensor_scalar(src_hot[c % SRING][:, i, :], iota16[:, :], src_in_cell[:, cell:cell + 1],
                                          None, ALU.is_equal)
                ins.then_inc(s_hot, 1)

            def prepare(k):
                if slot(k)[0] == "gather":
                    one_hots(*slot(k)[1:])
                for c in slot(k)[1] if slot(k)[0] == "cells" else ():
                    if c == 0:
                        e.wait_ge(s_cell, 2)
                    cell_one_hots(c)

            def sum_in(s, t):
                since(e, s_tu, max(s - 1, 0))
                u = U[s % 2][:, :]
                chain(e.tensor_scalar(u, X[:, t, :], rs[:, t:t + 1], nmr[:, t:t + 1], ALU.mult, ALU.add))
                chain(e.tensor_tensor(u, u, XT[:, t, :, :].rearrange("p a b -> p (a b)"), ALU.add))
                if t < FIRST:
                    e.wait_ge(s_mul, (t // 2 + 1) * len(PAIR_CHUNKS))
                    sums = bank[1 + t % 2]
                else:
                    e.wait_ge(s_agg, GROUPS * (t - FIRST + 1))
                    sums = bank[0]
                for i in range(2):
                    ins = e.scalar_tensor_tensor(out=u, in0=sums[:, i * D:(i + 1) * D], scalar=keep[:, 0:1], in1=u,
                                                 op0=ALU.mult, op1=ALU.add)
                    if i == 0:
                        chain(ins)
                ins.then_inc(s_u, 1)

            def residual(s, t):
                e.wait_ge(s_g, s + 1)
                e.tensor_tensor(X[:, t, :], X[:, t, :], bank[7][:, 0:D], ALU.add).then_inc(s_x1, 1)
                e.wait_ge(s_x1, s + 1)
                chain(e.bn_stats(stat2[:, :], X[:, t, :]))
                chain(e.bn_aggr(mv2[:, t, :], stat2[:, :]))
                rsqrt(rs2[:, t:t + 1], mv2[:, t, 1:2], rq[0][:, 0:1], rq[1][:, 0:1])
                chain(minus_mean(nmr2[:, t:t + 1], mv2[:, t, 0:1], rs2[:, t:t + 1]))
                since(e, s_tx, max(s - 1, 0))
                e.tensor_scalar(XB[s % 2][:, :], X[:, t, :], rs2[:, t:t + 1], nmr2[:, t:t + 1], ALU.mult, ALU.add)\
                    .then_inc(s_xb, 1)

            def find_runs():
                e.wait_ge(s_m, 2 * STEPS - 1)
                e.wait_ge(s_first, 1)
                for g in range(CELL_GROUPS):
                    step(e.tensor_scalar(below[:, g, :], bank[5][:, :], cell_base.bitcast(F32)[:, g:g + 1], None, ALU.is_lt))
                settle()
                chain(e.tensor_reduce(cell_n[:, :], below[:, :, :], AX.X, ALU.add))
                chain(e.tensor_scalar(run_no[:, :], cell_n[:, :], -1.0, 0.0, ALU.add, ALU.max))
                e.tensor_copy(run_no_i[:, :], run_no[:, :]).then_inc(s_run, 1)

            def find_cells():
                e.wait_ge(s_runs, 16 * CELL_GROUPS)
                for g in range(CELL_GROUPS):
                    step(e.tensor_scalar(below[:, g, 0:RUN], run_keys.bitcast(F32)[:, g, :],
                                         cell_base.bitcast(F32)[:, g:g + 1], None, ALU.is_lt))
                settle()
                chain(e.tensor_reduce(cell_n[:, :], below[:, :, 0:RUN], AX.X, ALU.add))
                e.scalar_tensor_tensor(out=cell_start[:, :], in0=run_no[:, :], scalar=float(RUN), in1=cell_n[:, :],
                                       op0=ALU.mult, op1=ALU.add).then_inc(s_cstart, 1)

            def split_cells():
                e.wait_ge(s_ckeys, 16 * CELL_GROUPS)
                for g in range(CELL_GROUPS):
                    step(e.tensor_scalar(cell_keys[:, g, :], cell_keys[:, g, :], cell_base[:, g:g + 1], None,
                                         ALU.bitwise_xor))
                settle()
                step(e.tensor_scalar(cell_part[0][:, :, :], cell_keys[:, :, 0:P], CELL_BITS - LOG_P, None,
                                     ALU.logical_shift_right))
                step(e.tensor_scalar(cell_part[1][:, :, :], cell_keys[:, :, 0:P], PAIR - 1, None, ALU.bitwise_and))
                step(e.tensor_scalar(full[:, 0:CELL_GROUPS], cell_keys[:, :, P], float(1 << CELL_BITS), None, ALU.is_lt))
                settle()
                for i in range(2):
                    step(e.tensor_copy(cell_partf[i][:, :, :], cell_part[i][:, :, :]))
                settle()
                e.tensor_reduce(full[:, CELL_GROUPS:CELL_GROUPS + 1], full[:, 0:CELL_GROUPS], AX.X, ALU.add)\
                    .then_inc(s_part, 1)

            def set_flags():
                e.wait_ge(s_turned, 1)
                chain(e.tensor_tensor(fits[:, 1:2], fits[:, 1:2], bank[7][0:1, 0:1], ALU.max))
                e.tensor_scalar(fits[:, 0:1], fits[:, 1:2], 0.0, None, ALU.is_le).then_inc(s_crowd, 1)
                e.tensor_scalar(crowded[:, :], fits[:, 1:2], 0.0, None, ALU.is_gt).then_inc(s_crowd, 1)
                e.wait_ge(s_crowd, 2)
                e.wait_ge(s_keep, 1)
                chain(e.tensor_tensor(keep[:, :], bank[7][:, 0:1], scales[:, 1:2], ALU.mult))

            def add_chunk(pair, chunk):
                def one(ins):
                    ins.then_inc(g_own, 1)
                    taken(e, g_own)

                taken(e, g_load, 16)
                k, ka, kb = g_key[:, 0:1], klo[:, 0:1], klo[:, 1:2]
                if pair < FIRST:
                    one(e.tensor_scalar(ka, k, KEY_TOP | pair // 2 << CELL_PAIR_BIT, None, ALU.bitwise_xor))
                    one(e.tensor_scalar(kb, ka, PAIR - 1, None, ALU.bitwise_and))
                    one(e.tensor_copy(g_lo[:, 1:2], kb))
                    one(e.tensor_scalar(kb, ka, CELL_PAIR_BIT, None, ALU.logical_shift_right))
                    one(e.scalar_tensor_tensor(out=g_lo[:, 0:1], in0=kb, scalar=float(2 * PAIR), in1=g_lo[:, 1:2],
                                               op0=ALU.mult, op1=ALU.add))
                    one(e.tensor_scalar(kb, ka, LOG_PAIR, NODE_MASK, ALU.logical_shift_right, ALU.bitwise_and))
                else:
                    one(e.tensor_scalar(ka, k, NODE_BITS, NODE_MASK, ALU.logical_shift_right, ALU.bitwise_and))
                    one(e.tensor_scalar(g_lo[:, 0:1], ka, float(-pair * P), None, ALU.add))
                    one(e.tensor_scalar(kb, k, NODE_MASK, None, ALU.bitwise_and))
                one(e.tensor_scalar(g_lo[:, 1:2], g_lo[:, 0:1], float(-P), None, ALU.add))
                for h in range(2):
                    one(e.tensor_scalar(g_onehot[:, h, :], iota16[:, 0:P], g_lo[:, h:h + 1], None, ALU.is_equal))
                e.tensor_scalar(g_ki[:, 0:1], kb, float(N - 1), None, ALU.min).then_inc(g_idx, 1)
                taken(e, g_sum)
                for h in range(min(2, TILES - pair)):
                    extra = XT[:, pair + h, :, :].rearrange("p a b -> p (a b)")
                    for i in range(2):
                        one(e.scalar_tensor_tensor(out=extra, in0=bank[6 + h][:, i * D:(i + 1) * D],
                                                   scalar=scales[:, 1:2], in1=extra, op0=ALU.mult, op1=ALU.add))
                e.memset(klo[:, 0:1], 0).then_inc(g_done, 1)

            unpack(0)
            prepare(0)
            find_runs()
            unpack(1)
            for k in range(SLOTS_ALL):
                for s, t in due(k, 4):
                    residual(s, t)
                prepare(k + 2)
                if slot(k)[0] == "gather" and slot(k)[2] == 0 and slot(k)[1] + 2 < ROUNDS:
                    unpack(slot(k)[1] + 2)
                if k == 0:
                    find_cells()
                if k == 2:
                    split_cells()
                if k == PART:
                    set_flags()
                    e.wait_ge(s_extra, 3)
                    crowded_path(e, add_chunk)
                for s, t in due(k, 0):
                    sum_in(s, t)

            e.wait_ge(s_txc, 2 * TILES)
            e.tensor_reduce(msum[:, :], colsum[:, :, :], AX.X, ALU.add).then_inc(s_msum, 1)
            free = [3]

            def row(n=EXPERTS):
                free[0] += 1
                return R[:, free[0] - 1, 0:n]

            def exp_small(d, n):
                acc = row(n)
                chain(e.memset(acc, 1.0))
                for k in range(8, 0, -1):
                    chain(e.scalar_tensor_tensor(out=acc, in0=acc, scalar=1.0 / k, in1=d, op0=ALU.mult, op1=ALU.mult))
                    chain(e.tensor_scalar(acc, acc, 1.0, None, ALU.add))
                return acc

            def over_sum(v):
                t, o = row(1), row()
                chain(e.tensor_reduce(t, v, AX.X, ALU.add))
                chain(e.reciprocal(t, t))
                chain(e.tensor_scalar(o, v, t, None, ALU.mult))
                return o

            def less_max(v, o):
                t = row(1)
                chain(e.tensor_reduce(t, v, AX.X, ALU.max))
                return e.tensor_scalar(o, v, t, None, ALU.subtract)

            e.wait_ge(s_logit, 1)
            logits = R[:, 0, :]
            chain(e.scalar_tensor_tensor(out=logits, in0=bank[6][0:1, 0:EXPERTS], scalar=1.0 / N, in1=brs[:, :],
                                         op0=ALU.mult, op1=ALU.add))
            less_max(logits, R[:, 1, :]).then_inc(s_dif, 1)
            e.wait_ge(s_exp, 1)
            probs = over_sum(R[:, 2, :])
            scale, capped = row(), row()
            chain(e.tensor_scalar(scale, probs, float(N), 1.0, ALU.mult, ALU.max))
            chain(e.reciprocal(scale, scale))
            chain(e.tensor_scalar(scale, scale, CAPACITY, 1.0, ALU.mult, ALU.min))
            chain(e.tensor_tensor(capped, probs, scale, ALU.mult))
            dif = row()
            chain(less_max(capped, dif))
            weights = over_sum(exp_small(dif, EXPERTS))
            best, at = [], []
            for i in range(TOP_K):
                m, t, a = row(1), row(), row(1)
                chain(e.tensor_reduce(m, weights, AX.X, ALU.max))
                chain(e.tensor_scalar(t, weights, m, None, ALU.is_equal))
                down = row()
                chain(e.tensor_scalar(down, iota[0:1, 0:EXPERTS], -1.0, float(EXPERTS), ALU.mult, ALU.add))
                chain(e.tensor_tensor(t, t, down, ALU.mult))
                chain(e.tensor_reduce(a, t, AX.X, ALU.max))
                chain(e.tensor_scalar(a, a, -1.0, float(EXPERTS), ALU.mult, ALU.add))
                chain(e.tensor_copy(chosen[:, i:i + 1], a))
                best.append(m)
                if i + 1 < TOP_K:
                    chain(e.tensor_scalar(t, iota[0:1, 0:EXPERTS], a, -2.0, ALU.is_equal, ALU.mult))
                    left = row()
                    chain(e.tensor_tensor(left, weights, t, ALU.add))
                    weights = left
            d, tot = row(1), row(1)
            chain(e.tensor_tensor(d, best[1], best[0], ALU.subtract))
            ex = exp_small(d, 1)
            chain(e.tensor_scalar(tot, ex, 1.0, None, ALU.add))
            chain(e.reciprocal(wts[:, 0:1], tot))
            e.tensor_tensor(wts[:, 1:2], ex, wts[:, 0:1], ALU.mult).then_inc(s_route, 1)

            e.wait_ge(s_wbp, 1)
            chain(e.tensor_copy(wb[:, :], bank[6][:, 0:TOP_K]))
            e.wait_ge(s_eb, 32 * TOP_K)
            chain(e.tensor_scalar(bias[:, :], eb2[:, 0, :], wb[:, 0:1], None, ALU.mult))
            e.scalar_tensor_tensor(out=bias[:, :], in0=eb2[:, 1, :], scalar=wb[:, 1:2], in1=bias[:, :],
                                   op0=ALU.mult, op1=ALU.add).then_inc(s_bias, 1)
            e.wait_ge(s_ew2, 16 * TOP_K)
            for i in range(TOP_K):
                w = ew2[:, i * KF:(i + 1) * KF, :]
                e.tensor_scalar(w, w, wb[:, i:i + 1], None, ALU.mult).then_inc(s_w2s, 1)

            for c in range(STEPS):
                tiles = tiles_of(c)
                r = res[c % 2]
                n = P if c < STEPS - 1 else LAST
                for i, t in enumerate(tiles):
                    e.wait_ge(s_xr, t + 1)
                    e.wait_ge(s_y, t + 1)
                    e.tensor_tensor(r[0:n, i, :], r[0:n, i, :], bank[4 + t % 2][0:n, 0:D], ALU.add).then_inc(s_yr, 1)
                    if i:
                        step(e.bn_stats(stat3[:, i - 1, :], r[:, i - 1, :]))
                    e.wait_ge(s_yr, t + 1)
                step(e.bn_stats(stat3[:, len(tiles) - 1, :], r[:, len(tiles) - 1, :]))
                settle()
                for i in range(len(tiles)):
                    step(e.bn_aggr(mv3[:, i, :], stat3[:, i, :]))
                settle()
                g = slice(0, len(tiles))
                rsqrt(rs3[:, g], mv3[:, g, 1], rq[0][:, g], rq[1][:, g])
                chain(minus_mean(nmr3[:, g], mv3[:, g, 0], rs3[:, g]))
                for i in range(len(tiles)):
                    ins = e.tensor_scalar(r[:, i, :], r[:, i, :], rs3[:, i:i + 1], nmr3[:, i:i + 1], ALU.mult, ALU.add)
                ins.then_inc(s_ln, 1)


_INS = ["x", "src", "dst", "L0_gnn_w1", "L0_gnn_b1", "L0_gnn_w2", "L0_gnn_b2", "L0_ffn_Wr", "L0_ffn_br",
        "L0_ffn_W1", "L0_ffn_b1", "L0_ffn_W2", "L0_ffn_b2", "L0_ffn_gamma", "L0_ffn_beta"]


def constants():
    import numpy as np
    p = np.arange(P)
    cf = np.concatenate([np.eye(P), np.broadcast_to(np.arange(PAIR), (P, PAIR))], axis=1).astype(np.float32)
    ci = np.zeros((P, 16 + CELL_GROUPS), np.int32)
    for g in range(CELL_GROUPS):
        cell = g * P + p
        number = cell // TILES << CELL_PAIR_BIT - CELL_BITS | cell % TILES
        ci[:, 16 + g] = np.where(cell < CELLS, KEY_TOP | number << CELL_BITS, 0)
    ci[:, 0] = KEY_BITS * (p & 1)
    ci[:, 1] = KEY_BITS * (1 - (p & 1))
    for k in range(LOG_SLOTS, LOG_ALL):
        m = k - LOG_SLOTS
        ci[:, 2 + m] = KEY_BITS * ((p >> m ^ p >> (m + 1)) & 1)
    return cf, ci


def kernel(**inputs):
    import numpy as np
    import concourse.bacc as bacc
    from concourse.bass_utils import run_bass_kernel_spmd

    nc = bacc.Bacc("TRN2", target_bir_lowering=False, num_devices=1)
    cf, ci = constants()
    given = {name: np.asarray(inputs[name]) for name in _INS}
    for name in ("L0_gnn_w1", "L0_gnn_w2", "L0_ffn_Wr"):
        given[name] = given[name].reshape(KD, P, -1).transpose(1, 0, 2)
    given["L0_gnn_b1"] = given["L0_gnn_b1"].reshape(KD, P).T
    given["L0_ffn_W1"] = given["L0_ffn_W1"].reshape(EXPERTS, KD, P, F).transpose(0, 2, 1, 3)
    given["L0_ffn_b1"] = given["L0_ffn_b1"].reshape(EXPERTS, KF, P).transpose(0, 2, 1)
    given["L0_ffn_W2"] = given["L0_ffn_W2"].reshape(EXPERTS, KF, P, D).transpose(0, 2, 1, 3)
    given |= {"cf": cf, "ci": ci}
    arrays, args = {}, []
    for name, a in given.items():
        a = np.ascontiguousarray(a)
        arrays[f"in_{name}"] = a
        args.append(nc.dram_tensor(f"in_{name}", a.shape, mybir.dt.from_np(a.dtype), kind="ExternalInput").ap())
    args.append(nc.dram_tensor("out_0", (N, D), F32, kind="ExternalOutput").ap())
    build(nc, *args)
    r = run_bass_kernel_spmd(nc, [arrays], core_ids=[0])
    return r.results[0]["out_0"]
```

```python
import math
from contextlib import ExitStack

import concourse.bass as bass
from concourse import mybir

F32 = mybir.dt.float32
I32 = mybir.dt.int32
BF16 = mybir.dt.bfloat16
F16 = mybir.dt.float16
ALU = mybir.AluOpType
ACT = mybir.ActivationFunctionType
AX = mybir.AxisListType

P = 128
N = 6250
D = 256
EDGES = 100000
F = 512
EXPERTS = 8
TOP_K = 2
EPS = 1e-5
CAPACITY = float(-(-N * 125 // (100 * EXPERTS)))

KD = D // P
KF = F // P
TILES = -(-N // P)
LAST = N - (TILES - 1) * P

SLOTS = 1024
LOG_SLOTS = 10
LOG_ALL = 17
EDGE_ROWS = 125
EDGE_COLS = EDGES // EDGE_ROWS
NODE_BITS = 13
NODE_MASK = (1 << NODE_BITS) - 1
KEY_BITS = (1 << 2 * NODE_BITS) - 1
KEY_TOP = 1 << 2 * NODE_BITS
KEY_NONE = KEY_TOP | NODE_MASK << NODE_BITS

DENSE_PAIRS = 9
PAIR = 2 * P
DENSE_NODES = DENSE_PAIRS * PAIR
CELLS = DENSE_PAIRS * TILES
LOG_P = P.bit_length() - 1
LOG_PAIR = PAIR.bit_length() - 1
CELL_BITS = LOG_P + LOG_PAIR
CELL_PAIR_BIT = LOG_PAIR + NODE_BITS
CELL_GROUPS = 4
RUN = 256
CHUNK = 2
PAIR_CHUNKS = [CHUNK] * (TILES // CHUNK) + [TILES % CHUNK] * (TILES % CHUNK > 0)
CHUNKS = DENSE_PAIRS * len(PAIR_CHUNKS)
SRING = 4
ARING = 3

FIRST = 2 * DENSE_PAIRS
ROUNDS = TILES - FIRST
BUCKET_TILES = [17] * (ROUNDS - 1) + [15]
GROUPS = 3
GROUP = 6
RING = 4

LNORM_MAX = math.sqrt(D)
XN_SCALE = 1024.0
HALF_TOP = 14
Y_BANKS = 3
XGROUP = 7
QTILES = 4


def groups(r):
    n = BUCKET_TILES[r]
    size = -(-n // GROUPS)
    return [(i * size, min(size, n - i * size)) for i in range(GROUPS)]


def schedule():
    room = [6 * r + 2 * i + 1 for r in range(1, ROUNDS - 1) for i in range(GROUPS)]
    batches = []
    for pair in range(DENSE_PAIRS):
        c, z = pair * len(PAIR_CHUNKS), (pair + 1) * len(PAIR_CHUNKS)
        n = len(room) // DENSE_PAIRS
        cuts = [c + (z - c) * i // n for i in range(n + 1)]
        batches += [(pair, range(a, b)) for a, b in zip(cuts, cuts[1:]) if b > a]
    slots = []
    for r in range(ROUNDS):
        for g in range(GROUPS):
            slots += [("gather", r, g), ("cells", range(0))]
    items = []
    for i, (pair, chunks) in enumerate(batches):
        k = room[i * len(room) // len(batches)]
        slots[k] = ("cells", chunks)
        if chunks[-1] == (pair + 1) * len(PAIR_CHUNKS) - 1:
            items += [(k, 2 * pair), (k + 1, 2 * pair + 1)]
    items += [(6 * r + 4, FIRST + r) for r in range(ROUNDS)]
    items.sort()
    starts, t = [], -1
    for k, tile in items:
        t = max(t + 1, k)
        starts.append((t, tile))
    return slots, starts


def build(nc, x, src, dst, w1, b1, w2, b2, wr, br, fw1, fb1, fw2, fb2, gamma, beta, cf, ci, out):
    ctx = ExitStack()
    with ctx:
        def sb(name, shape, dt=F32):
            return ctx.enter_context(nc.sbuf_tensor(name, shape, dt))

        def sem(name):
            return ctx.enter_context(nc.semaphore(name))

        table = nc.dram_tensor("table", (TILES * P, 2 * D), F16, kind="Internal").ap()
        edge_list = nc.dram_tensor("edge_list", (P * SLOTS,), I32, kind="Internal").ap()

        X = sb("X", [P, TILES, D])
        XT = sb("XT", [P, TILES, KD, P])
        MHL = sb("MHL", [P, TILES, 2 * D], F16)
        G_WORDS = 9216
        G = sb("G", [P, G_WORDS])

        def carver(flat, words):
            used = [0]

            def carve(shape, dt=F32):
                n = 1
                for s in shape:
                    n *= s
                if dt in (F16, BF16):
                    n //= 2
                a = flat[:, used[0]:used[0] + n]
                used[0] += n
                assert used[0] <= words, used
                if dt is not F32:
                    a = a.bitcast(dt)
                if len(shape) == 2:
                    a = a.rearrange("p (a b) -> p a b", b=shape[1])
                if len(shape) == 3:
                    a = a.rearrange("p (a b c) -> p a b c", b=shape[1], c=shape[2])
                return a
            return carve, used

        xt_flat = XT[:, :, :, :].rearrange("p a b c -> p (a b c)")
        XT_WORDS = TILES * KD * P
        carve, used = carver(xt_flat, XT_WORDS)
        src_in = carve([EDGE_COLS], I32)
        dst_in = carve([EDGE_COLS], I32)
        sign_out = carve([EDGE_COLS], BF16)
        key_part = [carve([EDGE_COLS]), carve([EDGE_COLS])]
        key = [carve([SLOTS], I32), carve([SLOTS], I32)]
        key_high = carve([SLOTS // 2])
        x_sum = carve([TILES])
        x_square = carve([TILES])
        stat_tmp = [carve([4 * XGROUP]) for _ in range(2)]
        search_at = used[0]
        xn_in = [carve([QTILES, D]) for _ in range(2)]
        xn_t = [carve([KD, QTILES * P]) for _ in range(2)]
        hid_t = [carve([KD, QTILES * P]) for _ in range(2)]
        used[0] = search_at
        below = carve([CELL_GROUPS, P * SLOTS // RUN])
        run_keys = carve([CELL_GROUPS, RUN], I32)
        cell_keys = carve([CELL_GROUPS, P + 1], I32)
        cell_part = [carve([CELL_GROUPS, P], I32) for _ in range(2)]
        cell_partf = [carve([CELL_GROUPS, P]) for _ in range(2)]
        search_end = used[0]
        carve, used = carver(G, G_WORDS)
        abs_w = [carve([KD, D]) for _ in range(2)]
        abs_b1 = carve([KD])
        abs_b2 = carve([D])
        iota = carve([PAIR])
        m_out = [carve([2, D]) for _ in range(2)]
        b2s = carve([D])[0:1, :]
        b2_part = carve([3, D], BF16)[0:1, :, :]
        b2_rest = carve([D])[0:1, :]
        used[0] = 0
        rows = [carve([GROUP, 2 * D], F16) for _ in range(RING)]
        onehot = [carve([GROUP, P], F16) for _ in range(2)]
        dst_hot = [carve([CHUNK, P], F16) for _ in range(SRING)]
        src_hot = [carve([CHUNK, PAIR], F16) for _ in range(SRING)]
        blocks = [carve([CHUNK, PAIR], F16) for _ in range(ARING)]
        used[0] = 0
        R = carve([64, EXPERTS])[0:1, :, :]
        eb2 = carve([TOP_K, D])
        bias = carve([D])
        gam = carve([D])
        bet = carve([D])
        res = [carve([QTILES, D]) for i in range(2)]
        gelu_first = [carve([QTILES * P]) for _ in range(2)]
        w1_at = used[0]
        w1_in = carve([TOP_K * KD, F])
        w2_at = used[0]
        w2_in = carve([TOP_K * KF, D])
        used[0] = w1_at
        xn_half = [[carve([QTILES * KD, P], F16) for _ in range(2)] for _ in range(2)]
        used[0] = w2_at
        gelu_out = [carve([QTILES * P]) for _ in range(4)]
        carve, used = carver(MHL[:, :, :].rearrange("p a b -> p (a b)").bitcast(F32), TILES * D)
        ew1 = [carve([TOP_K * KD, F], F16) for _ in range(2)]
        ew2 = [carve([TOP_K * KF, D], F16) for _ in range(2)]
        act = [[carve([TOP_K * KF, QTILES * P], F16) for _ in range(2)] for _ in range(2)]

        ident = sb("ident", [P, P])[:, :]
        iota16 = sb("iota16", [P, PAIR], F16)
        ones = sb("ones", [P, P])
        masks = sb("masks", [P, 16 + CELL_GROUPS], I32)
        cell_base = masks[:, 16:16 + CELL_GROUPS]
        w1s = sb("w1s", [P, KD, D])
        w2s = sb("w2s", [P, KD, D])
        b1s = sb("b1s", [P, KD])
        b2_rows = sb("b2_rows", [3, D], BF16)
        ones16 = sb("ones16", [3, P], BF16)
        wrs = sb("wrs", [P, KD, EXPERTS])
        brs = sb("brs", [1, EXPERTS])
        bound = sb("bound", [1, 4])
        hidden_bound = sb("hidden_bound", [P, KD])
        scales = sb("scales", [P, 2])
        b1_scaled = sb("b1_scaled", [P, KD])
        scale_rows = sb("scale_rows", [3, P], BF16)
        minus_m = sb("minus_m", [P, TILES])
        rs = sb("rs", [P, TILES])
        nmr = sb("nmr", [P, TILES])
        rq = [sb(f"rq{i}", [P, XGROUP]) for i in range(2)]
        N_STARTS = FIRST // 2 + ROUNDS + 1
        sign_sum = sb("sign_sum", [P, N_STARTS - 2])
        starts = sb("starts", [1, N_STARTS], I32)
        sign_total = sb("sign_total", [1, N_STARTS - 2])
        startf = sb("startf", [1, N_STARTS])
        over = sb("over", [1, ROUNDS])
        fits = sb("fits", [1, 2])
        crowded = sb("crowded", [1, 1], I32)
        keep = sb("keep", [P, 1])
        kt = [sb(f"kt{i}", [P, 17], I32) for i in range(4)]
        ki = [sb(f"ki{i}", [P, 17], I32) for i in range(3)]
        klo = sb("klo", [P, 17], I32)
        g_ki = sb("g_ki", [P, 1], I32)
        g_lo = sb("g_lo", [P, KD])
        lo = [sb(f"lo{i}", [P, 17]) for i in range(3)]
        cell_n = sb("cell_n", [P, CELL_GROUPS])
        run_no = sb("run_no", [P, CELL_GROUPS])
        run_no_i = sb("run_no_i", [P, CELL_GROUPS], I32)
        cell_start = sb("cell_start", [P, CELL_GROUPS], I32)
        full = sb("full", [P, CELL_GROUPS + 1])
        dst_in_cell = sb("dst_in_cell", [P, CELL_GROUPS * P])
        src_in_cell = sb("src_in_cell", [P, CELL_GROUPS * P])
        UXB = sb("UXB", [P, 4, D])
        U = [UXB[:, i, :] for i in range(2)]
        UT = [sb("UT", [P, KD, P])] * 2
        HC = [sb("HC", [P, KD, P])] * 2
        XB = [UXB[:, 2 + i, :] for i in range(2)]
        xn_first = [UXB[:, 2 * i:2 * i + 2, :].rearrange("p a b -> p (a b)").bitcast(F16).rearrange("p (a b) -> p a b", b=P)
                    for i in range(2)]
        stat2 = sb("stat2", [P, 6])
        mv2 = sb("mv2", [P, TILES, 2])
        rs2 = sb("rs2", [P, TILES])
        nmr2 = sb("nmr2", [P, TILES])
        colsum = sb("colsum", [P, KD, TILES])
        msum = sb("msum", [P, KD])
        chosen = sb("chosen", [1, TOP_K], I32)
        wts = sb("wts", [1, TOP_K])
        wb = sb("wb", [P, TOP_K])
        abs_sum = sb("abs_sum", [P, 3])
        xsc = sb("xsc", [P, 4, 3])
        inv_h = sb("inv_h", [P, 1])
        inv_y = sb("inv_y", [P, 1])
        eb1 = sb("eb1", [P, TOP_K, KF])
        stat3 = sb("stat3", [P, QTILES, 6])
        mv3 = sb("mv3", [P, QTILES, 2])
        rs3 = sb("rs3", [P, QTILES])

        bank = [ctx.enter_context(nc.psum_tensor(f"bank{i}", [P, 512], F32)) for i in range(8)]

        g_onehot = XB[0][:, :].bitcast(F16).rearrange("p (a b) -> p a b", b=P)
        g_row = U[0][:, :].bitcast(F16)
        g_key = kt[3]

        s_edges = sem("s_edges")
        s_masks = sem("s_masks")
        s_const = sem("s_const")
        s_weights = sem("s_weights")
        s_x = [sem(f"s_xload{j}") for j in range(TILES // XGROUP)]
        s_xpad = sem("s_xpad")
        s_extra = sem("s_extra")
        s_own = sem("s_own")
        s_keys = sem("s_keys")
        s_sum = sem("s_sum")
        s_mean = sem("s_mean")
        s_square = sem("s_square")
        s_stat = sem("s_stat")
        s_bndc = sem("s_bndc")
        s_sign = sem("s_sign")
        s_bnd = sem("s_bnd")
        s_starts = sem("s_starts")
        s_kv = sem("s_kv")
        s_kt = sem("s_kt")
        s_kc = sem("s_kc")
        s_sorted = sem("s_sorted")
        s_list = sem("s_list")
        s_xn = sem("s_xn")
        s_tp = sem("s_tp")
        s_xt = sem("s_xt")
        s_h = sem("s_h")
        s_relu = sem("s_relu")
        s_m = sem("s_m")
        s_mc = sem("s_mc")
        s_ml = sem("s_ml")
        s_mst = sem("s_mst")
        s_b2 = sem("s_b2")
        s_b2r = sem("s_b2r")
        s_abs = sem("s_abs")
        s_hb = sem("s_hb")
        s_hbc = sem("s_hbc")
        s_scale = sem("s_scale")
        s_scp = sem("s_scp")
        s_first = sem("s_first")
        s_run = sem("s_run")
        s_runs = sem("s_runs")
        s_cstart = sem("s_cstart")
        s_ckeys = sem("s_ckeys")
        s_part = sem("s_part")
        s_turned = sem("s_turned")
        s_cell = sem("s_cell")
        s_crowd = sem("s_crowd")
        s_hot = sem("s_hot")
        s_blk = sem("s_blk")
        s_ev = sem("s_ev")
        s_mul = sem("s_mul")
        s_kload = [sem(f"s_kload{i}") for i in range(4)]
        s_idx = sem("s_idx")
        s_oh = sem("s_oh")
        s_row = [sem(f"s_row{i}") for i in range(RING)]
        s_agg = sem("s_agg")
        s_u = sem("s_u")
        s_tu = sem("s_tu")
        s_ut = sem("s_ut")
        s_hc = sem("s_hc")
        s_rc = sem("s_rc")
        s_g = sem("s_g2")
        s_x1 = sem("s_x1")
        s_xb = sem("s_xb")
        s_tx = sem("s_tx")
        s_txc = sem("s_txc")
        s_msum = sem("s_msum")
        s_logit = sem("s_logit")
        s_dif = sem("s_dif")
        s_exp = sem("s_exp")
        s_chosen = sem("s_chosen")
        s_route = sem("s_route")
        s_wbp = sem("s_wbp")
        s_eb = sem("s_eb")
        s_ew1 = [sem(f"s_ew1_{i}") for i in range(TOP_K)]
        s_ew2 = sem("s_ew2")
        s_w2s = sem("s_w2s")
        s_warm = sem("s_warm")
        s_asum = sem("s_asum")
        s_asp = sem("s_asp")
        s_xsc = sem("s_xsc")
        s_wh = [sem(f"s_wh{i}") for i in range(2)]
        s_wl = [sem(f"s_wl{i}") for i in range(2)]
        s_xh = sem("s_xh")
        s_xl = sem("s_xl")
        s_ah = sem("s_ah")
        s_al = sem("s_al")
        s_bias = sem("s_bias")
        s_eh = sem("s_eh")
        s_gelu = sem("s_gelu")
        s_y = sem("s_y")
        s_nmr2 = sem("s_nmr2")
        s_xn1 = sem("s_xn1")
        s_xr = sem("s_xr")
        s_yr = sem("s_yr")
        s_ln = sem("s_ln")
        s_fin = sem("s_fin")
        s_fin_last = sem("s_fin_last")
        s_out = [sem(f"s_out{i}") for i in range(2)]
        s_pool = sem("s_pool")
        s_keep = sem("s_keep")
        g_load = sem("g_load")
        g_idx = sem("g_idx")
        g_rows = sem("g_rows")
        g_sum = sem("g_sum")
        g_done = sem("g_done")
        g_own = sem("g_own")

        STEPS = -(-TILES // QTILES)
        N_WEIGHTS = 4
        COUNT_FIRST = 4
        STAT_MERGES = [7, 8]
        COUNTED = 16
        LONG_TURN = 15
        STAT_BATCHES = [(0, 4 * XGROUP), (4 * XGROUP, TILES)]
        POOL_ENDS = STEPS - 2
        N_CONST = 4

        def tiles_of(q):
            return range(q * QTILES, min((q + 1) * QTILES, TILES))

        BOUNDS = list(range(2, FIRST, 2)) + list(range(FIRST, TILES))
        bound_at = {b: i for i, b in enumerate([0] + BOUNDS + [TILES])}

        plan = []
        n_before = 4
        steps = list(range(STEPS))
        counts = list(range(COUNT_FIRST, len(BOUNDS)))
        plan += [("mlp", steps.pop(0)) for _ in range(n_before)]
        for k in range(LOG_SLOTS + 1, LOG_ALL + 1):
            if k == COUNTED:
                plan.append(("bounds",))
            plan.append(("turn", k, 0))
            if k >= LONG_TURN and steps:
                plan.append(("mlp", steps.pop(0)))
            plan.append(("turn", k, 1))
            if steps:
                plan.append(("mlp", steps.pop(0)))
            if k < COUNTED:
                n = -(-len(counts) // (COUNTED - k))
                plan.append(("count", counts[:n]))
                counts = counts[n:]
        plan += [("mlp", q) for q in steps]
        def turn_no(k, back):
            return 2 * (k - LOG_SLOTS - 1) + back

        def key_after(stages):
            return stages % 2

        SORTED_IN = key_after(LOG_ALL * (LOG_ALL + 1) // 2)

        def turn_in(k, back):
            return key[key_after(k * (k - 1) // 2 + (k - LOG_SLOTS if back else 0))]

        rows_until, on_slot = [], [0] * RING
        for r in range(ROUNDS):
            for _, n in groups(r):
                on_slot[len(rows_until) % RING] += n
                rows_until.append(on_slot[len(rows_until) % RING])

        PAIRS = list(range(0, TILES, 2))
        assert len(BOUNDS) + 2 == N_STARTS

        slots, items = schedule()
        SLOTS_ALL = items[-1][0] + 6
        place = {tile: s for s, (_, tile) in enumerate(items)}
        PART = 4

        def due(k, after):
            return [(s, tile) for s, (t, tile) in enumerate(items) if t == k - after]

        def slot(k):
            return slots[k] if k < len(slots) else ("cells", range(0))

        def early(k):
            return slot(k)[1][:2] if slot(k)[0] == "cells" else range(0)

        def late(k):
            return slot(k)[1][2:] if slot(k)[0] == "cells" else range(0)

        def cells_of(c):
            pair, i = divmod(c, len(PAIR_CHUNKS))
            first = pair * TILES + i * CHUNK
            return range(first, first + PAIR_CHUNKS[i])

        def crowded_path(e, body):
            with e.If(e.value_load(crowded[0:1, 0:1], min_val=0, max_val=1) > 0):
                for pair in PAIRS:
                    lo_ = e.value_load(starts[0:1, bound_at[pair]:bound_at[pair] + 1], min_val=0, max_val=EDGES)
                    end = bound_at[min(pair + 2, TILES)]
                    hi_ = e.value_load(starts[0:1, end:end + 1], min_val=0, max_val=EDGES)
                    with e.Fori(0, -(-EDGES // P)) as chunk:
                        with e.If(chunk * P < hi_):
                            with e.If((chunk + 1) * P > lo_):
                                body(pair, chunk)

        def since(e, s, n):
            if n:
                e.wait_ge(s, n)

        def taken(e, s, n=1):
            e.wait_ge(s, n)
            e.sem_clear(s)

        FB = TOP_K * KF

        def gelu_buf(n):
            return gelu_first[n % 2] if n < FB else gelu_out[n % 4]

        def gelu_free(n):
            if n < FB:
                return max(n - 1, 0)
            return n - 3 if n >= FB + 4 else 0

        def xn_buf(c):
            return xn_first if c == 1 else xn_half[c % 2]

        def tokens_of(c):
            return len(tiles_of(c)) * P if c < STEPS - 1 else LAST

        block = ctx.enter_context(nc.Block())

        @block.sync
        def _(e):
            e.dma_start(src_in[0:EDGE_ROWS, :], src.rearrange("(p t) -> p t", t=EDGE_COLS)).then_inc(s_edges, 16)
            e.dma_start(dst_in[0:EDGE_ROWS, :], dst.rearrange("(p t) -> p t", t=EDGE_COLS)).then_inc(s_edges, 16)
            e.dma_start(ident, cf[:, 0:P]).then_inc(s_masks, 16)
            e.dma_start(iota, cf[:, P:P + PAIR]).then_inc(s_masks, 16)
            e.dma_start(masks[:, :], ci).then_inc(s_masks, 16)
            for a, b in ((w1s[:, :, :], w1), (b1s[:, :], b1), (w2s[:, :, :], w2), (b2s[:, :], b2.unsqueeze(0))):
                e.dma_start(a, b).then_inc(s_weights, 16)
            for j in range(TILES // XGROUP):
                a, z = j * XGROUP, (j + 1) * XGROUP
                if z * P <= N:
                    e.dma_start(X[:, a:z, :], x[a * P:z * P, :].rearrange("(t p) f -> p t f", p=P)).then_inc(s_x[j], 16)
                    continue
                e.dma_start(X[:, a:z - 1, :], x[a * P:(z - 1) * P, :].rearrange("(t p) f -> p t f", p=P)).then_inc(s_x[j], 16)
                e.wait_ge(s_xpad, 1)
                e.dma_start(X[0:LAST, z - 1, :], x[(z - 1) * P:N, :]).then_inc(s_x[j], 16)
            for a, b in ((wrs[:, :, :], wr), (brs[:, :], br.unsqueeze(0))):
                e.dma_start(a, b).then_inc(s_const, 16)
            e.wait_ge(s_b2, 6)
            e.dma_start(b2_rows[:, :], b2_part[:, :, :]).then_inc(s_b2r, 16)
            for q in range(STEPS):
                t = tiles_of(q)
                e.wait_ge(s_ml, 2 * q + (len(t) + 1) // 2)
                e.dma_start(table[t[0] * P:(t[-1] + 1) * P, :].rearrange("(t p) f -> p t f", p=P),
                            MHL[:, t[0]:t[-1] + 1, :]).then_inc(s_mst, 16)
            e.wait_ge(s_sorted, 1)
            e.dma_start(edge_list.rearrange("(p t) -> p t", p=P), key[SORTED_IN][:, :]).then_inc(s_list, 16)
            e.wait_ge(s_list, 16)
            e.wait_ge(s_starts, 1)

            def load_keys(r):
                first = bound_at[FIRST + r]
                at = e.value_load(starts[0:1, first:first + 1], min_val=0, max_val=EDGES)
                if r >= 4:
                    e.wait_ge(s_idx, r - 3)
                n = BUCKET_TILES[r]
                e.dma_start(kt[r % 4][:, 0:n], edge_list[bass.DynSlice(at, n * P)].rearrange("(p t) -> p t", p=P))\
                    .then_inc(s_kload[r % 4], 16)

            for r in range(3):
                load_keys(r)
            e.wait_ge(s_crowd, 2)

            def load_chunk(pair, chunk):
                e.dma_start(g_key[:, 0:1], edge_list[bass.DynSlice(chunk * P, P)].rearrange("(p t) -> p t", p=P))\
                    .then_inc(g_load, 16)
                taken(e, g_done)

            crowded_path(e, load_chunk)
            for r in range(3, ROUNDS):
                load_keys(r)
            e.wait_ge(s_agg, GROUPS * ROUNDS)
            e.wait_ge(s_mul, CHUNKS)
            e.dma_start(gam, gamma.unsqueeze(0).broadcast_to([P, D])).then_inc(s_const, 16)
            e.dma_start(bet, beta.unsqueeze(0).broadcast_to([P, D])).then_inc(s_const, 16)
            expert = []
            for i in range(TOP_K):
                e.wait_ge(s_chosen, i + 1)
                expert.append(e.value_load(chosen[0:1, i:i + 1], min_val=0, max_val=EXPERTS - 1))
                e.dma_start(w1_in[:, i * KD:(i + 1) * KD, :],
                            fw1[bass.DynSlice(expert[i], 1), :, :, :].rearrange("a p k f -> p (a k) f"))\
                    .then_inc(s_ew1[i], 16)
            for i, ex in enumerate(expert):
                e.dma_start(eb1[:, i, :], fb1[bass.DynSlice(ex, 1), :, :].rearrange("a p k -> p (a k)"))\
                    .then_inc(s_eb, 16)
                e.dma_start(eb2[:, i, :], fb2[bass.DynSlice(ex, 1), :].broadcast_to([P, D])).then_inc(s_eb, 16)
            for i, ex in enumerate(expert):
                e.dma_start(w2_in[:, i * KF:(i + 1) * KF, :],
                            fw2[bass.DynSlice(ex, 1), :, :, :].rearrange("a p k f -> p (a k) f")).then_inc(s_ew2, 16)
            for c in range(STEPS):
                t = tiles_of(c)
                if c < POOL_ENDS:
                    e.wait_ge(s_fin, c + 1)
                else:
                    e.wait_ge(s_fin_last, c - POOL_ENDS + 1)
                if t[-1] < TILES - 1:
                    e.dma_start(out[t[0] * P:(t[-1] + 1) * P, :].rearrange("(t p) f -> p t f", p=P),
                                res[c % 2][:, 0:len(t), :]).then_inc(s_out[c % 2], 16)
                else:
                    assert len(t) == 1
                    e.dma_start(out[t[0] * P:N, :], res[c % 2][0:LAST, 0, :]).then_inc(s_out[c % 2], 16)
            for i in range(2):
                e.wait_ge(s_out[i], 16 * len(range(i, STEPS, 2)))

        @block.gpsimd
        def _(e):
            e.memset(X[:, TILES - 1, :], 0.0).then_inc(s_xpad, 1)
            e.memset(ones[:, :], 1.0).then_inc(s_xpad, 1)
            e.wait_ge(s_masks, 48)
            e.tensor_copy(iota16[:, :], iota).then_inc(s_xpad, 1)
            e.wait_ge(s_weights, 16 * N_WEIGHTS)
            e.memset(ones16[:, :], 1.0).then_inc(s_b2, 1)
            e.tensor_copy(b2_part[:, 0, :], b2s[:, :]).then_inc(s_b2, 1)
            for i in range(1, 3):
                e.wait_ge(s_b2, 2 * i)
                e.tensor_tensor(b2_rest[:, :], (b2s, b2_rest)[i - 1][:, :], b2_part[:, i - 1, :], ALU.subtract)\
                    .then_inc(s_b2, 1)
                e.wait_ge(s_b2, 2 * i + 1)
                e.tensor_copy(b2_part[:, i, :], b2_rest[:, :]).then_inc(s_b2, 1)
            for q in range(STEPS):
                for i in range((len(tiles_of(q)) + 1) // 2):
                    t, n = tiles_of(q)[2 * i], min(2, len(tiles_of(q)) - 2 * i)
                    e.wait_ge(s_mc, 2 * q + i + 1)
                    m = m_out[(2 * q + i) % 2][:, 0:n, :]
                    e.tensor_copy(MHL[:, t:t + n, 0:D], m).then_inc(s_pool, 1)
                    e.wait_ge(s_pool, 2 * q + i + 1)
                    e.tensor_tensor(MHL[:, t:t + n, D:2 * D], m, MHL[:, t:t + n, 0:D], ALU.subtract).then_inc(s_ml, 1)
            e.wait_ge(s_mst, 16 * STEPS)

            def gather_chunk(pair, chunk):
                taken(e, g_idx)
                e.indirect_dma_start(g_row, None, table,
                                     bass.IndirectOffsetOnAxis(ap=g_ki[:, 0:1], axis=0)).then_inc(g_rows, 16)

            for g in range(GROUPS * ROUNDS):
                r, h = divmod(g, GROUPS)
                first, n = groups(r)[h]
                if h == 0:
                    e.wait_ge(s_idx, r + 1)
                if g >= RING:
                    e.wait_ge(s_agg, g - RING + 1)
                for j in range(n):
                    e.indirect_dma_start(
                        rows[g % RING][:, j, :], None, table,
                        bass.IndirectOffsetOnAxis(ap=ki[r % 3][:, first + j:first + j + 1], axis=0),
                    ).then_inc(s_row[g % RING], 16)
                if g == 0:
                    e.wait_ge(s_list, 16)
                    e.wait_ge(s_run, 1)
                    for i in range(CELL_GROUPS):
                        e.indirect_dma_start(
                            run_keys[:, i, :], None, edge_list.rearrange("(r t) -> r t", t=RUN),
                            bass.IndirectOffsetOnAxis(ap=run_no_i[:, i:i + 1], axis=0)).then_inc(s_runs, 16)
                if g == 1:
                    e.wait_ge(s_cstart, 1)
                    for i in range(CELL_GROUPS):
                        e.indirect_dma_start(
                            cell_keys[:, i, :], None, edge_list.rearrange("(r t) -> r t", t=1),
                            bass.IndirectOffsetOnAxis(ap=cell_start[:, i:i + 1], axis=0)).then_inc(s_ckeys, 16)
                if g == RING - 1:
                    e.wait_ge(s_crowd, 2)
                    crowded_path(e, gather_chunk)
            own = 2 * STEPS - 1
            e.wait_ge(s_bias, 1)
            e.wait_ge(s_const, 16 * N_CONST)
            for c in range(STEPS + 1):
                if c < STEPS:
                    for i, t in enumerate(tiles_of(c)):
                        e.wait_ge(s_xn1, t + 1)
                        e.tensor_tensor(X[:, t, :], X[:, t, :], bet[:, :], ALU.add).then_inc(s_pool, 1)
                        e.tensor_tensor(res[c % 2][:, i, :], res[c % 2][:, i, :], bias[:, :], ALU.add).then_inc(s_xr, 1)
                    own += len(tiles_of(c))
                if 1 <= c <= POOL_ENDS:
                    e.wait_ge(s_ln, c)
                    for i, t in enumerate(tiles_of(c - 1)):
                        e.tensor_tensor(res[(c - 1) % 2][:, i, :], res[(c - 1) % 2][:, i, :], gam[:, :],
                                        ALU.mult).then_inc(s_pool, 1)
                    own += len(tiles_of(c - 1))
                    e.wait_ge(s_pool, own)
                    for i, t in enumerate(tiles_of(c - 1)):
                        ins = e.tensor_tensor(res[(c - 1) % 2][:, i, :], res[(c - 1) % 2][:, i, :], X[:, t, :], ALU.add)
                    ins.then_inc(s_fin, 1)

        @block.scalar
        def _(e):
            e.wait_ge(s_edges, 32)
            def count(i):
                e.activation(sign_out[0:EDGE_ROWS, :], src_in[0:EDGE_ROWS, :], ACT.Sign, bias=BOUNDS[i] * P - 0.5,
                             scale=-1.0, accum_out=sign_sum[0:EDGE_ROWS, i:i + 1]).then_inc(s_sign, 1)
                e.wait_ge(s_sign, i + 1)

            for i in range(COUNT_FIRST):
                count(i)
            e.wait_ge(s_weights, 16 * N_WEIGHTS)
            for a, w in ((abs_w[0], w1s[:, :, :]), (abs_w[1], w2s[:, :, :]), (abs_b1, b1s[:, :]), (abs_b2[0:1], b2s[:, :])):
                e.activation(a, w, ACT.Abs).then_inc(s_abs, 1)

            def hidden_bounds():
                e.wait_ge(s_hb, 1)
                e.wait_ge(s_abs, 4)
                for m in range(KD):
                    e.activation(hidden_bound[:, m:m + 1], bank[7][:, m:m + 1], ACT.Identity,
                                 bias=abs_b1[:, m:m + 1], scale=LNORM_MAX).then_inc(s_hbc, 1)

            junk = sign_out.bitcast(F32)[:, 0:D]
            for j in range(TILES // XGROUP):
                a, z = j * XGROUP, (j + 1) * XGROUP
                e.wait_ge(s_x[j], 32 if j == TILES // XGROUP - 1 else 16)
                for t in range(a, z):
                    if t:
                        e.wait_ge(s_sum if t > a else s_square, t)
                    elif COUNT_FIRST:
                        e.wait_ge(s_sign, COUNT_FIRST)
                    e.activation(junk, X[:, t, :], ACT.Identity, accum_out=x_sum[:, t:t + 1]).then_inc(s_sum, 1)
                e.wait_ge(s_sum, z)
                e.activation(minus_m[:, a:z], x_sum[:, a:z], ACT.Copy, scale=-1.0 / D).then_inc(s_mean, 1)
                e.wait_ge(s_mean, j + 1)
                for t in range(a, z):
                    since(e, s_square, t)
                    e.activation(junk, X[:, t, :], ACT.Square, bias=minus_m[:, t:t + 1],
                                 accum_out=x_square[:, t:t + 1]).then_inc(s_square, 1)
                if j == 0:
                    hidden_bounds()

            def normalise(q):
                if q >= 2:
                    e.wait_ge(s_tp, 2 * (q - 1))
                for i, t in enumerate(tiles_of(q)):
                    e.wait_ge(s_stat, 1 if t < STAT_BATCHES[0][1] else 2)
                    e.activation(xn_in[q % 2][:, i, :], X[:, t, :], ACT.Identity, bias=nmr[:, t:t + 1],
                                 scale=rs[:, t:t + 1]).then_inc(s_xn, 1)

            def copy_m(q):
                for i in range((len(tiles_of(q)) + 1) // 2):
                    e.wait_ge(s_m, 2 * q + i + 1)
                    since(e, s_ml, max(2 * q + i - 1, 0))
                    n = min(2, len(tiles_of(q)) - 2 * i)
                    e.activation(m_out[(2 * q + i) % 2].rearrange("p a b -> p (a b)")[:, 0:n * D], bank[4 + i][:, 0:n * D],
                                 ACT.Copy).then_inc(s_mc, 1)

            normalise(0)
            e.wait_ge(s_scale, 3)
            for step in plan:
                if step[0] == "mlp":
                    q = step[1]
                    n = len(tiles_of(q)) * P
                    for k in range(KD):
                        e.wait_ge(s_tp, 2 * q + k + 1)
                        if q >= 2 and k == 0:
                            e.wait_ge(s_h, 2 * (q - 1))
                        e.activation(xn_t[q % 2][:, k, 0:n], bank[k][:, 0:n], ACT.Copy).then_inc(s_xt, 1)
                    if q + 1 < STEPS:
                        normalise(q + 1)
                    for m in range(KD):
                        e.wait_ge(s_h, 2 * q + m + 1)
                        if q >= 2 and m == 0:
                            e.wait_ge(s_m, 2 * (q - 1))
                        e.activation(hid_t[q % 2][:, m, 0:n], bank[2 + m][:, 0:n], ACT.Relu,
                                     bias=b1_scaled[:, m:m + 1], scale=scales[:, 0:1]).then_inc(s_relu, 1)
                    if q >= 1:
                        copy_m(q - 1)
                    if q == STEPS - 1:
                        copy_m(q)
                elif step[0] == "count":
                    for i in step[1]:
                        count(i)
                elif step[0] == "bounds":
                    e.wait_ge(s_bnd, 1)
                    e.activation(sign_total[:, :], bank[6][0:1, 0:len(BOUNDS)], ACT.Copy).then_inc(s_bndc, 1)
                else:
                    _, k, back = step
                    no = turn_no(k, back)
                    if not back:
                        r = 1 << (k - LOG_SLOTS - 1)
                        for h in range(2):
                            e.wait_ge(s_kt, 2 * no + h + 1)
                            v = bank[6 + h][:, :].rearrange("p (n c r) -> p n c r", c=2, r=r)
                            e.activation(key_high[:, h * 256:(h + 1) * 256].rearrange("p (n r) -> p n r", r=r),
                                         v[:, :, 1, :], ACT.Copy).then_inc(s_kc, 1)
                    else:
                        e.wait_ge(s_kt, 2 * no + 2)
                        e.activation(key_high[:, :], bank[7][:, :], ACT.Copy).then_inc(s_kc, 1)

            def clear(a, z):
                e.activation(xt_flat[:, a:z], ones[:, 0:1].broadcast_to([P, z - a]), ACT.Copy, scale=0.0)\
                    .then_inc(s_extra, 1)

            e.wait_ge(s_m, 2 * STEPS - 1)
            clear(search_end, XT_WORDS)
            e.wait_ge(s_list, 16)
            e.wait_ge(s_first, 1)
            clear(0, search_at)
            e.wait_ge(s_turned, 1)
            for i, a in enumerate((dst_in_cell, src_in_cell)):
                e.activation(a[:, :], bank[5 + i][:, :], ACT.Copy).then_inc(s_cell, 1)
            clear(search_at, search_end)

            def copy_blocks(chunks):
                for c in chunks:
                    e.wait_ge(s_blk, c + 1)
                    if c >= ARING:
                        e.wait_ge(s_mul, c - ARING + 1)
                    n = len(cells_of(c)) * PAIR
                    e.activation(blocks[c % ARING].rearrange("p a b -> p (a b)")[:, 0:n], bank[3 + c % 2][:, 0:n],
                                 ACT.Copy).then_inc(s_ev, 1)

            for k in range(SLOTS_ALL):
                copy_blocks(early(k + 1))
                copy_blocks(late(k))
                for s, t in due(k, 5):
                    n = P if t < TILES - 1 else LAST
                    e.wait_ge(s_tx, s + 1)
                    for h in range(KD):
                        e.activation(XT[:, t, h, 0:n], bank[5][:, D + h * P:D + h * P + n], ACT.Identity,
                                     accum_out=colsum[:, h, t:t + 1]).then_inc(s_txc, 1)
                for s, t in due(k, 2):
                    e.wait_ge(s_hc, s + 1)
                    since(e, s_g, s)
                    for m in range(KD):
                        e.activation(HC[s % 2][:, m, :], bank[6][:, m * P:(m + 1) * P], ACT.Relu,
                                     bias=b1s[:, m:m + 1]).then_inc(s_rc, 1)
                for s, t in due(k, 1):
                    e.wait_ge(s_tu, s + 1)
                    since(e, s_hc, s)
                    e.activation(UT[s % 2][:, :, :].rearrange("p a b -> p (a b)"), bank[5][:, 0:D], ACT.Copy)\
                        .then_inc(s_ut, 1)
            e.wait_ge(s_dif, 1)
            e.activation(R[:, 2, :], R[:, 1, :], ACT.Exp).then_inc(s_exp, 1)
            e.activation(R[:, 3, :], R[:, 1, :], ACT.Gelu).then_inc(s_warm, 1)

            def xn_high(c):
                if c == 2:
                    e.wait_ge(s_wl[0], 1)
                if c >= 2:
                    e.wait_ge(s_eh, (c - 1) * FB)
                    since(e, s_xl, c - 2)
                t = tiles_of(c)
                e.activation(xn_buf(c)[0].rearrange("p a b -> p (a b)")[:, 0:len(t) * D],
                             XT[:, t[0]:t[-1] + 1, :, :].rearrange("p a b c -> p (a b c)"), ACT.Copy,
                             scale=XN_SCALE).then_inc(s_xh, 1)

            xn_high(1)

            for i, (a, scratch, s, n) in enumerate((
                    (w1_in, act[0][0], s_ew1[-1], 16), (eb1[:, :, :], act[0][1], s_eb, 32 * TOP_K),
                    (w2_in, act[1][0], s_ew2, 16 * TOP_K))):
                if i == 0:
                    e.wait_ge(s_ew1[0], 16)
                e.wait_ge(s, n)
                z = a.shape[1] * a.shape[2]
                e.activation(scratch.rearrange("p a b -> p (a b)")[:, 0:z], a.rearrange("p a b -> p (a b)"), ACT.Abs,
                             accum_out=abs_sum[:, i:i + 1]).then_inc(s_asum, 1)

            def xn_again(c):
                if c >= 2:
                    e.wait_ge(s_out[c % 2], 16 * (c // 2))
                if c == 0:
                    e.wait_ge(s_nmr2, 1)
                for i, t in enumerate(tiles_of(c)):
                    e.activation(res[c % 2][:, i, :], X[:, t, :], ACT.Identity, bias=nmr2[:, t:t + 1],
                                 scale=rs2[:, t:t + 1]).then_inc(s_xn1, 1)

            def weight_high(i):
                e.activation(((ew1, ew2)[i])[0], (w1_in, w2_in)[i], ACT.Copy, scale=xsc[:, 2, 2 * i:2 * i + 1])\
                    .then_inc(s_wh[i], 1)

            def gelu_high(n):
                c, f = divmod(n, FB)
                tok = tokens_of(c)
                e.wait_ge(s_gelu, n + 1)
                if c >= 2 and f == 0:
                    e.wait_ge(s_y, tiles_of(c - 2)[-1] + 1)
                e.activation(act[c % 2][0][:, f, 0:tok], gelu_buf(n)[:, 0:tok], ACT.Copy, scale=xsc[:, 2, 1:2])\
                    .then_inc(s_ah, 1)

            e.wait_ge(s_xsc, 1)
            weight_high(0)
            for n in range(STEPS * FB):
                c, f = divmod(n, FB)
                tok = tokens_of(c)
                e.wait_ge(s_eh, n + 1)
                if n == FB:
                    e.wait_ge(s_wl[1], 1)
                since(e, s_al, gelu_free(n))
                e.activation(gelu_buf(n)[:, 0:tok], bank[n % 4][:, 0:tok], ACT.Gelu, bias=eb1[:, f // KF, f % KF:f % KF + 1],
                             scale=inv_h[:, 0:1] if c else 1.0).then_inc(s_gelu, 1)
                if n == 4:
                    e.wait_ge(s_w2s, TOP_K)
                    weight_high(1)
                if f:
                    gelu_high(n - 1)
                if f == FB - 1:
                    gelu_high(n)
                    if 1 <= c < STEPS - 1:
                        xn_high(c + 1)
                    xn_again(c)
        @block.tensor
        def _(e):
            e.wait_ge(s_masks, 48)
            e.wait_ge(s_xpad, 3)
            e.wait_ge(s_abs, 4)
            for m in range(KD):
                for k in range(KD):
                    ins = e.matmul(bank[7][:, m:m + 1], abs_w[0][:, k, m * P:(m + 1) * P], ones[:, 0:1],
                                   start=(k == 0), stop=(k == KD - 1))
            ins.then_inc(s_hb, 1)
            e.wait_ge(s_hbc, KD)
            for k in range(KD):
                e.matmul(bank[7][0:1, 0:D], hidden_bound[:, k:k + 1], abs_w[1][:, k, :], start=(k == 0), stop=False)
            e.matmul(bank[7][0:1, 0:D], ones[0:1, 0:1], abs_b2[0:1, :], start=False, stop=True).then_inc(s_hb, 1)
            e.wait_ge(s_scale, 1)
            e.matmul(bank[7][:, 0:2], ones[0:1, :], bound[0:1, 2:4], start=True, stop=True).then_inc(s_scp, 1)
            n_bounds = len(BOUNDS)
            e.wait_ge(s_scale, 3)

            def transposes(q):
                e.wait_ge(s_xn, tiles_of(q)[-1] + 1)
                if q >= 1:
                    e.wait_ge(s_xt, 2 * q)
                for k in range(KD):
                    for i in range(len(tiles_of(q))):
                        ins = e.transpose(bank[k][:, i * P:(i + 1) * P], xn_in[q % 2][:, i, k * P:(k + 1) * P], ident)
                    ins.then_inc(s_tp, 1)

            def hidden(q):
                n = len(tiles_of(q)) * P
                e.wait_ge(s_xt, 2 * q + 2)
                if q >= 1:
                    e.wait_ge(s_relu, 2 * q)
                for m in range(KD):
                    for k in range(KD):
                        ins = e.matmul(bank[2 + m][:, 0:n], w1s[:, k, m * P:(m + 1) * P], xn_t[q % 2][:, k, 0:n],
                                       start=(k == 0), stop=(k == KD - 1))
                    ins.then_inc(s_h, 1)

            def second(q):
                e.wait_ge(s_relu, 2 * q + 2)
                if q >= 1:
                    e.wait_ge(s_mc, 2 * q)
                n = len(tiles_of(q))
                for i in range(n):
                    o = bank[4 + i // 2][:, (i % 2) * D:(i % 2 + 1) * D]
                    for k in range(KD):
                        e.matmul(o, hid_t[q % 2][:, k, i * P:(i + 1) * P], w2s[:, k, :], start=(k == 0), stop=False)
                    ins = e.matmul(o, scale_rows[:, :], b2_rows[:, :], start=False, stop=True)
                    if i % 2 or i == n - 1:
                        ins.then_inc(s_m, 1)

            e.wait_ge(s_b2r, 16)
            for step in plan:
                if step[0] == "mlp":
                    q = step[1]
                    transposes(q)
                    hidden(q)
                    if q >= 1:
                        second(q - 1)
                    if q == STEPS - 1:
                        second(q)
                elif step[0] == "count":
                    pass
                elif step[0] == "bounds":
                    e.wait_ge(s_sign, n_bounds)
                    e.wait_ge(s_kv, 2 * turn_no(COUNTED, 0) + 2)
                    e.matmul(bank[6][0:1, 0:n_bounds], ones[0:EDGE_ROWS, 0:1], sign_sum[0:EDGE_ROWS, :],
                             start=True, stop=True).then_inc(s_bnd, 1)
                    e.wait_ge(s_bndc, 1)
                else:
                    _, k, back = step
                    no = turn_no(k, back)
                    for h in range(2):
                        e.wait_ge(s_kv, 2 * no + h + 1)
                        source = turn_in(k, back).bitcast(F32)
                        for g in range(4):
                            ins = e.transpose(bank[6 + h][:, g * P:(g + 1) * P],
                                              source[:, (4 * h + g) * P:(4 * h + g + 1) * P], ident)
                        ins.then_inc(s_kt, 1)

            e.wait_ge(s_sorted, 1)
            last_keys = key[SORTED_IN][:, :].bitcast(F32)
            for i in range(SLOTS // RUN):
                ins = e.transpose(bank[5][:, i * P:(i + 1) * P], last_keys[:, i * RUN:i * RUN + 1].broadcast_to([P, P]),
                                  ident)
            ins.then_inc(s_first, 1)

            def sums(r, h):
                g = GROUPS * r + h
                first, n = groups(r)[h]
                e.wait_ge(s_oh, g + 1)
                e.wait_ge(s_row[g % RING], 16 * rows_until[g])
                if h == 0 and r >= 1:
                    e.wait_ge(s_u, place[FIRST + r - 1] + 1)
                for j in range(n):
                    ins = e.matmul(bank[0][:, :], onehot[g % 2][:, j, :], rows[g % RING][:, j, :],
                                   start=(first + j == 0), stop=(first + j == BUCKET_TILES[r] - 1))
                ins.then_inc(s_agg, 1)

            def make_blocks(c):
                e.wait_ge(s_hot, c + 1)
                if c >= 2:
                    e.wait_ge(s_ev, c - 1)
                for i in range(len(cells_of(c))):
                    ins = e.matmul(bank[3 + c % 2][:, i * PAIR:(i + 1) * PAIR], dst_hot[c % SRING][:, i, :],
                                   src_hot[c % SRING][:, i, :], start=True, stop=True)
                ins.then_inc(s_blk, 1)

            def multiply(c):
                for i, cell in enumerate(cells_of(c)):
                    pair, t = divmod(cell, TILES)
                    if t == 0 and pair:
                        e.wait_ge(s_u, place[2 * pair - 1] + 1)
                    for h in range(2):
                        ins = e.matmul(bank[1 + h][:, :], blocks[c % ARING][:, i, h * P:(h + 1) * P], MHL[:, t, :],
                                       start=(t == 0), stop=(t == TILES - 1))
                ins.then_inc(s_mul, 1)

            def turn_u(s):
                e.wait_ge(s_u, s + 1)
                since(e, s_ut, turned[0])
                since(e, s_txc, 2 * turned[1])
                for k in range(KD):
                    ins = e.transpose(bank[5][:, k * P:(k + 1) * P], U[s % 2][:, k * P:(k + 1) * P], ident)
                ins.then_inc(s_tu, 1)
                turned[0] += 1

            def hidden2(s):
                e.wait_ge(s_ut, s + 1)
                since(e, s_rc, 2 * s)
                for m in range(KD):
                    for k in range(KD):
                        ins = e.matmul(bank[6][:, m * P:(m + 1) * P], w1s[:, k, m * P:(m + 1) * P], UT[s % 2][:, k, :],
                                       start=(k == 0), stop=(k == KD - 1))
                ins.then_inc(s_hc, 1)

            def second2(s):
                e.wait_ge(s_rc, 2 * s + 2)
                since(e, s_x1, s)
                for k in range(KD):
                    e.matmul(bank[7][:, 0:D], HC[s % 2][:, k, :], w2s[:, k, :], start=(k == 0), stop=False)
                e.matmul(bank[7][:, 0:D], ones16[:, :], b2_rows[:, :], start=False, stop=True).then_inc(s_g, 1)

            def turn_x(s):
                e.wait_ge(s_xb, s + 1)
                since(e, s_ut, turned[0])
                since(e, s_txc, 2 * turned[1])
                for k in range(KD):
                    ins = e.transpose(bank[5][:, D + k * P:D + (k + 1) * P], XB[s % 2][:, k * P:(k + 1) * P], ident)
                ins.then_inc(s_tx, 1)
                turned[1] += 1

            def turn_cells():
                e.wait_ge(s_part, 1)
                for i in range(2):
                    for g in range(CELL_GROUPS):
                        e.transpose(bank[5 + i][:, g * P:(g + 1) * P], cell_partf[i][:, g, :], ident)
                e.matmul(bank[7][0:1, 0:1], ones[:, 0:1], full[:, CELL_GROUPS:CELL_GROUPS + 1], start=True, stop=True)\
                    .then_inc(s_turned, 1)

            gathered = e.alloc_register("gathered")
            e.reg_mov(gathered, 0)

            def sum_chunk(pair, chunk):
                e.reg_add(gathered, gathered, 16)
                e.wait_ge(g_rows, e.snap(gathered))
                for h in range(2):
                    ins = e.matmul(bank[6 + h][:, :], g_onehot[:, h, :], g_row, start=True, stop=True)
                ins.then_inc(g_sum, 1)

            turned = [0, 0]
            for k in range(SLOTS_ALL):
                if k == PART:
                    turn_cells()
                for c in early(k + 1):
                    make_blocks(c)
                if slot(k)[0] == "gather":
                    sums(*slot(k)[1:])
                else:
                    chunks = slot(k)[1]
                    for c in chunks:
                        e.wait_ge(s_ev, c + 1)
                        if c + 2 in chunks:
                            make_blocks(c + 2)
                        multiply(c)
                if k == PART:
                    e.wait_ge(s_crowd, 2)
                    e.wait_ge(s_cell, 2)
                    e.matmul(bank[7][:, 0:1], ones[0:1, :], fits[0:1, 0:1], start=True, stop=True).then_inc(s_keep, 1)
                    crowded_path(e, sum_chunk)
                for s, _ in due(k, 5):
                    turn_x(s)
                for s, _ in due(k, 3):
                    second2(s)
                for s, _ in due(k, 2):
                    hidden2(s)
                for s, _ in due(k, 1):
                    turn_u(s)

            e.wait_ge(s_msum, 1)
            for k in range(KD):
                ins = e.matmul(bank[6][0:1, 0:EXPERTS], msum[:, k:k + 1], wrs[:, k, :], start=(k == 0), stop=(k == KD - 1))
            ins.then_inc(s_logit, 1)
            e.wait_ge(s_route, 1)
            e.matmul(bank[6][:, 0:TOP_K], ones[0:1, :], wts[0:1, :], start=True, stop=True).then_inc(s_wbp, 1)

            def expert_hidden(c):
                tiles = tiles_of(c)
                tok = tokens_of(c)
                if c:
                    e.wait_ge(s_xl, c)
                    e.wait_ge(s_wl[0], 1)
                    passes = [(ew1[a], xn_buf(c)[b].rearrange("p (t k) n -> p t k n", k=KD)) for a, b in
                              ((0, 0), (0, 1), (1, 0))]
                    base = 0
                else:
                    passes = [(w1_in, XT)]
                    base = tiles[0]
                for f in range(FB):
                    i, m = divmod(f, KF)
                    n = c * FB + f
                    if c == 0 and m == 0:
                        e.wait_ge(s_ew1[i], 16)
                    if n == 3:
                        e.wait_ge(s_asum, 3)
                        e.matmul(bank[7][:, 0:3], ones[:, :], abs_sum[:, :], start=True, stop=True).then_inc(s_asp, 1)
                    if n >= 4:
                        e.wait_ge(s_gelu, n - 3)
                    o = bank[n % 4][:, 0:tok]
                    if tok > P:
                        o = o.rearrange("p (a b) -> p a b", b=P)
                    todo = [(k, w, v) for k in range(KD) for w, v in passes]
                    for j, (k, w, v) in enumerate(todo):
                        moving = v[:, base:base + len(tiles), k, :] if tok > P else v[:, base, k, 0:tok]
                        ins = e.matmul(o, w[:, i * KD + k, m * P:(m + 1) * P], moving,
                                       start=(j == 0), stop=(j == len(todo) - 1))
                    ins.then_inc(s_eh, 1)

            def expert_out(c):
                for i, t in enumerate(tiles_of(c)):
                    n = P if t < TILES - 1 else LAST
                    if i == 0:
                        e.wait_ge(s_al, (c + 1) * FB)
                    if t >= Y_BANKS:
                        e.wait_ge(s_yr, t - Y_BANKS + 1)
                    todo = [(f, a, b) for f in range(FB) for a, b in ((0, 0), (0, 1), (1, 0))]
                    for j, (f, a, b) in enumerate(todo):
                        ins = e.matmul(bank[4 + t % Y_BANKS][0:n, 0:D], act[c % 2][a][:, f, i * P:i * P + n], ew2[b][:, f, :],
                                       start=(j == 0), stop=(j == len(todo) - 1))
                    ins.then_inc(s_y, 1)

            for c in range(STEPS + 1):
                if c < STEPS:
                    expert_hidden(c)
                if c == 1:
                    e.wait_ge(s_wl[1], 1)
                if c >= 1:
                    expert_out(c - 1)

        @block.vector
        def _(e):
            own = [0]

            def step(ins):
                own[0] += 1
                ins.then_inc(s_own, 1)

            def settle():
                e.wait_ge(s_own, own[0])

            def chain(ins):
                step(ins)
                settle()

            def rsqrt(y, v, t, w):
                chain(e.tensor_scalar(w, v, EPS, None, ALU.add))
                chain(e.tensor_scalar(y.bitcast(I32), w.bitcast(I32), -0.5, 1597463007.0, ALU.mult, ALU.add))
                for _ in range(3):
                    chain(e.tensor_tensor(t, y, y, ALU.mult))
                    chain(e.tensor_tensor(t, t, w, ALU.mult))
                    chain(e.tensor_scalar(t, t, -0.5, 1.5, ALU.mult, ALU.add))
                    chain(e.tensor_tensor(y, y, t, ALU.mult))

            def rsqrt_column(y, v, t, w):
                chain(e.tensor_scalar(w, v, EPS, -0.5, ALU.add, ALU.mult))
                chain(e.tensor_scalar(y.bitcast(I32), w.bitcast(I32), -0.5, float(1597463007 - (1 << 30) - (1 << 22)),
                                      ALU.mult, ALU.add))
                for _ in range(3):
                    chain(e.scalar_tensor_tensor(out=t, in0=y, scalar=w, in1=y, op0=ALU.mult, op1=ALU.mult))
                    chain(e.scalar_tensor_tensor(out=y, in0=t, scalar=1.5, in1=y, op0=ALU.add, op1=ALU.mult))

            def minus_mean(o, mean, y):
                return e.scalar_tensor_tensor(out=o, in0=mean, scalar=-1.0, in1=y, op0=ALU.mult, op1=ALU.mult)

            def kf(i):
                return key[i][:, :].bitcast(F32)

            chain(e.memset(key[0][:, :], KEY_NONE))
            e.wait_ge(s_edges, 32)
            s_, d_ = src_in[0:EDGE_ROWS, :], dst_in[0:EDGE_ROWS, :]
            k_, h_ = key[0][0:EDGE_ROWS, 0:EDGE_COLS], key[1][0:EDGE_ROWS, 0:EDGE_COLS]
            a_, b_ = key_part[0][0:EDGE_ROWS, :], key_part[1][0:EDGE_ROWS, :]
            top = NODE_MASK & ~(PAIR - 1)
            step(e.tensor_scalar(a_, s_, float(DENSE_NODES), float(PAIR - 1), ALU.is_lt, ALU.mult))
            step(e.tensor_scalar(b_, s_, float(DENSE_NODES), float(-NODE_MASK), ALU.is_lt, ALU.mult))
            step(e.tensor_scalar(h_, s_, PAIR - 1, None, ALU.bitwise_and))
            settle()
            step(e.scalar_tensor_tensor(out=a_, in0=a_, scalar=1.0, in1=d_, op0=ALU.add, op1=ALU.mult))
            step(e.scalar_tensor_tensor(out=b_, in0=b_, scalar=float(NODE_MASK + 1), in1=h_, op0=ALU.add, op1=ALU.mult))
            settle()
            step(e.tensor_scalar(h_, s_, top, 1 << NODE_BITS, ALU.bitwise_and, ALU.bitwise_or))
            step(e.tensor_tensor(k_, a_, b_, ALU.add))
            settle()
            chain(e.tensor_scalar(h_, h_, NODE_BITS, None, ALU.logical_shift_left))
            chain(e.tensor_tensor(k_, k_, h_, ALU.bitwise_or))
            v = key[0][:, :].rearrange("p (n c r) -> p n c r", c=2, r=2)
            chain(e.tensor_scalar(v[:, :, 1, :], v[:, :, 1, :], KEY_BITS, None, ALU.bitwise_xor))
            e.wait_ge(s_masks, 48)
            cur = [0]

            def stage(j, last=None):
                s, o = kf(cur[0]), kf(1 - cur[0])
                sv = s.rearrange("p (n c r) -> p n c r", c=2, r=1 << j)
                ov = o.rearrange("p (n c r) -> p n c r", c=2, r=1 << j)
                step(e.tensor_tensor(ov[:, :, 0, :], sv[:, :, 0, :], sv[:, :, 1, :], ALU.min))
                ins = e.tensor_tensor(ov[:, :, 1, :], sv[:, :, 0, :], sv[:, :, 1, :], ALU.max)
                if last is None:
                    step(ins)
                else:
                    ins.then_inc(last, 1)

            def flip(k):
                c = key[cur[0]]
                if k + 1 < LOG_SLOTS:
                    v = c[:, :].rearrange("p (n c r) -> p n c r", c=4, r=1 << k)
                    chain(e.tensor_scalar(v[:, :, 1:3, :], v[:, :, 1:3, :], KEY_BITS, None, ALU.bitwise_xor))
                elif k + 1 == LOG_SLOTS:
                    h = SLOTS // 2
                    step(e.tensor_scalar(c[:, 0:h], c[:, 0:h], masks[:, 0:1], None, ALU.bitwise_xor))
                    step(e.tensor_scalar(c[:, h:], c[:, h:], masks[:, 1:2], None, ALU.bitwise_xor))
                    settle()
                else:
                    m = 2 + k - LOG_SLOTS
                    for h in range(2):
                        a, z = h * SLOTS // 2, (h + 1) * SLOTS // 2
                        e.tensor_scalar(c[:, a:z], c[:, a:z], masks[:, m:m + 1], None, ALU.bitwise_xor).then_inc(s_kv, 1)

            def free_merge(k):
                for j in reversed(range(k)):
                    stage(j)
                    settle()
                    cur[0] = 1 - cur[0]
                flip(k)

            for k in range(1, 6):
                free_merge(k)
                if k == 3:
                    e.wait_ge(s_hb, 2)
                    b, bi = bound, bound[:, :].bitcast(I32)
                    one_bit = 1 << 23
                    chain(e.tensor_reduce(b[:, 0:1], bank[7][0:1, 0:D], AX.X, ALU.max))
                    chain(e.tensor_scalar(b[:, 0:1], b[:, 0:1], 1e-18, 1e18, ALU.max, ALU.min))
                    chain(e.tensor_scalar(bi[:, 1:2], bi[:, 0:1], 0xff * one_bit, None, ALU.bitwise_and))
                    chain(e.tensor_scalar(bi[:, 2:3], bi[:, 1:2], -1.0, float((2 * 127 + HALF_TOP) * one_bit),
                                          ALU.mult, ALU.add))
                    chain(e.tensor_scalar(bi[:, 3:4], bi[:, 1:2], float(-HALF_TOP * one_bit), None, ALU.add))
                    e.tensor_copy(b[:, 0:1], b[:, 1:2]).then_inc(s_scale, 1)
                    e.wait_ge(s_scp, 1)
                    chain(e.tensor_copy(scales[:, :], bank[7][:, 0:2]))
                    e.tensor_scalar(scale_rows[:, :], ones[0:3, :], scales[0:3, 0:1], None, ALU.mult).then_inc(s_scale, 1)
                    e.tensor_scalar(b1_scaled[:, :], b1s[:, :], scales[:, 0:1], None, ALU.mult).then_inc(s_scale, 1)

            def statistics(i):
                a, z = STAT_BATCHES[i]
                e.wait_ge(s_square, z)
                t, w = (q[:, 0:z - a] for q in stat_tmp)
                chain(e.tensor_scalar(w, x_square[:, a:z], 1.0 / D, None, ALU.mult))
                rsqrt(rs[:, a:z], w, t, w)
                e.tensor_tensor(nmr[:, a:z], minus_m[:, a:z], rs[:, a:z], ALU.mult).then_inc(s_stat, 1)

            def bucket_starts():
                e.wait_ge(s_bndc, 1)
                n = N_STARTS - 1
                chain(e.memset(startf[:, 0:1], 0.0))
                chain(e.memset(startf[:, n:n + 1], float(EDGES)))
                chain(e.tensor_scalar(startf[:, 1:n], sign_total[:, :], float(EDGES), 0.5, ALU.add, ALU.mult))
                chain(e.tensor_copy(starts[:, :], startf[:, :]))
                at = bound_at[FIRST]
                chain(e.tensor_tensor(over[:, :], startf[:, at + 1:], startf[:, at:n], ALU.subtract))
                for a, z in ((0, ROUNDS - 1), (ROUNDS - 1, ROUNDS)):
                    chain(e.tensor_scalar(over[:, a:z], over[:, a:z], float(-BUCKET_TILES[a] * P), None, ALU.add))
                e.tensor_reduce(fits[:, 1:2], over[:, :], AX.X, ALU.max).then_inc(s_starts, 1)

            for k in range(6, LOG_SLOTS + 1):
                free_merge(k)
                if k in STAT_MERGES:
                    statistics(STAT_MERGES.index(k))

            halfn = SLOTS // 2
            for k in range(LOG_SLOTS + 1, LOG_ALL + 1):
                assert turn_in(k, 0) is key[cur[0]]
                no = turn_no(k, 0)
                top = k - LOG_SLOTS - 1
                r = 1 << top
                o = kf(1 - cur[0])
                for h in range(2):
                    e.wait_ge(s_kc, 3 * (k - LOG_SLOTS - 1) + h + 1)
                    lo_ = bank[6 + h][:, :].rearrange("p (n c r) -> p n c r", c=2, r=r)[:, :, 0, :]
                    hi_ = key_high[:, h * 256:(h + 1) * 256].rearrange("p (n r) -> p n r", r=r)
                    ov = o[:, h * halfn:(h + 1) * halfn].rearrange("p (n c r) -> p n c r", c=2, r=r)
                    step(e.tensor_tensor(ov[:, :, 0, :], lo_, hi_, ALU.min))
                    last = e.tensor_tensor(ov[:, :, 1, :], lo_, hi_, ALU.max)
                    if top == 0:
                        last.then_inc(s_kv, 1)
                    else:
                        step(last)
                cur[0] = 1 - cur[0]
                if top:
                    e.wait_ge(s_kt, 2 * no + 2)
                    settle()
                for j in reversed(range(top)):
                    s, o = kf(cur[0]), kf(1 - cur[0])
                    for h in range(2):
                        a, z = h * halfn, (h + 1) * halfn
                        sv = s[:, a:z].rearrange("p (n c r) -> p n c r", c=2, r=1 << j)
                        ov = o[:, a:z].rearrange("p (n c r) -> p n c r", c=2, r=1 << j)
                        step(e.tensor_tensor(ov[:, :, 0, :], sv[:, :, 0, :], sv[:, :, 1, :], ALU.min))
                        last = e.tensor_tensor(ov[:, :, 1, :], sv[:, :, 0, :], sv[:, :, 1, :], ALU.max)
                        if j == 0:
                            last.then_inc(s_kv, 1)
                        else:
                            step(last)
                    if j:
                        settle()
                    cur[0] = 1 - cur[0]
                assert turn_in(k, 1) is key[cur[0]]
                e.wait_ge(s_kc, 3 * (k - LOG_SLOTS - 1) + 3)
                settle()
                o = kf(1 - cur[0])
                step(e.tensor_tensor(o[:, 0:halfn], bank[6][:, :], key_high[:, :], ALU.min))
                step(e.tensor_tensor(o[:, halfn:], bank[6][:, :], key_high[:, :], ALU.max))
                settle()
                cur[0] = 1 - cur[0]
                for j in reversed(range(LOG_SLOTS - 1)):
                    stage(j, last=s_sorted if (k, j) == (LOG_ALL, 0) else None)
                    settle()
                    cur[0] = 1 - cur[0]
                if k < LOG_ALL:
                    flip(k)
                if k == COUNTED - 1:
                    bucket_starts()
            assert cur[0] == SORTED_IN

            def unpack(r):
                n = BUCKET_TILES[r]
                e.wait_ge(s_kload[r % 4], 16 * (r // 4 + 1))
                if r >= 3:
                    e.wait_ge(s_agg, GROUPS * (r - 2))
                k = kt[r % 4]
                chain(e.tensor_scalar(klo[:, 0:n], k[:, 0:n], NODE_BITS, NODE_MASK, ALU.logical_shift_right,
                                      ALU.bitwise_and))
                step(e.tensor_scalar(lo[r % 3][:, 0:n], klo[:, 0:n], float(-(FIRST + r) * P), None, ALU.add))
                e.tensor_scalar(ki[r % 3][:, 0:n], k[:, 0:n], NODE_MASK, None, ALU.bitwise_and).then_inc(s_idx, 1)
                settle()

            def one_hots(r, h):
                g = GROUPS * r + h
                first, n = groups(r)[h]
                if g >= 2:
                    e.wait_ge(s_agg, g - 1)
                for j in range(n):
                    ins = e.tensor_scalar(onehot[g % 2][:, j, :], iota16[:, 0:P], lo[r % 3][:, first + j:first + j + 1],
                                          None, ALU.is_equal)
                ins.then_inc(s_oh, 1)

            def cell_one_hots(c):
                if c >= SRING:
                    e.wait_ge(s_blk, c - SRING + 1)
                for i, cell in enumerate(cells_of(c)):
                    e.tensor_scalar(dst_hot[c % SRING][:, i, :], iota16[:, 0:P], dst_in_cell[:, cell:cell + 1],
                                    None, ALU.is_equal)
                    ins = e.tensor_scalar(src_hot[c % SRING][:, i, :], iota16[:, :], src_in_cell[:, cell:cell + 1],
                                          None, ALU.is_equal)
                ins.then_inc(s_hot, 1)

            def prepare(k):
                if slot(k)[0] == "gather":
                    one_hots(*slot(k)[1:])
                for c in slot(k)[1] if slot(k)[0] == "cells" else ():
                    if c == 0:
                        e.wait_ge(s_cell, 2)
                    cell_one_hots(c)

            def sum_in(s, t):
                since(e, s_tu, max(s - 1, 0))
                u = U[s % 2][:, :]
                chain(e.tensor_scalar(u, X[:, t, :], rs[:, t:t + 1], nmr[:, t:t + 1], ALU.mult, ALU.add))
                chain(e.tensor_tensor(u, u, XT[:, t, :, :].rearrange("p a b -> p (a b)"), ALU.add))
                if t < FIRST:
                    e.wait_ge(s_mul, (t // 2 + 1) * len(PAIR_CHUNKS))
                    sums = bank[1 + t % 2]
                else:
                    e.wait_ge(s_agg, GROUPS * (t - FIRST + 1))
                    sums = bank[0]
                for i in range(2):
                    ins = e.scalar_tensor_tensor(out=u, in0=sums[:, i * D:(i + 1) * D], scalar=keep[:, 0:1], in1=u,
                                                 op0=ALU.mult, op1=ALU.add)
                    if i == 0:
                        chain(ins)
                ins.then_inc(s_u, 1)

            def residual(s, t):
                e.wait_ge(s_g, s + 1)
                e.tensor_tensor(X[:, t, :], X[:, t, :], bank[7][:, 0:D], ALU.add).then_inc(s_x1, 1)
                e.wait_ge(s_x1, s + 1)
                chain(e.bn_stats(stat2[:, :], X[:, t, :]))
                chain(e.bn_aggr(mv2[:, t, :], stat2[:, :]))
                rsqrt_column(rs2[:, t:t + 1], mv2[:, t, 1:2], rq[0][:, 0:1], rq[1][:, 0:1])
                since(e, s_tx, max(s - 1, 0))
                e.tensor_scalar(XB[s % 2][:, :], X[:, t, :], mv2[:, t, 0:1], rs2[:, t:t + 1], ALU.subtract, ALU.mult)\
                    .then_inc(s_xb, 1)

            def find_runs():
                e.wait_ge(s_m, 2 * STEPS - 1)
                e.wait_ge(s_first, 1)
                for g in range(CELL_GROUPS):
                    step(e.tensor_scalar(below[:, g, :], bank[5][:, :], cell_base.bitcast(F32)[:, g:g + 1], None, ALU.is_lt))
                settle()
                chain(e.tensor_reduce(cell_n[:, :], below[:, :, :], AX.X, ALU.add))
                chain(e.tensor_scalar(run_no[:, :], cell_n[:, :], -1.0, 0.0, ALU.add, ALU.max))
                e.tensor_copy(run_no_i[:, :], run_no[:, :]).then_inc(s_run, 1)

            def find_cells():
                e.wait_ge(s_runs, 16 * CELL_GROUPS)
                for g in range(CELL_GROUPS):
                    step(e.tensor_scalar(below[:, g, 0:RUN], run_keys.bitcast(F32)[:, g, :],
                                         cell_base.bitcast(F32)[:, g:g + 1], None, ALU.is_lt))
                settle()
                chain(e.tensor_reduce(cell_n[:, :], below[:, :, 0:RUN], AX.X, ALU.add))
                e.scalar_tensor_tensor(out=cell_start[:, :], in0=run_no[:, :], scalar=float(RUN), in1=cell_n[:, :],
                                       op0=ALU.mult, op1=ALU.add).then_inc(s_cstart, 1)

            def split_cells():
                e.wait_ge(s_ckeys, 16 * CELL_GROUPS)
                for g in range(CELL_GROUPS):
                    step(e.tensor_scalar(cell_keys[:, g, :], cell_keys[:, g, :], cell_base[:, g:g + 1], None,
                                         ALU.bitwise_xor))
                settle()
                step(e.tensor_scalar(cell_part[0][:, :, :], cell_keys[:, :, 0:P], CELL_BITS - LOG_P, None,
                                     ALU.logical_shift_right))
                step(e.tensor_scalar(cell_part[1][:, :, :], cell_keys[:, :, 0:P], PAIR - 1, None, ALU.bitwise_and))
                step(e.tensor_scalar(full[:, 0:CELL_GROUPS], cell_keys[:, :, P], float(1 << CELL_BITS), None, ALU.is_lt))
                settle()
                for i in range(2):
                    step(e.tensor_copy(cell_partf[i][:, :, :], cell_part[i][:, :, :]))
                settle()
                e.tensor_reduce(full[:, CELL_GROUPS:CELL_GROUPS + 1], full[:, 0:CELL_GROUPS], AX.X, ALU.add)\
                    .then_inc(s_part, 1)

            def set_flags():
                e.wait_ge(s_turned, 1)
                chain(e.tensor_tensor(fits[:, 1:2], fits[:, 1:2], bank[7][0:1, 0:1], ALU.max))
                e.tensor_scalar(fits[:, 0:1], fits[:, 1:2], 0.0, None, ALU.is_le).then_inc(s_crowd, 1)
                e.tensor_scalar(crowded[:, :], fits[:, 1:2], 0.0, None, ALU.is_gt).then_inc(s_crowd, 1)
                e.wait_ge(s_crowd, 2)
                e.wait_ge(s_keep, 1)
                chain(e.tensor_tensor(keep[:, :], bank[7][:, 0:1], scales[:, 1:2], ALU.mult))

            def add_chunk(pair, chunk):
                def one(ins):
                    ins.then_inc(g_own, 1)
                    taken(e, g_own)

                taken(e, g_load, 16)
                k, ka, kb = g_key[:, 0:1], klo[:, 0:1], klo[:, 1:2]
                if pair < FIRST:
                    one(e.tensor_scalar(ka, k, KEY_TOP | pair // 2 << CELL_PAIR_BIT, None, ALU.bitwise_xor))
                    one(e.tensor_scalar(kb, ka, PAIR - 1, None, ALU.bitwise_and))
                    one(e.tensor_copy(g_lo[:, 1:2], kb))
                    one(e.tensor_scalar(kb, ka, CELL_PAIR_BIT, None, ALU.logical_shift_right))
                    one(e.scalar_tensor_tensor(out=g_lo[:, 0:1], in0=kb, scalar=float(2 * PAIR), in1=g_lo[:, 1:2],
                                               op0=ALU.mult, op1=ALU.add))
                    one(e.tensor_scalar(kb, ka, LOG_PAIR, NODE_MASK, ALU.logical_shift_right, ALU.bitwise_and))
                else:
                    one(e.tensor_scalar(ka, k, NODE_BITS, NODE_MASK, ALU.logical_shift_right, ALU.bitwise_and))
                    one(e.tensor_scalar(g_lo[:, 0:1], ka, float(-pair * P), None, ALU.add))
                    one(e.tensor_scalar(kb, k, NODE_MASK, None, ALU.bitwise_and))
                one(e.tensor_scalar(g_lo[:, 1:2], g_lo[:, 0:1], float(-P), None, ALU.add))
                for h in range(2):
                    one(e.tensor_scalar(g_onehot[:, h, :], iota16[:, 0:P], g_lo[:, h:h + 1], None, ALU.is_equal))
                e.tensor_scalar(g_ki[:, 0:1], kb, float(N - 1), None, ALU.min).then_inc(g_idx, 1)
                taken(e, g_sum)
                for h in range(min(2, TILES - pair)):
                    extra = XT[:, pair + h, :, :].rearrange("p a b -> p (a b)")
                    for i in range(2):
                        one(e.scalar_tensor_tensor(out=extra, in0=bank[6 + h][:, i * D:(i + 1) * D],
                                                   scalar=scales[:, 1:2], in1=extra, op0=ALU.mult, op1=ALU.add))
                e.memset(klo[:, 0:1], 0).then_inc(g_done, 1)

            unpack(0)
            prepare(0)
            find_runs()
            unpack(1)
            for k in range(SLOTS_ALL):
                prepare(k + 2)
                for s, t in due(k, 4):
                    residual(s, t)
                if slot(k)[0] == "gather" and slot(k)[2] == 0 and slot(k)[1] + 2 < ROUNDS:
                    unpack(slot(k)[1] + 2)
                if k == 0:
                    find_cells()
                if k == 2:
                    split_cells()
                if k == PART:
                    set_flags()
                    e.wait_ge(s_extra, 3)
                    crowded_path(e, add_chunk)
                for s, t in due(k, 0):
                    sum_in(s, t)

            def low(o, a, scale, high):
                return e.scalar_tensor_tensor(out=o, in0=a, scalar=scale, in1=high, op0=ALU.mult, op1=ALU.subtract)

            def xn_low(c):
                e.wait_ge(s_xh, c)
                t = tiles_of(c)
                z = len(t) * D
                high, o = (h.rearrange("p a b -> p (a b)")[:, 0:z] for h in xn_buf(c))
                low(o, XT[:, t[0]:t[-1] + 1, :, :].rearrange("p a b c -> p (a b c)"), XN_SCALE, high).then_inc(s_xl, 1)

            e.wait_ge(s_txc, 2 * TILES)
            e.tensor_reduce(msum[:, :], colsum[:, :, :], AX.X, ALU.add).then_inc(s_msum, 1)
            free = [4]

            def row(n=EXPERTS):
                free[0] += 1
                return R[:, free[0] - 1, 0:n]

            def exp_small(d, n):
                acc = row(n)
                chain(e.tensor_scalar(acc, d, 1.0 / math.factorial(8), None, ALU.mult))
                for k in range(7, 0, -1):
                    chain(e.scalar_tensor_tensor(out=acc, in0=acc, scalar=1.0 / math.factorial(k), in1=d,
                                                 op0=ALU.add, op1=ALU.mult))
                chain(e.tensor_scalar(acc, acc, 1.0, None, ALU.add))
                return acc

            def over_sum(v):
                t, o = row(1), row()
                chain(e.tensor_reduce(t, v, AX.X, ALU.add))
                chain(e.reciprocal(t, t))
                chain(e.tensor_scalar(o, v, t, None, ALU.mult))
                return o

            def less_max(v, o):
                t = row(1)
                chain(e.tensor_reduce(t, v, AX.X, ALU.max))
                return e.tensor_scalar(o, v, t, None, ALU.subtract)

            e.wait_ge(s_logit, 1)
            logits = R[:, 0, :]
            chain(e.scalar_tensor_tensor(out=logits, in0=bank[6][0:1, 0:EXPERTS], scalar=1.0 / N, in1=brs[:, :],
                                         op0=ALU.mult, op1=ALU.add))
            less_max(logits, R[:, 1, :]).then_inc(s_dif, 1)
            e.wait_ge(s_exp, 1)
            probs = over_sum(R[:, 2, :])
            scale, capped = row(), row()
            chain(e.tensor_scalar(scale, probs, float(N), 1.0, ALU.mult, ALU.max))
            chain(e.reciprocal(scale, scale))
            chain(e.tensor_scalar(scale, scale, CAPACITY, 1.0, ALU.mult, ALU.min))
            chain(e.tensor_tensor(capped, probs, scale, ALU.mult))
            dif = row()
            chain(less_max(capped, dif))
            weights = over_sum(exp_small(dif, EXPERTS))
            best, at = [], []
            for i in range(TOP_K):
                m, t, a = row(1), row(), row(1)
                chain(e.tensor_reduce(m, weights, AX.X, ALU.max))
                chain(e.tensor_scalar(t, weights, m, None, ALU.is_equal))
                down = row()
                chain(e.tensor_scalar(down, iota16[0:1, 0:EXPERTS], -1.0, float(EXPERTS), ALU.mult, ALU.add))
                chain(e.tensor_tensor(t, t, down, ALU.mult))
                chain(e.tensor_reduce(a, t, AX.X, ALU.max))
                chain(e.tensor_scalar(a, a, -1.0, float(EXPERTS), ALU.mult, ALU.add))
                e.tensor_copy(chosen[:, i:i + 1], a).then_inc(s_chosen, 1)
                best.append(m)
                if i + 1 < TOP_K:
                    chain(e.tensor_scalar(t, iota16[0:1, 0:EXPERTS], a, -2.0, ALU.is_equal, ALU.mult))
                    left = row()
                    chain(e.tensor_tensor(left, weights, t, ALU.add))
                    weights = left
            d, tot = row(1), row(1)
            chain(e.tensor_tensor(d, best[1], best[0], ALU.subtract))
            ex = exp_small(d, 1)
            chain(e.tensor_scalar(tot, ex, 1.0, None, ALU.add))
            chain(e.reciprocal(wts[:, 0:1], tot))
            e.tensor_tensor(wts[:, 1:2], ex, wts[:, 0:1], ALU.mult).then_inc(s_route, 1)

            nmr_all = minus_mean(nmr2[:, :], mv2[:, :, 0], rs2[:, :])
            nmr_all.then_inc(s_nmr2, 1)
            xn_low(1)
            e.wait_ge(s_wbp, 1)
            chain(e.tensor_copy(wb[:, :], bank[6][:, 0:TOP_K]))
            e.wait_ge(s_eb, 32 * TOP_K)
            chain(e.tensor_scalar(bias[:, :], eb2[:, 0, :], wb[:, 0:1], None, ALU.mult))
            e.scalar_tensor_tensor(out=bias[:, :], in0=eb2[:, 1, :], scalar=wb[:, 1:2], in1=bias[:, :],
                                   op0=ALU.mult, op1=ALU.add).then_inc(s_bias, 1)
            e.wait_ge(s_asp, 1)
            xi = xsc[:, :, :].bitcast(I32)
            chain(e.tensor_copy(xsc[:, 0, :], bank[7][:, 0:3]))
            chain(e.scalar_tensor_tensor(out=xsc[:, 0, 1:2], in0=xsc[:, 0, 0:1], scalar=LNORM_MAX, in1=xsc[:, 0, 1:2],
                                         op0=ALU.mult, op1=ALU.add))
            chain(e.tensor_scalar(xsc[:, 0, :], xsc[:, 0, :], 1e-18, 1e18, ALU.max, ALU.min))
            chain(e.tensor_scalar(xi[:, 1, :], xi[:, 0, :], 0xff * one_bit, None, ALU.bitwise_and))
            step(e.tensor_scalar(xi[:, 2, :], xi[:, 1, :], -1.0, float((2 * 127 + HALF_TOP) * one_bit), ALU.mult, ALU.add))
            step(e.tensor_scalar(xi[:, 3, :], xi[:, 1, :], float(-HALF_TOP * one_bit), None, ALU.add))
            settle()
            step(e.tensor_scalar(inv_h[:, :], xsc[:, 3, 0:1], 1.0 / XN_SCALE, None, ALU.mult))
            step(e.tensor_tensor(inv_y[:, :], xsc[:, 3, 1:2], xsc[:, 3, 2:3], ALU.mult))
            settle()
            e.memset(stat3[:, :, :], 0.0).then_inc(s_xsc, 1)

            def weight_low(i):
                e.wait_ge(s_wh[i], 1)
                low((ew1, ew2)[i][1], (w1_in, w2_in)[i], xsc[:, 2, 2 * i:2 * i + 1], (ew1, ew2)[i][0]).then_inc(s_wl[i], 1)

            def gelu_low(n):
                c, f = divmod(n, FB)
                tok = tokens_of(c)
                e.wait_ge(s_ah, n + 1)
                if c >= 2 and f == 0:
                    e.wait_ge(s_y, tiles_of(c - 2)[-1] + 1)
                low(act[c % 2][1][:, f, 0:tok], gelu_buf(n)[:, 0:tok], xsc[:, 2, 1:2], act[c % 2][0][:, f, 0:tok])\
                    .then_inc(s_al, 1)

            def add_y(c):
                tiles = tiles_of(c)
                r = res[c % 2]
                n = P if c < STEPS - 1 else LAST
                for i, t in enumerate(tiles):
                    e.wait_ge(s_xr, t + 1)
                    e.wait_ge(s_y, t + 1)
                    e.scalar_tensor_tensor(out=r[0:n, i, :], in0=bank[4 + t % Y_BANKS][0:n, 0:D], scalar=inv_y[0:n, 0:1],
                                           in1=r[0:n, i, :], op0=ALU.mult, op1=ALU.add).then_inc(s_yr, 1)
                    if i:
                        step(e.bn_stats(stat3[:, i - 1, :], r[:, i - 1, :]))
                    e.wait_ge(s_yr, t + 1)
                step(e.bn_stats(stat3[:, len(tiles) - 1, :], r[:, len(tiles) - 1, :]))
                settle()

            def normalise(c):
                n = len(tiles_of(c))
                r = res[c % 2]
                for i in range(n):
                    step(e.bn_aggr(mv3[:, i, :], stat3[:, i, :]))
                settle()
                rsqrt(rs3[:, 0:n], mv3[:, 0:n, 1], rq[0][:, 0:n], rq[1][:, 0:n])
                for i in range(n):
                    ins = e.tensor_scalar(r[:, i, :], r[:, i, :], mv3[:, i, 0:1], rs3[:, i:i + 1], ALU.subtract, ALU.mult)
                ins.then_inc(s_ln, 1)
                if c >= POOL_ENDS:
                    e.wait_ge(s_ln, c + 1)
                    for i in range(n):
                        step(e.tensor_tensor(r[:, i, :], r[:, i, :], gam, ALU.mult))
                    settle()
                    for i, t in enumerate(tiles_of(c)):
                        ins = e.tensor_tensor(r[:, i, :], r[:, i, :], X[:, t, :], ALU.add)
                    ins.then_inc(s_fin_last, 1)

            weight_low(0)
            e.wait_ge(s_ew2, 16 * TOP_K)
            for i in range(TOP_K):
                w = w2_in[:, i * KF:(i + 1) * KF, :]
                e.tensor_scalar(w, w, wb[:, i:i + 1], None, ALU.mult).then_inc(s_w2s, 1)
            for c in range(STEPS + 1):
                for f in range(FB):
                    if c < STEPS:
                        gelu_low(c * FB + f)
                    if c == 0 and f == 3:
                        weight_low(1)
                if 1 <= c < STEPS - 1:
                    xn_low(c + 1)
                if c >= 1:
                    add_y(c - 1)
                    normalise(c - 1)


_INS = ["x", "src", "dst", "L0_gnn_w1", "L0_gnn_b1", "L0_gnn_w2", "L0_gnn_b2", "L0_ffn_Wr", "L0_ffn_br",
        "L0_ffn_W1", "L0_ffn_b1", "L0_ffn_W2", "L0_ffn_b2", "L0_ffn_gamma", "L0_ffn_beta"]


def constants():
    import numpy as np
    p = np.arange(P)
    cf = np.concatenate([np.eye(P), np.broadcast_to(np.arange(PAIR), (P, PAIR))], axis=1).astype(np.float32)
    ci = np.zeros((P, 16 + CELL_GROUPS), np.int32)
    for g in range(CELL_GROUPS):
        cell = g * P + p
        number = cell // TILES << CELL_PAIR_BIT - CELL_BITS | cell % TILES
        ci[:, 16 + g] = np.where(cell < CELLS, KEY_TOP | number << CELL_BITS, 0)
    ci[:, 0] = KEY_BITS * (p & 1)
    ci[:, 1] = KEY_BITS * (1 - (p & 1))
    for k in range(LOG_SLOTS, LOG_ALL):
        m = k - LOG_SLOTS
        ci[:, 2 + m] = KEY_BITS * ((p >> m ^ p >> (m + 1)) & 1)
    return cf, ci


def kernel(**inputs):
    import numpy as np
    import concourse.bacc as bacc
    from concourse.bass_utils import run_bass_kernel_spmd

    nc = bacc.Bacc("TRN2", target_bir_lowering=False, num_devices=1)
    cf, ci = constants()
    given = {name: np.asarray(inputs[name]) for name in _INS}
    for name in ("L0_gnn_w1", "L0_gnn_w2", "L0_ffn_Wr"):
        given[name] = given[name].reshape(KD, P, -1).transpose(1, 0, 2)
    given["L0_gnn_b1"] = given["L0_gnn_b1"].reshape(KD, P).T
    given["L0_ffn_W1"] = given["L0_ffn_W1"].reshape(EXPERTS, KD, P, F).transpose(0, 2, 1, 3)
    given["L0_ffn_b1"] = given["L0_ffn_b1"].reshape(EXPERTS, KF, P).transpose(0, 2, 1)
    given["L0_ffn_W2"] = given["L0_ffn_W2"].reshape(EXPERTS, KF, P, D).transpose(0, 2, 1, 3)
    given |= {"cf": cf, "ci": ci}
    arrays, args = {}, []
    for name, a in given.items():
        a = np.ascontiguousarray(a)
        arrays[f"in_{name}"] = a
        args.append(nc.dram_tensor(f"in_{name}", a.shape, mybir.dt.from_np(a.dtype), kind="ExternalInput").ap())
    args.append(nc.dram_tensor("out_0", (N, D), F32, kind="ExternalOutput").ap())
    build(nc, *args)
    r = run_bass_kernel_spmd(nc, [arrays], core_ids=[0])
    return r.results[0]["out_0"]
```
